# Optimizing a Trainium2 kernel written in Bass

```python
import numpy as np
import jax
import jax.numpy as jnp

def _softmax(x, axis=-1):
    return jax.nn.softmax(x, axis=axis)

def _gelu(x):
    return jax.nn.gelu(x, approximate=True)

def _silu(x):
    return jax.nn.silu(x)

def _sigmoid(x):
    return jax.nn.sigmoid(x)

def _layernorm(x, axis=-1, eps=1e-05):
    m = jnp.mean(x, axis=axis, keepdims=True)
    v = jnp.var(x, axis=axis, keepdims=True)
    return (x - m) / jnp.sqrt(v + eps)

def _scatter_add(tgt, idx, src, axis=0):
    return tgt.at[idx].add(src)

def _segment_sum(src, seg, n):
    return jax.ops.segment_sum(src, seg, n)
kernel_name = 'mk_hybrid_d1_jaxref_r8_7ec2b7'

def setup_inputs(seed: int=0):
    np.random.seed(seed)
    _w = jnp.asarray

    def _L0_attn_a_setup():
        import jax, jax.numpy as jnp
        import numpy as np
        N_SCALES = 11
        D4 = [0.4829629131445341, 0.8365163037378079, 0.2241438680420134, -0.1294095225512604]
        B, N, D, H = (4, 256, 128, 16)
        HD = D // H

        def _shift(t, offset):
            return jnp.pad(t, ((0, 0), (0, 0), (offset, 0), (0, 0)))[:, :, :t.shape[2], :]
        key = jax.random.key(seed)
        ks = jax.random.split(key, 10)
        s = 0.02
        return {'x': jax.random.normal(ks[0], (B, N, D), jnp.float32), 'W_qkv': jax.random.normal(ks[1], (3 * D, D), jnp.float32) * s, 'b_qkv': jnp.zeros((3 * D,), jnp.float32), 'W_out': jax.random.normal(ks[2], (D, D), jnp.float32) * s, 'b_out': jnp.zeros((D,), jnp.float32), 'W_gate': jax.random.normal(ks[3], (D, D), jnp.float32) * s, 'b_gate': jnp.full((D,), 2.0, jnp.float32), 'scale_gain': jnp.zeros((N_SCALES, H), jnp.float32), 'W_qscale': jax.random.normal(ks[4], (N_SCALES, HD), jnp.float32) * 0.01, 'identity_bypass': jnp.full((H,), -4.0, jnp.float32)}
    _L0_attn_a_in = _L0_attn_a_setup()

    def _L0_attn_b_setup():
        import jax, jax.numpy as jnp
        import numpy as np
        LN_EPS = 1e-05
        key = jax.random.key(seed)
        ks = jax.random.split(key, 4)
        B_, S, D = (32, 128, 128)
        return {'x': jax.random.normal(ks[0], (B_, S, D), dtype=jnp.float32), 'A': jax.random.normal(ks[1], (D, D), dtype=jnp.float32) * 0.01, 'B': jax.random.normal(ks[2], (D, D), dtype=jnp.float32) * 0.01, 'C': jax.random.normal(ks[3], (D, D), dtype=jnp.float32) * 0.01, 'gamma': jnp.ones((D,), dtype=jnp.float32), 'beta': jnp.zeros((D,), dtype=jnp.float32)}
    _L0_attn_b_in = _L0_attn_b_setup()

    def _L0_ffn_setup():
        import jax, jax.numpy as jnp
        import numpy as np
        DIM, HIDDEN, E = (128, 512, 8)
        B, L = (2, 256)
        key = jax.random.key(seed)
        ks = jax.random.split(key, 6)
        s_in = 1.0 / np.sqrt(DIM)
        s_h = 1.0 / np.sqrt(HIDDEN)
        return {'x': jax.random.normal(ks[0], (B, L, DIM), dtype=jnp.float32), 'Wg': jax.random.uniform(ks[1], (E, DIM), jnp.float32, -s_in, s_in), 'W1': jax.random.uniform(ks[2], (E, DIM, HIDDEN), jnp.float32, -s_in, s_in), 'b1': jax.random.uniform(ks[3], (E, HIDDEN), jnp.float32, -s_in, s_in), 'W2': jax.random.uniform(ks[4], (E, HIDDEN, DIM), jnp.float32, -s_h, s_h), 'b2': jax.random.uniform(ks[5], (E, DIM), jnp.float32, -s_h, s_h)}
    _L0_ffn_in = _L0_ffn_setup()
    _d = {'L0_attn_a_x': _L0_attn_a_in['x'], 'L0_attn_a_W_qkv': _L0_attn_a_in['W_qkv'], 'L0_attn_a_b_qkv': _L0_attn_a_in['b_qkv'], 'L0_attn_a_W_out': _L0_attn_a_in['W_out'], 'L0_attn_a_b_out': _L0_attn_a_in['b_out'], 'L0_attn_a_W_gate': _L0_attn_a_in['W_gate'], 'L0_attn_a_b_gate': _L0_attn_a_in['b_gate'], 'L0_attn_a_scale_gain': _L0_attn_a_in['scale_gain'], 'L0_attn_a_W_qscale': _L0_attn_a_in['W_qscale'], 'L0_attn_a_identity_bypass': _L0_attn_a_in['identity_bypass'], 'L0_attn_b_A': _L0_attn_b_in['A'], 'L0_attn_b_B': _L0_attn_b_in['B'], 'L0_attn_b_C': _L0_attn_b_in['C'], 'L0_attn_b_gamma': _L0_attn_b_in['gamma'], 'L0_attn_b_beta': _L0_attn_b_in['beta'], 'L0_ffn_Wg': _L0_ffn_in['Wg'], 'L0_ffn_W1': _L0_ffn_in['W1'], 'L0_ffn_b1': _L0_ffn_in['b1'], 'L0_ffn_W2': _L0_ffn_in['W2'], 'L0_ffn_b2': _L0_ffn_in['b2']}
    _x0 = _d['L0_attn_a_x']
    _d['L0_attn_a_x'] = jax.random.normal(jax.random.fold_in(jax.random.key(seed), 1), (16, 512, 128), dtype=_x0.dtype)
    del _x0
    return _d

def reference(L0_attn_a_x, L0_attn_a_W_qkv, L0_attn_a_b_qkv, L0_attn_a_W_out, L0_attn_a_b_out, L0_attn_a_W_gate, L0_attn_a_b_gate, L0_attn_a_scale_gain, L0_attn_a_W_qscale, L0_attn_a_identity_bypass, L0_attn_b_A, L0_attn_b_B, L0_attn_b_C, L0_attn_b_gamma, L0_attn_b_beta, L0_ffn_Wg, L0_ffn_W1, L0_ffn_b1, L0_ffn_W2, L0_ffn_b2):

    def _L0_attn_a_ref(x, W_qkv, b_qkv, W_out, b_out, W_gate, b_gate, scale_gain, W_qscale, identity_bypass):
        import jax, jax.numpy as jnp
        import numpy as np
        N_SCALES = 11
        D4 = [0.4829629131445341, 0.8365163037378079, 0.2241438680420134, -0.1294095225512604]
        B, N, D, H = (4, 256, 128, 16)
        HD = D // H

        def _shift(t, offset):
            return jnp.pad(t, ((0, 0), (0, 0), (offset, 0), (0, 0)))[:, :, :t.shape[2], :]
        Bx, Nx, Dx = x.shape
        qkv = x @ W_qkv.T + b_qkv
        q, k, v = jnp.split(qkv, 3, axis=-1)
        q = q.reshape(Bx, Nx, H, HD).transpose(0, 2, 1, 3)
        k = k.reshape(Bx, Nx, H, HD).transpose(0, 2, 1, 3)
        v = v.reshape(Bx, Nx, H, HD).transpose(0, 2, 1, 3)
        q_offset = jnp.einsum('bhnd,sd->bhns', q, W_qscale)
        prior = scale_gain.T[None, :, None, :]
        gains = jax.nn.softmax(q_offset + prior, axis=-1)
        out = jnp.zeros_like(q)
        for j in range(N_SCALES):
            d = 1 << j
            g_j = gains[:, :, :, j:j + 1]
            for tau, h_coef in enumerate(D4):
                offset = d * tau
                if offset >= Nx:
                    continue
                k_s = k if offset == 0 else _shift(k, offset)
                v_s = v if offset == 0 else _shift(v, offset)
                qk = jnp.sum(q * k_s, axis=-1, keepdims=True)
                out = out + g_j * h_coef * qk * v_s
        bypass = jax.nn.softplus(identity_bypass)[None, :, None, None]
        local_qk = jnp.sum(q * k, axis=-1, keepdims=True)
        out = out + bypass * local_qk * v
        gathered = out.transpose(0, 2, 1, 3).reshape(Bx, Nx, Dx)
        gate = jax.nn.sigmoid(x @ W_gate.T + b_gate)
        return gathered * gate @ W_out.T + b_out

    def _L0_attn_b_ref(x, A, B, C, gamma, beta):
        import jax, jax.numpy as jnp
        import numpy as np
        LN_EPS = 1e-05
        batch, seq_len, d = x.shape
        xb = jnp.einsum('bsd,ed->sbe', x, B)

        def step(h, xb_t):
            h = jnp.tanh(h @ A.T + xb_t)
            y = h @ C.T
            return (h, y)
        h0 = jnp.zeros((batch, d), dtype=x.dtype)
        _, ys = jax.lax.scan(step, h0, xb)
        out = jnp.transpose(ys, (1, 0, 2)) + x
        mu = jnp.mean(out, axis=-1, keepdims=True)
        var = jnp.mean(jnp.square(out - mu), axis=-1, keepdims=True)
        return (out - mu) * jax.lax.rsqrt(var + LN_EPS) * gamma + beta

    def _L0_ffn_ref(x, Wg, W1, b1, W2, b2):
        import jax, jax.numpy as jnp
        import numpy as np
        DIM, HIDDEN, E = (128, 512, 8)
        B, L = (2, 256)
        gate_logits = jnp.einsum('bld,ed->ble', x, Wg)
        top1 = jnp.argmax(gate_logits, axis=-1)
        out = jnp.zeros_like(x)
        for e in range(E):
            mask = (top1 == e)[..., None]
            h = jax.nn.gelu(jnp.einsum('bld,dh->blh', x, W1[e]) + b1[e], approximate=False)
            y = jnp.einsum('blh,hd->bld', h, W2[e]) + b2[e]
            out = jnp.where(mask, y, out)
        return out
    x = L0_attn_a_x
    x = x + _L0_attn_a_ref(_layernorm(x, axis=-1), L0_attn_a_W_qkv, L0_attn_a_b_qkv, L0_attn_a_W_out, L0_attn_a_b_out, L0_attn_a_W_gate, L0_attn_a_b_gate, L0_attn_a_scale_gain, L0_attn_a_W_qscale, L0_attn_a_identity_bypass)
    x = x + _L0_ffn_ref(_layernorm(x, axis=-1), L0_ffn_Wg, L0_ffn_W1, L0_ffn_b1, L0_ffn_W2, L0_ffn_b2)
    x = x + _L0_attn_b_ref(_layernorm(x, axis=-1), L0_attn_b_A, L0_attn_b_B, L0_attn_b_C, L0_attn_b_gamma, L0_attn_b_beta)
    x = x + _L0_ffn_ref(_layernorm(x, axis=-1), L0_ffn_Wg, L0_ffn_W1, L0_ffn_b1, L0_ffn_W2, L0_ffn_b2)
    return x

_drawn_inputs = setup_inputs


def setup_inputs(seed=0):
    import zlib

    import numpy as np

    out = dict(_drawn_inputs(seed))
    spreads = {'L0_attn_a_b_qkv': (0.0, 0.443),
     'L0_attn_a_b_out': (0.0, 0.1),
     'L0_attn_a_b_gate': (2.0, 0.6),
     'L0_attn_a_scale_gain': (0.0, 0.8),
     'L0_attn_a_identity_bypass': (-4.0, 0.6),
     'L0_attn_b_gamma': (1.0, 0.2),
     'L0_attn_b_beta': (0.0, 0.1)}
    factors = {'L0_attn_a_W_qkv': 3.324,
     'L0_attn_a_W_out': 3.277,
     'L0_attn_a_W_gate': 8.0,
     'L0_attn_a_W_qscale': 8.0,
     'L0_attn_b_A': 8.0,
     'L0_attn_b_B': 4.987,
     'L0_attn_b_C': 5.377}
    for name, (base, spread) in spreads.items():
        noise = np.random.default_rng([zlib.crc32(name.encode()), seed]).standard_normal(out[name].shape)
        drawn = base * np.exp(spread * noise) if base else spread * noise
        out[name] = jnp.asarray(drawn.astype(out[name].dtype))
    for name, factor in factors.items():
        out[name] = (out[name] * factor).astype(out[name].dtype)
    return out
```

```python
from contextlib import ExitStack

import numpy as np

import concourse.bass as bass
from concourse import mybir

F32 = mybir.dt.float32
F32R = mybir.dt.float32r
I32 = mybir.dt.int32
ACT = mybir.ActivationFunctionType
ALU = mybir.AluOpType
X_AXIS = mybir.AxisListType.X
ds = bass.ds

P = 128
NB, NT, D, H, NS, NE, NH = 16, 512, 128, 16, 11, 8, 512
HD = D // H
TILES = NB * NT // P
TT = P // NB
CT = 32
CW = CT * NB
TPC = CW // P
CHUNKS = NT // CT
SLOT_TILES = TILES + NE - 1
HC = NH // P
RING = 4
EPS = 1e-5
D4 = [0.4829629131445341, 0.8365163037378079, 0.2241438680420134, -0.1294095225512604]

POW = [1 << m for m in range(9)]
TRI = [3 << m for m in range(8)]
PAD = 96 * NB

C_ID, C_UP, C_BLK, C_SEL = 0, 128, 256, 384
C_HM = C_SEL + 64
C_REV = C_HM + H
C_KT = C_REV + NE
C_SI = C_KT + TILES
C_KEPT = C_SI + SLOT_TILES
C_ESEL = C_KEPT
C_ALL = C_ESEL + 8 * P


def constants():
    c = np.zeros((P, C_ALL), np.float32)
    k = np.arange(P)
    c[:, C_ID:C_ID + P] = np.eye(P)
    c[:, C_UP:C_UP + P] = k[:, None] < k[None, :]
    c[:, C_BLK:C_BLK + P] = k[:, None] // HD == k[None, :] // HD
    for s in range(2):
        c[:, C_SEL + 32 * s + 16 * s:C_SEL + 32 * s + 16 * s + H] = k[:, None] // HD == np.arange(H)[None, :]
    for m in range(8):
        c[:, C_ESEL + P * m:C_ESEL + P * m + P] = k[:, None] == H * m + k[None, :] // HD
    c[:, C_HM:C_HM + H] = k[:, None] // HD == np.arange(H)[None, :]
    c[:, C_REV:C_REV + NE] = NE - np.arange(NE)
    c[:, C_KT:C_KT + TILES] = P * np.arange(TILES)
    c[:, C_SI:C_SI + SLOT_TILES] = np.arange(SLOT_TILES)
    return c


class Steps:

    def __init__(self, eng, sem):
        self.eng, self.sem, self.base, self.n = eng, sem, 0, 0

    def enter(self, start, i, per):
        self.base, self.n = i * per + start, 0

    def leave(self, total):
        self.base, self.n = 0, total

    def done(self, ins):
        ins.then_inc(self.sem, 1)
        self.n += 1

    def wait(self):
        self.eng.wait_ge(self.sem, self.base + self.n)


def active(i):
    last = CT * (i + 1) - 1
    g0 = [m for m in range(8) if POW[m] <= last]
    g1 = [m for m in range(8) if TRI[m] <= last]
    return g0, g1, POW[8] <= last


def products_of(i):
    g0, g1, g2 = active(i)
    return 1 + len(g0) + len(g1) + int(g2)


RANGES = [(1, 2), (2, 3), (3, 4), (4, 6), (6, 8), (8, 12), (12, CHUNKS - 1)]
for _lo, _hi in RANGES:
    assert all(active(x) == active(_lo) for x in range(_lo, _hi))
PRODUCTS_BEFORE = [sum(products_of(x) for x in range(i)) for i in range(CHUNKS + 1)]


STAGE = 9


def build(nc, a, consts, out, stage=9):
    with ExitStack() as ctx:
        def sb(name, shape, dt=F32):
            return ctx.enter_context(nc.sbuf_tensor(name, shape, dt))

        def sem(name):
            return ctx.enter_context(nc.semaphore(name))

        xs = [nc.dram_tensor(f"sorted_x{f}", (SLOT_TILES * P, D), F32, kind="Internal").ap() for f in range(2)]
        ys = [nc.dram_tensor(f"sorted_y{f}", (SLOT_TILES * P, D), F32, kind="Internal").ap() for f in range(2)]

        X = sb("X", [P, TILES * D])
        XN = sb("XN", [P, TILES * D])
        cst = sb("cst", [P, C_KEPT])
        w2 = sb("w2", [P, NE * HC * D])
        b1T = sb("b1T", [P, NE * HC])
        b2bc = sb("b2bc", [P, NE * D])
        wgT = sb("wgT", [P, 32])
        projT = sb("projT", [P, 4 * D])
        outT = sb("outT", [P, D])
        abcT = sb("abcT", [P, 3 * D])
        qkvb = sb("qkvb", [P, 4])
        halfgb = sb("halfgb", [P, 1])
        brow = sb("brow", [P, 3 * D])
        zero = sb("zero", [P, 512])
        ones = sb("ones", [P, P])
        mqs = sb("mqs", [P, H * NS])
        prow = sb("prow", [1, H * NS])
        prior = sb("prior", [P, H * NS])
        byp = sb("byp", [P, 6])
        blkw = sb("blkw", [P, P])
        esel = sb("esel", [P, 8 * P], F32R)
        nums = sb("nums", [P, 4])
        raw = sb("raw", [P, TILES * 6])
        mean = sb("mean", [P, TILES])
        rstd = sb("rstd", [P, TILES])
        raw2 = sb("raw2", [P, TPC * 6])
        mean2 = sb("mean2", [P, TPC])
        rstd2 = sb("rstd2", [P, TPC])
        mom = sb("mom", [P, 5 * TILES])
        slot_i = sb("slot_i", [P, TILES], I32)
        te_i = sb("te_i", [1, SLOT_TILES], I32)
        xn = [sb("xn0", [P, CW])]
        xnT = sb("xnT", [P, CW])
        ah = [sb(f"ah{g}", [P, CW], F32R) for g in range(3)]
        al = [sb(f"al{g}", [P, CW], F32R) for g in range(3)]
        K = sb("K", [P, PAD + NB * NT])
        V = sb("V", [P, PAD + NB * NT])

        at = [0]

        def in_xn(n):
            at[0] += n
            assert at[0] <= TILES * D
            return XN[:, at[0] - n:at[0]]

        qT, th, acc, att = in_xn(CW), in_xn(CW), in_xn(CW), in_xn(CW)
        NPROD = 4
        prod = [in_xn(CW) for _ in range(NPROD)]
        NTERM = 4
        term = [in_xn(CW) for _ in range(NTERM)]
        gains = in_xn(TPC * H * NS)
        gmax, gsum = in_xn(TPC * H), in_xn(TPC * H)
        wload = V[:, PAD:PAD + 8 * D]
        small = V[:, PAD + 8 * D:PAD + 10 * D]
        srows = V[0:NS, PAD + 18 * D:PAD + 19 * D]
        eload = V[:, PAD + 10 * D:PAD + 18 * D]
        w8 = sb("w8", [P, TPC * H])
        w01 = [sb(f"w{g}", [P, TPC * P]) for g in range(2)]
        wt = [sb("wt0", [P, CW]), in_xn(CW), in_xn(CW)]
        af = [sb(f"af{g}", [P, CW]) for g in range(2)]

        kat = [0]

        def in_k(n):
            if kat[0] < PAD + NB * NT < kat[0] + n:
                kat[0] = PAD + NB * NT
            kat[0] += n
            end = kat[0] % (PAD + NB * NT)
            return (K if kat[0] <= PAD + NB * NT else V)[:, end - n:end]

        xn.append(in_k(CW))
        w1b = [in_k(NH) for _ in range(RING)]
        xsb = [in_k(P) for _ in range(RING)]
        xTb = [in_k(P) for _ in range(2)]
        hb = [in_k(HC * P) for _ in range(2)]
        hT = [in_k(HC * P) for _ in range(2)]
        ysb = [in_k(P) for _ in range(2)]
        lT = in_k(CW)
        lg = in_k(TILES * NE)
        oh = in_k(TILES * NE)
        tmp = in_k(TILES * NE)
        incl = in_k(TILES * NE)
        m64, slotf, tef = in_k(TILES), in_k(TILES), in_k(SLOT_TILES)
        ntl, ctl, bas = in_k(NE), in_k(NE), in_k(NE)
        hid = [in_k(CW) for _ in range(2)]
        res = in_k(CW)

        bank = [ctx.enter_context(nc.psum_tensor(f"bank{j}", [P, 512], F32)) for j in range(8)]

        names = """consts_in weights_in w2_in norm_in filled wT_psum softplus setup_done
            zeros_written dve_step act_step pool_step
            stats rstd xn_ready xT_psum xT_ready kv_psum kv_ready q_psum q_ready gate_psum gate_ready
            logits shifted exp gains_ready scaled weights_ready rows_psum rows_ready
            products_ready products_used a0_ready a1_ready a2_ready a0_high a1_high a2_high
            a0_low a1_low a2_low spread_ready terms_ready terms_added gated y_psum xb_ready resid
            r_stats r_rstd r_xn r_kept r_xT_psum r_xT r_xb step_psum h_ready r_y r_stats2 r_rstd2 r_out
            out_stored""".split()
        S = {n: sem(n) for n in names}
        x_in = [sem(f"x_in{j}") for j in range(4)]
        fnames = """stats rstd xn kept xT_psum xT lT_psum lT lg_psum lg onehot counts slots_ready scattered
            transposed turned hidden biased gelu y_psum y_ready added""".split()
        FS = [{n: sem(f"f{f}_{n}") for n in fnames} for f in range(2)]
        for f in range(2):
            for n, r in (("xs_in", RING), ("w1_in", RING), ("ys_out", 2)):
                FS[f][n] = [sem(f"f{f}_{n}{u}") for u in range(r)]
            FS[f]["gathered"] = [sem(f"f{f}_gathered{q}") for q in range(4)]

        ident = cst[:, C_ID:C_ID + P]
        g2_first = next(i for i in range(CHUNKS) if active(i)[2])

        def sl(buf, at, width):
            return buf[:, at:at + width] if isinstance(at, int) else buf[:, ds(at, width)]

        def rows(t, at, n):
            return t[at:at + n, :] if isinstance(at, int) else t[ds(at, n), :]

        def x_dram(t, g):
            v = t.rearrange("b (g t) d -> g t b d", t=TT)
            return v[g] if isinstance(g, int) else v[ds(g, 1)].rearrange("a t b d -> (a t) b d")

        def later(i):
            return not isinstance(i, int) or i > 0

        def before(i, kind):
            return PRODUCTS_BEFORE[i] if isinstance(i, int) else (i - kind) * products_of(kind) + PRODUCTS_BEFORE[kind]

        def spread_before(i, kind):
            if isinstance(i, int):
                return PRODUCTS_BEFORE[i] - i
            return (i - kind) * (products_of(kind) - 1) + (PRODUCTS_BEFORE[kind] - kind)

        def bc_out(v):
            return v.unsqueeze(1).broadcast_to([P, TPC, D])

        block = ctx.enter_context(nc.Block())

        def ffn_sync(sp, f):
            s_ = FS[f]

            def load(s, u):
                if not isinstance(s, int) or s >= RING:
                    sp.wait_ge(s_["hidden"], s - (RING - 1))
                e = sp.value_load(sl(te_i, s, 1), min_val=0, max_val=NE - 1)
                sp.dma_start(xsb[u], rows(xs[f], s * P, P)).then_inc(s_["xs_in"][u], 16)
                sp.dma_start(w1b[u], a["W1"][ds(e, 1), :, :].rearrange("a d h -> (a d) h")).then_inc(s_["w1_in"][u], 16)

            sp.wait_ge(s_["slots_ready"], 2)
            sp.wait_ge(s_["scattered"], 16 * TILES)
            for s in range(RING):
                load(s, s)
            with sp.Fori(1, SLOT_TILES // RING) as j:
                for u in range(RING):
                    load(j * RING + u, u)
            for s in range(SLOT_TILES // RING * RING, SLOT_TILES):
                load(s, s % RING)

        @block.sync
        def _(sp):
            sp.dma_start(cst[:], consts[:, 0:C_KEPT]).then_inc(S["consts_in"], 16)
            sp.dma_start(eload, consts[:, C_ESEL:C_ALL]).then_inc(S["consts_in"], 16)
            for i in range(4):
                for c in range(TPC):
                    g = i * TPC + c
                    sp.dma_start(X[:, g * D:(g + 1) * D], x_dram(a["x"], g)).then_inc(x_in[i], 16)
            with sp.Fori(1, CHUNKS // 4) as r:
                for j in range(4):
                    sp.wait_ge(x_in[j], r * (16 * TPC))
                    for c in range(TPC):
                        g = r * (4 * TPC) + (j * TPC + c)
                        sp.dma_start(X[:, ds(g * D, D)], x_dram(a["x"], g)).then_inc(x_in[j], 16)
            sp.dma_start(w2[:].rearrange("p (e c d) -> p e c d", e=NE, c=HC),
                         a["W2"].rearrange("e (c p) d -> p e c d", p=P)).then_inc(S["w2_in"], 16)
            sp.dma_start(b2bc[:], a["b2"].rearrange("e d -> (e d)").partition_broadcast(P)).then_inc(S["w2_in"], 16)
            sp.wait_ge(S["filled"], 1)
            for f in range(2):
                v = xs[f].rearrange("(t p) d -> p t d", p=P)
                for t in range(0, SLOT_TILES, 4):
                    n = min(4, SLOT_TILES - t)
                    sp.dma_start(v[:, t:t + n, :],
                                 zero[:, 0:n * D].rearrange("p (t d) -> p t d", t=n)).then_inc(S["zeros_written"], 16)
            if stage >= 2:
                ffn_sync(sp, 0)
            if stage >= 4:
                ffn_sync(sp, 1)
            if stage < 4:
                sp.wait_ge(S["resid"], CHUNKS)
                if stage >= 2:
                    sp.wait_ge(FS[0]["added"], 4)
                if stage >= 3:
                    sp.wait_ge(S["r_out"], CHUNKS)
            for q in range(4):
                if stage >= 4:
                    sp.wait_ge(FS[1]["added"], q + 1)
                with sp.Fori(q * TILES // 4, (q + 1) * TILES // 4) as g:
                    sp.dma_start(x_dram(out, g), X[:, ds(g * D, D)]).then_inc(S["out_stored"], 16)
            sp.wait_ge(S["out_stored"], 16 * TILES)

        @block.gpsimd
        def _(pool):
            step = Steps(pool, S["pool_step"])
            for k, x in enumerate((-0.5, 0.5, 1.0 / D, EPS)):
                last = nc.gpsimd.memset(nums[:, k:k + 1], x)
            step.done(last)
            step.wait()

            def moments(r, mu, rs, n):
                def op(dst, x, y, o):
                    return nc.gpsimd.tensor_tensor(dst, x, y, o)

                r = r.rearrange("p (t s) -> p t s", s=6)
                m_even, q_even, m_odd, q_odd = (r[:, :, k] for k in (1, 2, 4, 5))
                total, diff, half, sq, var = (mom[:, k * TILES:k * TILES + n] for k in range(5))
                mhalf, phalf, inv, eps = (nums[:, k:k + 1].broadcast_to([P, n]) for k in range(4))
                op(total, m_even, m_odd, ALU.add)
                op(diff, m_even, m_odd, ALU.subtract)
                step.done(op(sq, q_even, q_odd, ALU.add))
                step.wait()
                op(mu, total, phalf, ALU.mult)
                op(half, diff, phalf, ALU.mult)
                step.done(op(var, sq, inv, ALU.mult))
                step.wait()
                op(diff, half, half, ALU.mult)
                step.done(op(total, var, eps, ALU.add))
                step.wait()
                step.done(op(var, total, diff, ALU.add))
                step.wait()
                return op(rs, var, mhalf, ALU.pow)

            MOMENTS = 4

            def head(n):
                pool.wait_ge(S["stats"], n + 1)
                moments(raw[:, 0:6 * TPC], mean[:, 0:TPC], rstd[:, 0:TPC], TPC).then_inc(S["rstd"], 1)
                pool.wait_ge(S["xn_ready"], n + 1)
                v = sl(X, n * CW, CW).rearrange("p (c d) -> p c d", d=D)
                nc.gpsimd.tensor_tensor(v, v, bc_out(brow[:, 0:D]), ALU.add).then_inc(S["xb_ready"], 1)

            def chunk(i, kind, nxt):
                n, base, adds = products_of(kind), before(i, kind), spread_before(i, kind)
                if nxt is not None:
                    head(nxt)
                if later(i):
                    pool.wait_ge(S["gated"], i)
                for j in range(1, n):
                    pool.wait_ge(S["terms_ready"], base + (j + 1))
                    if j > 1:
                        pool.wait_ge(S["terms_added"], adds + (j - 1))
                    nc.gpsimd.tensor_tensor(acc, acc if j > 1 else term[0], term[j % NTERM],
                                            ALU.add).then_inc(S["terms_added"], 1)

            pool.wait_ge(S["norm_in"], 16 * 3)
            head(0)
            chunk(0, 0, 1)
            for lo, hi in RANGES:
                start = step.n
                with pool.Fori(lo, hi) as i:
                    step.enter(start, i - lo, MOMENTS)
                    chunk(i, lo, i + 1)
                step.leave(start + (hi - lo) * MOMENTS)
            chunk(CHUNKS - 1, CHUNKS - 1, None)

            def ffn(f):
                s_ = FS[f]
                pool.wait_ge(s_["stats"], CHUNKS)
                moments(raw[:], mean[:], rstd[:], TILES).then_inc(s_["rstd"], 1)
                if f == 0:
                    pool.wait_ge(S["zeros_written"], 16 * 2 * ((SLOT_TILES + 3) // 4))
                pool.wait_ge(s_["kept"], CHUNKS)
                pool.wait_ge(s_["slots_ready"], 1)
                for g in range(TILES):
                    nc.gpsimd.indirect_dma_start(
                        out=xs[f], out_offset=bass.IndirectOffsetOnAxis(ap=slot_i[:, g:g + 1], axis=0),
                        in_=XN[:, g * D:(g + 1) * D], in_offset=None).then_inc(s_["scattered"], 16)
                pool.wait_ge(s_["scattered"], 16 * TILES)

                def store(s, u):
                    pool.wait_ge(s_["y_ready"], s + 1)
                    pool.dma_start(rows(ys[f], s * P, P), ysb[u]).then_inc(s_["ys_out"][u], 16)

                with pool.Fori(0, SLOT_TILES // 2) as j:
                    store(j * 2, 0)
                    store(j * 2 + 1, 1)
                store(SLOT_TILES - 1, 0)
                for u in range(2):
                    pool.wait_ge(s_["ys_out"][u], 16 * ((SLOT_TILES + 1 - u) // 2))
                for g in range(TILES):
                    nc.gpsimd.indirect_dma_start(
                        out=XN[:, g * D:(g + 1) * D], out_offset=None, in_=ys[f],
                        in_offset=bass.IndirectOffsetOnAxis(ap=slot_i[:, g:g + 1], axis=0),
                    ).then_inc(s_["gathered"][g * 4 // TILES], 16)

            if stage >= 2:
                ffn(0)
            if stage >= 3:
                pool.wait_ge(S["r_stats"], CHUNKS)
                moments(raw[:], mean[:], rstd[:], TILES).then_inc(S["r_rstd"], 1)
                start = step.n
                with pool.Fori(0, CHUNKS) as i:
                    step.enter(start, i, MOMENTS)
                    pool.wait_ge(S["r_stats2"], i + 1)
                    moments(raw2[:], mean2[:], rstd2[:], TPC).then_inc(S["r_rstd2"], 1)
                step.leave(start + CHUNKS * MOMENTS)
            if stage >= 4:
                ffn(1)

        @block.scalar
        def _(act):
            def load(dst, src):
                act.dma_start(dst, src).then_inc(S["weights_in"], 16)

            for j in range(3):
                load(wload[:, j * D:(j + 1) * D], a["W_qkv"][j * D:(j + 1) * D, :])
            for j, n in enumerate(["W_gate", "W_out", "A", "B", "C"]):
                load(wload[:, (3 + j) * D:(4 + j) * D], a[n])
            load(small[0:NE, 0:D], a["Wg"])
            load(small[0:32, P:2 * P], a["b1"].rearrange("e (c p) -> (e c) p", p=P))
            with nc.allow_non_contiguous_dma(reason="a few small vectors become columns"):
                load(qkvb[:, 0:3], a["b_qkv"].rearrange("(a p) -> p a", p=P))
                load(qkvb[:, 3:4], a["b_gate"].rearrange("(p a) -> p a", a=1))
                load(byp[:, 0:1], bass.AP(a["identity_bypass"].tensor, 0, [[1, H], [0, HD], [1, 1]]))
                load(srows.rearrange("s (h i) -> s h i", i=HD),
                     bass.AP(a["W_qscale"].tensor, 0, [[HD, NS], [0, H], [1, HD]]))
                load(prow[:].rearrange("a (h s) -> a h s", h=H), bass.AP(a["scale_gain"].tensor, 0, [[0, 1], [1, H], [H, NS]]))
            for j, n in enumerate(["b_out", "gamma", "beta"]):
                act.dma_start(brow[:, j * D:(j + 1) * D], a[n].partition_broadcast(P)).then_inc(S["norm_in"], 16)
            step = Steps(act, S["act_step"])
            act.wait_ge(S["weights_in"], 16 * 15)
            step.done(nc.scalar.activation(byp[:, 1:2], byp[:, 0:1], ACT.Abs))
            step.wait()
            step.done(nc.scalar.activation(byp[:, 2:3], byp[:, 1:2], ACT.Exp, scale=-1.0))
            step.wait()
            nc.scalar.activation(byp[:, 3:4], byp[:, 2:3], ACT.Ln, bias=1.0).then_inc(S["softplus"], 1)
            act.wait_ge(S["setup_done"], 1)

            def head(n):
                act.wait_ge(S["xT_psum"], n + 1)
                nc.scalar.activation(xnT[:], bank[0][:], ACT.Copy).then_inc(S["xT_ready"], 1)
                for j, buf in ((0, K), (1, V)):
                    act.wait_ge(S["kv_psum"], n * 2 + (j + 1))
                    nc.scalar.activation(sl(buf, n * CW + PAD, CW), bank[2 + j][:], ACT.Identity,
                                         bias=qkvb[:, 1 + j:2 + j]).then_inc(S["kv_ready"], 1)

            def queries(n, products):
                act.wait_ge(S["q_psum"], n + 1)
                if products is not None:
                    act.wait_ge(S["products_ready"], products)
                nc.scalar.activation(qT, bank[1][:], ACT.Identity, bias=qkvb[:, 0:1]).then_inc(S["q_ready"], 1)

            by_scale = gains.rearrange("p (c h s) -> p c s h", c=TPC, h=H)

            def weights(n):
                act.wait_ge(S["shifted"], n + 1)
                nc.scalar.activation(gains, gains, ACT.Exp).then_inc(S["exp"], 1)
                act.wait_ge(S["gains_ready"], n + 1)
                nc.scalar.activation(w01[0][:].rearrange("p (c m h) -> p c m h", c=TPC, h=H), by_scale[:, :, 0:8, :],
                                     ACT.Copy, scale=D4[1]).then_inc(S["scaled"], 1)
                nc.scalar.activation(w8[:].rearrange("p (c h) -> p c h", c=TPC), by_scale[:, :, 8, :],
                                     ACT.Copy, scale=D4[1]).then_inc(S["scaled"], 1)
                nc.scalar.activation(w01[1][:].rearrange("p (c m h) -> p c m h", c=TPC, h=H), by_scale[:, :, 0:8, :],
                                     ACT.Copy, scale=D4[3]).then_inc(S["scaled"], 1)
                act.wait_ge(S["rows_psum"], n + 1)
                nc.scalar.activation(wt[0][:], bank[2][:], ACT.Copy).then_inc(S["rows_ready"], 1)
                nc.scalar.activation(wt[1], bank[3][:], ACT.Copy).then_inc(S["rows_ready"], 1)
                nc.scalar.activation(wt[2][0:H, :], bank[0][0:H, :], ACT.Copy).then_inc(S["rows_ready"], 1)

            def chunk(i, kind, nxt):
                n, base = products_of(kind), before(i, kind)
                act.wait_ge(S["gate_psum"], i + 1)
                if later(i):
                    act.wait_ge(S["gated"], i)
                nc.scalar.activation(th, bank[1][:], ACT.Tanh, scale=0.5, bias=halfgb[:]).then_inc(S["gate_ready"], 1)
                if nxt is not None:
                    head(nxt)
                act.wait_ge(S["a0_ready"], i + 1)
                nc.scalar.activation(ah[0][:], af[0][:], ACT.Copy).then_inc(S["a0_high"], 1)
                if nxt is not None:
                    queries(nxt, base + n)
                act.wait_ge(S["a1_ready"], i + 1)
                nc.scalar.activation(ah[1][:], af[1][:], ACT.Copy).then_inc(S["a1_high"], 1)
                if kind >= g2_first:
                    act.wait_ge(S["a2_ready"], i + (1 - g2_first))
                    nc.scalar.activation(ah[2][0:H, :], af[0][0:H, :], ACT.Copy).then_inc(S["a2_high"], 1)
                if nxt is not None:
                    weights(nxt)

            head(0)
            queries(0, None)
            weights(0)
            chunk(0, 0, 1)
            for lo, hi in RANGES:
                with act.Fori(lo, hi) as i:
                    chunk(i, lo, i + 1)
            chunk(CHUNKS - 1, CHUNKS - 1, None)

            def ffn(f):
                s_ = FS[f]

                def prepare(i, q):
                    u = q % 2
                    act.wait_ge(s_["xn"], i + 1)
                    nc.scalar.activation(sl(XN, i * CW, CW), xn[u][:, :], ACT.Copy).then_inc(s_["kept"], 1)
                    act.wait_ge(s_["xT_psum"], i + 1)
                    if later(i):
                        act.wait_ge(s_["lT_psum"], i)
                    nc.scalar.activation(xnT[:], bank[u][:], ACT.Copy).then_inc(s_["xT"], 1)

                def logits_out(r):
                    act.wait_ge(s_["lT_psum"], r * 4 + 4)
                    if later(r):
                        act.wait_ge(s_["lg_psum"], r)
                    nc.scalar.activation(lT, bank[2][:], ACT.Copy).then_inc(s_["lT"], 1)

                for q in range(4):
                    prepare(q, q)
                logits_out(0)
                with act.Fori(1, CHUNKS // 4) as r:
                    for q in range(4):
                        prepare(r * 4 + q, q)
                    logits_out(r)

                def turned(s, u):
                    act.wait_ge(s_["transposed"], s + 1)
                    if not isinstance(s, int) or s >= 2:
                        act.wait_ge(s_["hidden"], s - 1)
                    nc.scalar.activation(xTb[u], bank[u][:, 0:P], ACT.Copy).then_inc(s_["turned"], 1)

                def gelu(s, u):
                    act.wait_ge(s_["biased"], s + 1)
                    if not isinstance(s, int) or s >= 2:
                        act.wait_ge(s_["y_psum"], s - 1)
                    nc.scalar.activation(hT[u], hb[u], ACT.Gelu).then_inc(s_["gelu"], 1)

                turned(0, 0)
                turned(1, 1)
                gelu(0, 0)
                turned(2, 0)
                gelu(1, 1)
                with act.Fori(1, (SLOT_TILES - 1) // 2) as j:
                    turned(j * 2 + 1, 1)
                    gelu(j * 2, 0)
                    turned(j * 2 + 2, 0)
                    gelu(j * 2 + 1, 1)
                gelu(SLOT_TILES - 1, 0)

            if stage >= 2:
                ffn(0)
            if stage >= 3:
                def steps(i, u):
                    for k in range(CT):
                        act.wait_ge(S["step_psum"], i * CT + (k + 1))
                        nc.scalar.activation(hid[u][:, k * NB:(k + 1) * NB], bank[u][:, k * NB:(k + 1) * NB],
                                             ACT.Tanh).then_inc(S["h_ready"], 1)

                with act.Fori(0, CHUNKS // 2) as j:
                    steps(j * 2, 0)
                    steps(j * 2 + 1, 1)
            if stage >= 4:
                ffn(1)

        @block.tensor
        def _(pe):
            pe.wait_ge(S["consts_in"], 32)
            pe.wait_ge(S["weights_in"], 16 * 15)
            for j in range(8):
                nc.tensor.transpose(bank[j // 4][:, (j % 4) * P:(j % 4 + 1) * P], wload[:, j * D:(j + 1) * D], ident)
            nc.tensor.transpose(bank[2][:, 0:NE], small[0:NE, 0:D], ident[0:NE, 0:NE])
            nc.tensor.transpose(bank[2][:, 32:64], small[0:32, P:2 * P], ident[0:32, 0:32])
            nc.tensor.transpose(bank[2][:, 64:64 + NS], srows, ident[0:NS, 0:NS])
            pe.wait_ge(S["filled"], 1)
            nc.tensor.matmul(bank[3][:, 0:H * NS], ones[0:1, :], prow[:], start=True, stop=True).then_inc(S["wT_psum"], 1)
            pe.wait_ge(S["setup_done"], 1)

            def tokens(n):
                pe.wait_ge(S["xn_ready"], n + 1)
                for c in range(TPC):
                    last = nc.tensor.transpose(bank[0][:, c * P:(c + 1) * P], xn[0][:, c * D:(c + 1) * D], ident)
                last.then_inc(S["xT_psum"], 1)
                pe.wait_ge(S["xT_ready"], n + 1)
                for j in range(2):
                    nc.tensor.matmul(bank[2 + j][:], projT[:, (1 + j) * D:(2 + j) * D], xnT[:],
                                     start=True, stop=True).then_inc(S["kv_psum"], 1)

            def queries(n):
                nc.tensor.matmul(bank[1][:], projT[:, 0:D], xnT[:], start=True, stop=True).then_inc(S["q_psum"], 1)

            def logits(n):
                pe.wait_ge(S["q_ready"], n + 1)
                pe.wait_ge(S["kv_ready"], n * 2 + 2)
                w = H * NS
                for c in range(TPC):
                    last = nc.tensor.matmul(bank[2 + c // 2][:, (c % 2) * w:(c % 2 + 1) * w], qT[:, c * P:(c + 1) * P],
                                            mqs[:], start=True, stop=True)
                last.then_inc(S["logits"], 1)

            def weight_rows(n):
                pe.wait_ge(S["weights_ready"], n + 1)
                for c in range(TPC):
                    cs = slice(c * P, (c + 1) * P)
                    nc.tensor.transpose(bank[2][:, cs], w01[0][:, cs], ident)
                    nc.tensor.transpose(bank[3][:, cs], w01[1][:, cs], ident)
                    last = nc.tensor.transpose(bank[0][0:H, cs], w8[:, c * H:(c + 1) * H], ident)
                last.then_inc(S["rows_psum"], 1)

            def output(n):
                pe.wait_ge(S["gated"], n + 1)
                for c in range(TPC):
                    last = nc.tensor.matmul(bank[0][:, c * D:(c + 1) * D], att[:, c * P:(c + 1) * P], outT[:],
                                            start=True, stop=True)
                last.then_inc(S["y_psum"], 1)

            sel = [cst[:, C_SEL + 32 * s:C_SEL + 32 * s + 32] for s in range(2)]

            def chunk(i, kind, nxt):
                g0, g1, g2 = active(kind)
                base = before(i, kind)
                if later(i):
                    pe.wait_ge(S["terms_ready"], base)
                pe.wait_ge(S["products_ready"], base + 1)
                nc.tensor.matmul(bank[6][:], blkw[:], prod[0], start=True, stop=True).then_inc(S["products_used"], 1)
                pe.wait_ge(S["rows_ready"], i * 3 + 3)
                nc.tensor.matmul(bank[1][:], projT[:, 3 * D:4 * D], xnT[:], start=True, stop=True).then_inc(S["gate_psum"], 1)
                if later(i):
                    output(i - 1)
                count = [0]

                def reduce(ms, bk):
                    for q in range(4):
                        if 2 * q not in ms:
                            nc.tensor.matmul(bank[bk][32 * q:32 * q + 32, :], sel[0], zero[:], start=True, stop=True)
                    for m in ms:
                        q, s = divmod(m, 2)
                        count[0] += 1
                        pe.wait_ge(S["products_ready"], base + (count[0] + 1))
                        nc.tensor.matmul(bank[bk][32 * q:32 * q + 32, :], sel[s], prod[count[0] % NPROD], start=(s == 0),
                                         stop=(s == 1 or m + 1 not in ms)).then_inc(S["products_used"], 1)

                reduce(g0, 4)
                if nxt is not None:
                    if later(i):
                        pe.wait_ge(S["resid"], i)
                    tokens(nxt)
                    pe.wait_ge(S["gate_ready"], i + 1)
                    queries(nxt)
                reduce(g1, 5)
                if g2:
                    count[0] += 1
                    pe.wait_ge(S["products_ready"], base + (count[0] + 1))
                    pe.wait_ge(S["a0_ready"], i + 1)
                    nc.tensor.matmul(bank[4][0:32, :], sel[0], prod[count[0] % NPROD], start=True,
                                     stop=True).then_inc(S["products_used"], 1)
                j = 0
                for g, ms in enumerate((g0, g1, [0] if g2 else [])):
                    if ms:
                        pe.wait_ge(S[f"a{g}_low"], i + 1 if g < 2 else i + (1 - g2_first))
                    for k, m in enumerate(ms):
                        j += 1
                        if j >= 2:
                            pe.wait_ge(S["terms_ready"], base + (j - 1))
                        lhs = esel[:, m * P:(m + 1) * P]
                        nc.tensor.matmul(bank[6 + j % 2][:], lhs, ah[g][:], start=True, stop=False)
                        nc.tensor.matmul(bank[6 + j % 2][:], lhs, al[g][:], start=False, stop=True).then_inc(
                            S["spread_ready"], 1)
                        if nxt is not None and (g, k) == (0, 0):
                            logits(nxt)
                        if nxt is not None and (g, k) == (1, 2):
                            weight_rows(nxt)

            tokens(0)
            queries(0)
            logits(0)
            weight_rows(0)
            chunk(0, 0, 1)
            for lo, hi in RANGES:
                with pe.Fori(lo, hi) as i:
                    chunk(i, lo, i + 1)
            chunk(CHUNKS - 1, CHUNKS - 1, None)
            output(CHUNKS - 1)

            def ffn(f):
                s_ = FS[f]

                def prepare(i, q):
                    u = q % 2
                    pe.wait_ge(s_["xn"], i + 1)
                    if not isinstance(i, int) or i >= 2:
                        pe.wait_ge(s_["xT"], i - 1)
                    for c in range(TPC):
                        last = nc.tensor.transpose(bank[u][:, c * P:(c + 1) * P], xn[u][:, c * D:(c + 1) * D], ident)
                    last.then_inc(s_["xT_psum"], 1)

                def logits(i, q):
                    pe.wait_ge(s_["xT"], i + 1)
                    nc.tensor.matmul(bank[2][32 * q:32 * q + 32, :], wgT[:], xnT[:], start=True,
                                     stop=True).then_inc(s_["lT_psum"], 1)

                def logit_rows(r):
                    pe.wait_ge(s_["lT"], r + 1)
                    if later(r):
                        pe.wait_ge(s_["lg"], r)
                    for c in range(TPC):
                        last = nc.tensor.transpose(bank[3][:, c * P:(c + 1) * P], lT[:, c * P:(c + 1) * P], ident)
                    last.then_inc(s_["lg_psum"], 1)

                def four(r):
                    for q in range(4):
                        i = r * 4 + q
                        prepare(i, q)
                        if q == 0 and later(r):
                            pe.wait_ge(s_["lT"], r)
                        logits(i, q)
                    logit_rows(r)

                four(0)
                with pe.Fori(1, CHUNKS // 4) as r:
                    four(r)
                pe.wait_ge(s_["onehot"], 1)
                nc.tensor.matmul(bank[4][:], cst[:, C_UP:C_UP + P], oh, start=True, stop=True)
                nc.tensor.matmul(bank[5][:], ones[:], oh, start=True, stop=True).then_inc(s_["counts"], 1)

                def turn(s, u, uses):
                    pe.wait_ge(s_["xs_in"][u], uses * 16)
                    if not isinstance(s, int) or s >= 2:
                        pe.wait_ge(s_["turned"], s - 1)
                    nc.tensor.transpose(bank[u % 2][:, 0:P], xsb[u], ident).then_inc(s_["transposed"], 1)

                def hidden(s, u, uses):
                    pe.wait_ge(s_["turned"], s + 1)
                    pe.wait_ge(s_["w1_in"][u], uses * 16)
                    if not isinstance(s, int) or s >= 2:
                        pe.wait_ge(s_["biased"], s - 1)
                    for c in range(HC):
                        last = nc.tensor.matmul(bank[2 + u % 2][:, c * P:(c + 1) * P], w1b[u][:, c * P:(c + 1) * P],
                                                xTb[u % 2], start=True, stop=True)
                    last.then_inc(s_["hidden"], 1)

                def result(s, u):
                    e = pe.value_load(sl(te_i, s, 1), min_val=0, max_val=NE - 1)
                    pe.wait_ge(s_["gelu"], s + 1)
                    if not isinstance(s, int) or s >= 2:
                        pe.wait_ge(s_["y_ready"], s - 1)
                    for c in range(HC):
                        last = nc.tensor.matmul(bank[4 + u % 2][:, 0:D], hT[u % 2][:, c * P:(c + 1) * P],
                                                w2[:, ds(e * (HC * D) + c * D, D)], start=(c == 0), stop=(c == HC - 1))
                    last.then_inc(s_["y_psum"], 1)

                def tile(s, u, uses):
                    if not isinstance(s, int) or s + 1 < SLOT_TILES:
                        turn(s + 1, (u + 1) % RING, uses + (u + 1) // RING)
                    hidden(s, u, uses)
                    if not isinstance(s, int) or s >= 2:
                        result(s - 2, (u - 2) % RING)

                pe.wait_ge(s_["slots_ready"], 2)
                turn(0, 0, 1)
                for s in range(RING):
                    tile(s, s, 1)
                with pe.Fori(1, SLOT_TILES // RING) as j:
                    for u in range(RING):
                        tile(j * RING + u, u, j + 1)
                for s in range(SLOT_TILES // RING * RING, SLOT_TILES):
                    tile(s, s % RING, s // RING + 1)
                for s in (SLOT_TILES - 2, SLOT_TILES - 1):
                    result(s, s % RING)

            if stage >= 2:
                pe.wait_ge(S["w2_in"], 32)
                ffn(0)

            def recurrence():
                def prepare(i, u):
                    pe.wait_ge(S["r_xn"], i + 1)
                    for c in range(TPC):
                        last = nc.tensor.transpose(bank[2][:, c * P:(c + 1) * P], xn[u][:, c * D:(c + 1) * D], ident)
                    last.then_inc(S["r_xT_psum"], 1)

                def inputs(i, u):
                    pe.wait_ge(S["r_xT"], i + 1)
                    nc.tensor.matmul(bank[u][:], abcT[:, D:2 * D], xnT[:], start=True, stop=True,
                                     skip_group_check=True).then_inc(S["r_xb"], 1)

                def output(i, u):
                    if later(i):
                        pe.wait_ge(S["r_stats2"], i)
                    for c in range(TPC):
                        last = nc.tensor.matmul(bank[3][:, c * D:(c + 1) * D], hid[u][:, c * P:(c + 1) * P],
                                                abcT[:, 2 * D:3 * D], start=True, stop=True)
                    last.then_inc(S["r_y"], 1)

                def chunk(i, u, more, last_out):
                    for k in range(CT):
                        prev = hid[u][:, (k - 1) * NB:k * NB] if k else hid[1 - u][:, CW - NB:CW]
                        pe.wait_ge(S["h_ready"], i * CT + (k + 1))
                        for q in range(4):
                            last = nc.tensor.matmul(bank[u][32 * q:32 * q + 32, k * NB:(k + 1) * NB],
                                                    abcT[:, 32 * q:32 * q + 32], prev, start=False, stop=True,
                                                    skip_group_check=True)
                        last.then_inc(S["step_psum"], 1)
                        if k == 0 and last_out:
                            output(i - 1, 1 - u)
                        if k == 8 and more:
                            prepare(i + 1, 1 - u)
                        if k == 16 and more:
                            inputs(i + 1, 1 - u)

                prepare(0, 0)
                inputs(0, 0)
                chunk(0, 0, True, False)
                with pe.Fori(0, CHUNKS // 2 - 1) as j:
                    chunk(j * 2 + 1, 1, True, True)
                    chunk(j * 2 + 2, 0, True, True)
                chunk(CHUNKS - 1, 1, False, True)
                pe.wait_ge(S["h_ready"], CHUNKS * CT + 1)
                output(CHUNKS - 1, 1)

            if stage >= 3:
                recurrence()
            if stage >= 4:
                ffn(1)

        @block.vector
        def _(dve):
            V_ = nc.vector
            step = Steps(dve, S["dve_step"])
            V_.memset(zero[:], 0.0)
            V_.memset(ones[:], 1.0).then_inc(S["filled"], 1)
            V_.memset(K[:, 0:PAD], 0.0)
            V_.memset(V[:, 0:PAD], 0.0)
            step.done(V_.memset(wgT[:], 0.0))
            dve.wait_ge(S["consts_in"], 32)
            V_.tensor_copy(esel[:], eload)
            dve.wait_ge(S["filled"], 1)
            for t in (ah[2], al[2]):
                V_.tensor_copy(t[:], zero[:])
            dve.wait_ge(S["weights_in"], 16 * 15)
            V_.tensor_scalar(halfgb[:], qkvb[:, 3:4], 0.5, None, ALU.mult)
            dve.wait_ge(S["softplus"], 1)
            step.done(V_.scalar_tensor_tensor(out=byp[:, 4:5], in0=byp[:, 0:1], scalar=0.0, in1=byp[:, 3:4],
                                              op0=ALU.max, op1=ALU.add))
            step.wait()
            step.done(V_.tensor_scalar(byp[:, 5:6], byp[:, 4:5], D4[0], None, ALU.add))
            step.wait()
            V_.tensor_scalar(blkw[:], cst[:, C_BLK:C_BLK + P], byp[:, 5:6], None, ALU.mult)
            dve.wait_ge(S["wT_psum"], 1)
            V_.tensor_copy(projT[:], bank[0][:])
            V_.tensor_tensor(mqs[:].rearrange("p (h s) -> p h s", h=H),
                             cst[:, C_HM:C_HM + H].unsqueeze(2).broadcast_to([P, H, NS]),
                             bank[2][:, 64:64 + NS].unsqueeze(1).broadcast_to([P, H, NS]), ALU.mult)
            V_.tensor_scalar(outT[:], bank[1][:, 0:D], 0.5, None, ALU.mult)
            V_.tensor_copy(abcT[:], bank[1][:, D:4 * D])
            step.wait()
            V_.tensor_copy(wgT[:, 0:NE], bank[2][:, 0:NE])
            V_.tensor_copy(b1T[:], bank[2][:, 32:64])
            V_.tensor_copy(prior[:], bank[3][:, 0:H * NS]).then_inc(S["setup_done"], 1)
            dve.wait_ge(S["setup_done"], 1)

            def statistics(src, raw_of, ready):
                for c in range(TPC):
                    last = V_.bn_stats(raw_of(c), src(c))
                last.then_inc(ready, 1)

            def stats(n, j):
                if j is not None:
                    dve.wait_ge(x_in[j[0]], j[1])
                statistics(lambda c: sl(X, n * CW + c * D, D), lambda c: raw[:, 6 * c:6 * c + 6], S["stats"])

            def normalise(n):
                dve.wait_ge(S["rstd"], n + 1)
                if later(n):
                    dve.wait_ge(S["xT_psum"], n)
                for c in range(TPC):
                    last = V_.tensor_scalar(xn[0][:, c * D:(c + 1) * D], sl(X, n * CW + c * D, D), mean[:, c:c + 1],
                                            rstd[:, c:c + 1], ALU.subtract, ALU.mult)
                last.then_inc(S["xn_ready"], 1)

            def shift_logits(n):
                dve.wait_ge(S["logits"], n + 1)
                w = H * NS
                g3 = gains.rearrange("p (ch s) -> p ch s", s=NS)
                for k in range(2):
                    last = V_.tensor_tensor(gains[:, k * 2 * w:(k + 1) * 2 * w].rearrange("p (c w) -> p c w", c=2),
                                            bank[2 + k][:, 0:2 * w].rearrange("p (c w) -> p c w", c=2),
                                            prior[:].unsqueeze(1).broadcast_to([P, 2, w]), ALU.add)
                step.done(last)
                step.wait()
                step.done(V_.tensor_reduce(gmax, g3, X_AXIS, ALU.max))
                step.wait()
                V_.tensor_tensor(g3, g3, gmax.unsqueeze(2).broadcast_to([P, TPC * H, NS]),
                                 ALU.subtract).then_inc(S["shifted"], 1)

            def softmax(n):
                g3 = gains.rearrange("p (ch s) -> p ch s", s=NS)
                dve.wait_ge(S["exp"], n + 1)
                step.done(V_.tensor_reduce(gsum, g3, X_AXIS, ALU.add))
                step.wait()
                step.done(V_.reciprocal(gmax, gsum))
                step.wait()
                V_.tensor_tensor(g3, g3, gmax.unsqueeze(2).broadcast_to([P, TPC * H, NS]),
                                 ALU.mult).then_inc(S["gains_ready"], 1)

            def shift_weights(n):
                by_scale = gains.rearrange("p (c h s) -> p c s h", c=TPC, h=H)
                wv = w01[0][:].rearrange("p (c m h) -> p c m h", c=TPC, h=H)
                dve.wait_ge(S["scaled"], n * 3 + 3)
                for c in range(TPC):
                    V_.scalar_tensor_tensor(out=wv[:, c, 1:8, :], in0=by_scale[:, c, 0:7, :], scalar=D4[2],
                                            in1=wv[:, c, 1:8, :], op0=ALU.mult, op1=ALU.add)
                w8v = w8[:].rearrange("p (c h) -> p c h", c=TPC)
                V_.scalar_tensor_tensor(out=w8v, in0=by_scale[:, :, 7, :], scalar=D4[2], in1=w8v,
                                        op0=ALU.mult, op1=ALU.add).then_inc(S["weights_ready"], 1)

            def gate(n, adds):
                dve.wait_ge(S["gate_ready"], n + 1)
                dve.wait_ge(S["terms_added"], adds)
                V_.scalar_tensor_tensor(out=att, in0=th, scalar=1.0, in1=acc, op0=ALU.add,
                                        op1=ALU.mult).then_inc(S["gated"], 1)

            def residual(n):
                dve.wait_ge(S["y_psum"], n + 1)
                dve.wait_ge(S["xb_ready"], n + 1)
                V_.tensor_tensor(sl(X, n * CW, CW), sl(X, n * CW, CW), bank[0][:], ALU.add).then_inc(S["resid"], 1)

            STEPS = 4

            def chunk(i, kind, nxt, loaded):
                g0, g1, g2 = active(kind)
                n, base = products_of(kind), before(i, kind)
                adds = spread_before(i, kind)
                shifts = [0] + [POW[m] for m in g0] + [TRI[m] for m in g1] + ([POW[8]] if g2 else [])
                assert len(shifts) == n

                def product(j):
                    if j >= NPROD:
                        dve.wait_ge(S["products_used"], base + (j - NPROD + 1))
                    elif later(i):
                        dve.wait_ge(S["products_used"], base)
                    V_.tensor_tensor(prod[j % NPROD], qT, sl(K, i * CW + (PAD - NB * shifts[j]), CW),
                                     ALU.mult).then_inc(S["products_ready"], 1)

                def pack(g, bk, used, h=P):
                    dve.wait_ge(S["products_used"], used)
                    V_.tensor_tensor(af[g % 2][0:h, :], bank[bk][0:h, :], wt[g][0:h, :], ALU.mult).then_inc(
                        S[f"a{g}_ready"], 1)

                def low(g, h=P):
                    dve.wait_ge(S[f"a{g}_high"], i + 1 if g < 2 else i + (1 - g2_first))
                    V_.tensor_tensor(al[g][0:h, :], af[g % 2][0:h, :], ah[g][0:h, :].bitcast(F32),
                                     ALU.subtract).then_inc(S[f"a{g}_low"], 1)

                def make_term(j):
                    if j == 0:
                        dve.wait_ge(S["products_used"], base + 1)
                    else:
                        dve.wait_ge(S["spread_ready"], adds + j)
                    if j >= NTERM:
                        dve.wait_ge(S["terms_added"], adds + max(1, j - NTERM))
                    elif later(i):
                        dve.wait_ge(S["terms_added"], adds)
                    V_.tensor_tensor(term[j % NTERM], bank[6 + j % 2][:], sl(V, i * CW + (PAD - NB * shifts[j]), CW),
                                     ALU.mult).then_inc(S["terms_ready"], 1)

                dve.wait_ge(S["q_ready"], i + 1)
                dve.wait_ge(S["kv_ready"], i * 2 + 2)
                product(0)
                if later(i):
                    gate(i - 1, adds)
                if nxt is not None:
                    stats(nxt, loaded)
                for j in range(1, 5):
                    product(j)
                if later(i):
                    residual(i - 1)
                if nxt is not None:
                    normalise(nxt)
                split = min(1 + len(g0) + 2, n)
                for j in range(5, split):
                    product(j)
                dve.wait_ge(S["rows_ready"], i * 3 + 3)
                pack(0, 4, base + (1 + len(g0)))
                for j in range(split, 1 + len(g0) + len(g1)):
                    product(j)
                low(0)
                if g2:
                    product(n - 1)
                pack(1, 5, base + (1 + len(g0) + len(g1)))
                make_term(0)
                if g2:
                    pack(2, 4, base + n, H)
                low(1)
                if g2:
                    low(2, H)
                for j in range(1, n):
                    make_term(j)
                    if nxt is not None:
                        if j == 3:
                            shift_logits(nxt)
                        if j == 5:
                            softmax(nxt)
                        if j == 7:
                            shift_weights(nxt)

            stats(0, (0, 16 * TPC))
            normalise(0)
            shift_logits(0)
            softmax(0)
            shift_weights(0)
            chunk(0, 0, 1, (1, 16 * TPC))
            for lo, hi in RANGES:
                start = step.n
                for x in range(lo + 1, hi + 1):
                    dve.wait_ge(x_in[x % 4], 16 * TPC * (x // 4 + 1))
                with dve.Fori(lo, hi) as i:
                    step.enter(start, i - lo, STEPS)
                    chunk(i, lo, i + 1, None)
                    assert step.n == STEPS
                step.leave(start + (hi - lo) * STEPS)
            chunk(CHUNKS - 1, CHUNKS - 1, None, None)
            gate(CHUNKS - 1, PRODUCTS_BEFORE[CHUNKS] - CHUNKS)
            residual(CHUNKS - 1)
            dve.wait_ge(S["resid"], CHUNKS)

            def all_statistics(ready):
                with dve.Fori(0, CHUNKS) as i:
                    statistics(lambda c: sl(X, i * CW + c * D, D), lambda c: sl(raw, i * (6 * TPC) + 6 * c, 6), ready)

            def normalise_chunk(i, u, ready):
                for c in range(TPC):
                    last = V_.tensor_scalar(xn[u][:, c * D:(c + 1) * D], sl(X, i * CW + c * D, D),
                                            sl(mean, i * TPC + c, 1), sl(rstd, i * TPC + c, 1),
                                            ALU.subtract, ALU.mult)
                last.then_inc(ready, 1)

            def ffn(f):
                s_ = FS[f]
                all_statistics(s_["stats"])
                dve.wait_ge(s_["rstd"], 1)

                def prepare(i, q):
                    if not isinstance(i, int) or i >= 2:
                        dve.wait_ge(s_["xT_psum"], i - 1)
                        dve.wait_ge(s_["kept"], i - 1)
                    normalise_chunk(i, q % 2, s_["xn"])

                def logits_out(r):
                    dve.wait_ge(s_["lg_psum"], r + 1)
                    n = 4 * TPC * NE
                    V_.tensor_copy(sl(lg, r * n, n).rearrange("p (q c e) -> p q c e", q=4, e=NE),
                                   bank[3][:].rearrange("p (c q e) -> p q c e", q=4, e=32)[:, :, :, 0:NE]
                                   ).then_inc(s_["lg"], 1)

                for q in range(4):
                    prepare(q, q)
                with dve.Fori(1, CHUNKS // 4) as r:
                    for q in range(4):
                        prepare(r * 4 + q, q)
                    logits_out(r - 1)
                logits_out(CHUNKS // 4 - 1)
                dve.wait_ge(s_["lg"], CHUNKS // 4)

                def v3(t):
                    return t.rearrange("p (g e) -> p g e", e=NE)

                full = [P, TILES, NE]
                rev = cst[:, C_REV:C_REV + NE].unsqueeze(1).broadcast_to(full)
                step.done(V_.tensor_reduce(m64, v3(lg), X_AXIS, ALU.max))
                step.wait()
                step.done(V_.tensor_tensor(v3(tmp), v3(lg), m64.unsqueeze(2).broadcast_to(full), ALU.is_equal))
                step.wait()
                step.done(V_.tensor_tensor(v3(tmp), v3(tmp), rev, ALU.mult))
                step.wait()
                step.done(V_.tensor_reduce(m64, v3(tmp), X_AXIS, ALU.max))
                step.wait()
                V_.tensor_tensor(v3(oh), v3(tmp), m64.unsqueeze(2).broadcast_to(full), ALU.is_equal).then_inc(s_["onehot"], 1)
                dve.wait_ge(s_["onehot"], 1)
                dve.wait_ge(s_["counts"], 1)
                tot = v3(bank[5][:])
                inc3 = incl.rearrange("p (e g) -> p e g", e=NE)
                for e in range(NE):
                    last = V_.tensor_tensor_scan(inc3[:, e, :], ones[:, 0:TILES], tot[:, :, e], 0.0, ALU.mult, ALU.add)
                step.done(last)
                step.wait()
                kt = cst[:, C_KT:C_KT + TILES].unsqueeze(1).broadcast_to([P, NE, TILES])
                step.done(V_.tensor_tensor(tmp.rearrange("p (e k) -> p e k", e=NE),
                                           inc3[:, :, TILES - 1:TILES].broadcast_to([P, NE, TILES]), kt, ALU.is_gt))
                step.wait()
                step.done(V_.tensor_reduce(ntl, tmp.rearrange("p (e k) -> p e k", e=NE), X_AXIS, ALU.add))
                step.wait()
                step.done(V_.tensor_tensor_scan(ctl, ones[:, 0:NE], ntl, 0.0, ALU.mult, ALU.add))
                step.wait()
                step.done(V_.tensor_tensor(bas, ctl, ntl, ALU.subtract))
                step.done(V_.tensor_tensor(v3(tmp), incl.rearrange("p (e g) -> p g e", e=NE), tot, ALU.subtract))
                step.wait()
                step.done(V_.tensor_tensor(v3(tmp), v3(tmp), v3(bank[4][:]), ALU.add))
                step.wait()
                step.done(V_.scalar_tensor_tensor(out=v3(tmp), in0=bas.unsqueeze(1).broadcast_to(full), scalar=float(P),
                                                  in1=v3(tmp), op0=ALU.mult, op1=ALU.add))
                step.wait()
                step.done(V_.tensor_tensor(tmp, tmp, oh, ALU.mult))
                step.wait()
                step.done(V_.tensor_reduce(slotf, v3(tmp), X_AXIS, ALU.add))
                step.wait()
                V_.tensor_copy(slot_i[:], slotf).then_inc(s_["slots_ready"], 1)
                ns = [1, SLOT_TILES, NE - 1]
                t3 = lg[0:1, 0:SLOT_TILES * (NE - 1)] if SLOT_TILES * (NE - 1) <= TILES * NE else None
                step.done(V_.tensor_tensor(t3.rearrange("p (s e) -> p s e", e=NE - 1),
                                           cst[0:1, C_SI:C_SI + SLOT_TILES].unsqueeze(2).broadcast_to(ns),
                                           ctl[0:1, 0:NE - 1].unsqueeze(1).broadcast_to(ns), ALU.is_ge))
                step.wait()
                step.done(V_.tensor_reduce(tef[0:1, :], t3.rearrange("p (s e) -> p s e", e=NE - 1), X_AXIS, ALU.add))
                step.wait()
                V_.tensor_copy(te_i[:], tef[0:1, :]).then_inc(s_["slots_ready"], 1)
                dve.wait_ge(s_["slots_ready"], 2)

                def bias(s, u):
                    e = dve.value_load(sl(te_i, s, 1), min_val=0, max_val=NE - 1)
                    dve.wait_ge(s_["hidden"], s + 1)
                    if not isinstance(s, int) or s >= 2:
                        dve.wait_ge(s_["gelu"], s - 1)
                    V_.tensor_tensor(hb[u].rearrange("p (c t) -> p c t", c=HC), bank[2 + u][:].rearrange("p (c t) -> p c t", c=HC),
                                     b1T[:, ds(e * HC, HC)].unsqueeze(2).broadcast_to([P, HC, P]),
                                     ALU.add).then_inc(s_["biased"], 1)

                def result(s, u, uses):
                    e = dve.value_load(sl(te_i, s, 1), min_val=0, max_val=NE - 1)
                    dve.wait_ge(s_["y_psum"], s + 1)
                    if uses is not None:
                        dve.wait_ge(s_["ys_out"][u], uses * 16)
                    V_.tensor_tensor(ysb[u], bank[4 + u][:, 0:D], b2bc[:, ds(e * D, D)], ALU.add).then_inc(s_["y_ready"], 1)

                bias(0, 0)
                bias(1, 1)
                bias(2, 0)
                result(0, 0, None)
                bias(3, 1)
                result(1, 1, None)
                with dve.Fori(2, (SLOT_TILES - 1) // 2) as j:
                    bias(j * 2, 0)
                    result(j * 2 - 2, 0, j - 1)
                    bias(j * 2 + 1, 1)
                    result(j * 2 - 1, 1, j - 1)
                s = SLOT_TILES - 1
                bias(s, 0)
                for k in (2, 1, 0):
                    result(s - k, (s - k) % 2, (s - k) // 2)
                for q in range(4):
                    dve.wait_ge(s_["gathered"][q], 16 * TILES // 4)
                    w = TILES * D // 4
                    V_.tensor_tensor(X[:, q * w:(q + 1) * w], X[:, q * w:(q + 1) * w], XN[:, q * w:(q + 1) * w],
                                     ALU.add).then_inc(s_["added"], 1)

            if stage >= 2:
                dve.wait_ge(S["w2_in"], 32)
                ffn(0)

            def recurrence():
                dve.wait_ge(FS[0]["added"], 4)
                V_.memset(hid[1][:, CW - NB:CW], 0.0).then_inc(S["h_ready"], 1)
                all_statistics(S["r_stats"])
                dve.wait_ge(S["r_rstd"], 1)

                def prepare(i, u):
                    normalise_chunk(i, u, S["r_xn"])
                    dve.wait_ge(S["r_xn"], i + 1)
                    V_.tensor_copy(sl(XN, i * CW, CW), xn[u][:, :]).then_inc(S["r_kept"], 1)
                    dve.wait_ge(S["r_xT_psum"], i + 1)
                    if later(i):
                        dve.wait_ge(S["r_xb"], i)
                    V_.tensor_copy(xnT[:], bank[2][:]).then_inc(S["r_xT"], 1)

                def output(i):
                    dve.wait_ge(S["r_y"], i + 1)
                    dve.wait_ge(S["r_kept"], i + 1)
                    if later(i):
                        dve.wait_ge(S["r_out"], i)
                    step.done(V_.tensor_tensor(res, sl(XN, i * CW, CW), bank[3][:], ALU.add))
                    step.wait()
                    statistics(lambda c: res[:, c * D:(c + 1) * D], lambda c: raw2[:, 6 * c:6 * c + 6], S["r_stats2"])
                    dve.wait_ge(S["r_rstd2"], i + 1)
                    for c in range(TPC):
                        last = V_.tensor_scalar(res[:, c * D:(c + 1) * D], res[:, c * D:(c + 1) * D],
                                                mean2[:, c:c + 1], rstd2[:, c:c + 1], ALU.subtract, ALU.mult)
                    step.done(last)
                    step.wait()
                    r3 = res.rearrange("p (c d) -> p c d", d=D)
                    step.done(V_.tensor_tensor(r3, r3, bc_out(brow[:, D:2 * D]), ALU.mult))
                    step.wait()
                    step.done(V_.tensor_tensor(r3, r3, bc_out(brow[:, 2 * D:3 * D]), ALU.add))
                    step.wait()
                    V_.tensor_tensor(sl(X, i * CW, CW), sl(X, i * CW, CW), res, ALU.add).then_inc(S["r_out"], 1)

                prepare(0, 0)
                prepare(1, 1)
                output(0)
                prepare(2, 0)
                start, rounds = step.n, CHUNKS // 2 - 2
                with dve.Fori(0, rounds) as j:
                    step.enter(start, j, 8)
                    output(j * 2 + 1)
                    prepare(j * 2 + 3, 1)
                    output(j * 2 + 2)
                    prepare(j * 2 + 4, 0)
                    assert step.n == 8
                step.leave(start + 8 * rounds)
                output(CHUNKS - 3)
                prepare(CHUNKS - 1, 1)
                output(CHUNKS - 2)
                output(CHUNKS - 1)
                dve.wait_ge(S["r_out"], CHUNKS)

            if stage >= 3:
                recurrence()
            if stage >= 4:
                ffn(1)


_ARGS = {
    "x": "L0_attn_a_x", "W_qkv": "L0_attn_a_W_qkv", "b_qkv": "L0_attn_a_b_qkv", "W_out": "L0_attn_a_W_out",
    "b_out": "L0_attn_a_b_out", "W_gate": "L0_attn_a_W_gate", "b_gate": "L0_attn_a_b_gate",
    "scale_gain": "L0_attn_a_scale_gain", "W_qscale": "L0_attn_a_W_qscale",
    "identity_bypass": "L0_attn_a_identity_bypass", "A": "L0_attn_b_A", "B": "L0_attn_b_B", "C": "L0_attn_b_C",
    "gamma": "L0_attn_b_gamma", "beta": "L0_attn_b_beta", "Wg": "L0_ffn_Wg", "W1": "L0_ffn_W1", "b1": "L0_ffn_b1",
    "W2": "L0_ffn_W2", "b2": "L0_ffn_b2",
}


def kernel(**inputs):
    import concourse.bacc as _bacc
    from concourse.bass_utils import run_bass_kernel_spmd as _run

    nc = _bacc.Bacc("TRN2", target_bir_lowering=False, num_devices=1)
    arrays, args = {}, {}
    for short, name in _ARGS.items():
        arr = np.ascontiguousarray(inputs[name])
        arrays[f"in_{short}"] = arr
        args[short] = nc.dram_tensor(f"in_{short}", arr.shape, mybir.dt.from_np(arr.dtype), kind="ExternalInput").ap()
    arrays["in_consts"] = constants()
    consts = nc.dram_tensor("in_consts", (P, C_ALL), F32, kind="ExternalInput").ap()
    out = nc.dram_tensor("out_x", (NB, NT, D), F32, kind="ExternalOutput").ap()
    build(nc, args, consts, out, STAGE)
    r = _run(nc, [arrays], core_ids=[0])
    return r.results[0]["out_x"]
```

```python
from collections import namedtuple
from contextlib import ExitStack

import numpy as np

import concourse.bass as bass
from concourse import mybir

F32 = mybir.dt.float32
F32R = mybir.dt.float32r
I32 = mybir.dt.int32
ACT = mybir.ActivationFunctionType
ALU = mybir.AluOpType
X_AXIS = mybir.AxisListType.X
ds = bass.ds

P = 128
NB, NT, D, H, NS, NE, NH = 16, 512, 128, 16, 11, 8, 512
HD = D // H
TILES = NB * NT // P
TT = P // NB
CT = 32
CW = CT * NB
TPC = CW // P
CHUNKS = NT // CT
GROUPS = 4
GT = TILES // GROUPS
GC = CHUNKS // GROUPS
JOBS = 2 * GROUPS
HALF = 12
ST = 2 * HALF
PACK = 6
assert NE == 8 and ST % PACK == 0 and ST >= GT + NE - 1
HC = NH // P
RING = 6
EPS = 1e-5
D4 = [0.4829629131445341, 0.8365163037378079, 0.2241438680420134, -0.1294095225512604]

POW = [1 << m for m in range(9)]
TRI = [3 << m for m in range(8)]
PAD = 96 * NB

C_ID, C_UP, C_BLK, C_SEL = 0, 128, 256, 384
C_HM = C_SEL + 64
C_REV = C_HM + H
C_KT = C_REV + NE
C_SI = C_KT + GT
C_PW = C_SI + ST
C_KEPT = C_PW + ST
C_ESEL = C_KEPT
C_ALL = C_ESEL + 8 * P


def constants():
    c = np.zeros((P, C_ALL), np.float32)
    k = np.arange(P)
    c[:, C_ID:C_ID + P] = np.eye(P)
    c[:, C_UP:C_UP + P] = k[:, None] < k[None, :]
    c[:, C_BLK:C_BLK + P] = k[:, None] // HD == k[None, :] // HD
    for s in range(2):
        c[:, C_SEL + 32 * s + 16 * s:C_SEL + 32 * s + 16 * s + H] = k[:, None] // HD == np.arange(H)[None, :]
    for m in range(8):
        c[:, C_ESEL + P * m:C_ESEL + P * m + P] = k[:, None] == H * m + k[None, :] // HD
    c[:, C_HM:C_HM + H] = k[:, None] // HD == np.arange(H)[None, :]
    c[:, C_REV:C_REV + NE] = NE - np.arange(NE)
    c[:, C_KT:C_KT + GT] = P * np.arange(GT)
    c[:, C_SI:C_SI + ST] = np.arange(ST)
    c[:, C_PW:C_PW + ST] = NE ** (np.arange(ST) % PACK)
    return c


class Steps:

    def __init__(self, eng, sem):
        self.eng, self.sem, self.base, self.n = eng, sem, 0, 0

    def enter(self, start, i, per):
        self.base, self.n = i * per + start, 0

    def leave(self, total):
        self.base, self.n = 0, total

    def done(self, ins):
        ins.then_inc(self.sem, 1)
        self.n += 1

    def wait(self):
        self.eng.wait_ge(self.sem, self.base + self.n)


def active(i):
    last = CT * (i + 1) - 1
    g0 = [m for m in range(8) if POW[m] <= last]
    g1 = [m for m in range(8) if TRI[m] <= last]
    return g0, g1, POW[8] <= last


def products_of(i):
    g0, g1, g2 = active(i)
    return 1 + len(g0) + len(g1) + int(g2)


RANGES = [(1, 2), (2, 3), (3, 4), (4, 6), (6, 8), (8, 12), (12, CHUNKS - 1)]
for _lo, _hi in RANGES:
    assert all(active(x) == active(_lo) for x in range(_lo, _hi))
PRODUCTS_BEFORE = [sum(products_of(x) for x in range(i)) for i in range(CHUNKS + 1)]


def chunk_of(slot, h):
    return None if slot.pair is None else 2 * slot.pair + h


Slot = namedtuple("Slot", "tiles prep gather pair")
SLOTS = [
    Slot(None, 0, None, None),
    Slot(0, 1, None, None),
    Slot(1, 2, None, 0),
    Slot(2, 3, 1, 1),
    Slot(3, 4, 2, 2),
    Slot(4, None, 3, 3),
    Slot(None, 5, 4, 4),
    Slot(5, None, None, 5),
    Slot(None, 6, 5, 6),
    Slot(6, None, None, 7),
    Slot(None, 7, 6, None),
    Slot(7, None, None, None),
]
PREP_STEPS = [14 + 4 * q for q in range(GC)]
LEAD = 3
PIECES = 5 * HALF


def pieces_after(h, k):
    lead = LEAD if h == 0 else 0
    if k < lead:
        return []
    n = CT - lead
    return [(h * HALF + p // 5, p % 5) for p in range((k - lead) * PIECES // n, (k - lead + 1) * PIECES // n)]



def build(nc, a, consts, out):
    with ExitStack() as ctx:
        def sb(name, shape, dt=F32):
            return ctx.enter_context(nc.sbuf_tensor(name, shape, dt))

        def sem(name):
            return ctx.enter_context(nc.semaphore(name))

        xs = [nc.dram_tensor(f"sorted_x{f}", (ST * P, D), F32, kind="Internal").ap() for f in range(2)]
        ys = [nc.dram_tensor(f"sorted_y{f}", (ST * P, D), F32, kind="Internal").ap() for f in range(2)]

        X = sb("X", [P, TILES * D])
        XN = sb("XN", [P, TILES * D])
        cst = sb("cst", [P, C_KEPT])
        w2 = sb("w2", [P, NE * HC * D])
        b1T = sb("b1T", [P, NE * HC])
        b2bc = sb("b2bc", [P, NE * D])
        wgT = sb("wgT", [P, 32])
        projT = sb("projT", [P, 4 * D])
        outT = sb("outT", [P, D])
        abcT = sb("abcT", [P, 3 * D])
        qkvb = sb("qkvb", [P, 4])
        halfgb = sb("halfgb", [P, 1])
        brow = sb("brow", [P, 3 * D])
        zero = sb("zero", [P, 512])
        ones = sb("ones", [P, P])
        mqs = sb("mqs", [P, H * NS])
        prow = sb("prow", [1, H * NS])
        prior = sb("prior", [P, H * NS])
        byp = sb("byp", [P, 6])
        blkw = sb("blkw", [P, P])
        esel = sb("esel", [P, 8 * P], F32R)
        nums = sb("nums", [P, 4])
        raw = sb("raw", [P, GT * 6])
        mean = sb("mean", [P, GT])
        rstd = sb("rstd", [P, GT])
        raw2 = sb("raw2", [P, TPC * 6])
        mean2 = sb("mean2", [P, TPC])
        rstd2 = sb("rstd2", [P, TPC])
        raw3 = sb("raw3", [P, TPC * 6])
        mean3 = sb("mean3", [P, TPC])
        rstd3 = sb("rstd3", [P, TPC])
        mom = sb("mom", [P, 5 * GT])
        slot_i = sb("slot_i", [P, JOBS * GT], I32)
        te_i = sb("te_i", [1, JOBS * ST], I32)
        te_p = sb("te_p", [1, JOBS * ST // PACK], I32)
        xn = [sb("xn0", [P, CW])]
        xnT = sb("xnT", [P, CW])
        ah = [sb(f"ah{g}", [P, CW], F32R) for g in range(3)]
        al = [sb(f"al{g}", [P, CW], F32R) for g in range(3)]
        K = sb("K", [P, PAD + NB * NT])
        V = sb("V", [P, PAD + NB * NT])

        at = [0]

        def in_xn(n):
            at[0] += n
            assert at[0] <= TILES * D
            return XN[:, at[0] - n:at[0]]

        qT, th, acc, att = in_xn(CW), in_xn(CW), in_xn(CW), in_xn(CW)
        NPROD = 4
        prod = [in_xn(CW) for _ in range(NPROD)]
        NTERM = 4
        term = [in_xn(CW) for _ in range(NTERM)]
        gains = in_xn(TPC * H * NS)
        gmax, gsum = in_xn(TPC * H), in_xn(TPC * H)
        wload = V[:, PAD:PAD + 8 * D]
        small = V[:, PAD + 8 * D:PAD + 10 * D]
        srows = V[0:NS, PAD + 18 * D:PAD + 19 * D]
        eload = V[:, PAD + 10 * D:PAD + 18 * D]
        w8 = sb("w8", [P, TPC * H])
        w01 = [sb(f"w{g}", [P, TPC * P]) for g in range(2)]
        wt = [sb("wt0", [P, CW]), in_xn(CW), in_xn(CW)]
        af = [sb(f"af{g}", [P, CW]) for g in range(2)]

        kat = [0]

        def in_k(n):
            if kat[0] < PAD + NB * NT < kat[0] + n:
                kat[0] = PAD + NB * NT
            kat[0] += n
            end = kat[0] % (PAD + NB * NT)
            return (K if kat[0] <= PAD + NB * NT else V)[:, end - n:end]

        w1b = [in_k(NH) for _ in range(RING)]
        xsb = [in_k(P) for _ in range(RING)]
        xTb = [in_k(P) for _ in range(2)]
        hT = [in_k(HC * P) for _ in range(2)]
        ysb = [in_k(P) for _ in range(2)]
        lT = in_k(CW)
        lg = in_k(GT * NE)
        oh = in_k(GT * NE)
        tmp = in_k(GT * NE)
        incl = in_k(GT * NE)
        t3 = in_k(ST * (NE - 1))
        m64, slotf, tef = in_k(GT), in_k(GT), in_k(ST)
        ntl, ctl, bas = in_k(NE), in_k(NE), in_k(NE)
        hid = [in_k(CW) for _ in range(2)]
        res = in_k(CW)
        xrT = in_k(CW)

        bank = [ctx.enter_context(nc.psum_tensor(f"bank{j}", [P, 512], F32)) for j in range(8)]

        names = """consts_in weights_in w2_in norm_in filled wT_psum softplus setup_done
            zeros_written dve_step act_step pool_step
            stats rstd xn_ready xT_psum xT_ready kv_psum kv_ready q_psum q_ready gate_psum gate_ready
            logits shifted exp gains_ready scaled weights_ready rows_psum rows_ready
            products_ready products_used a0_ready a1_ready a2_ready a0_high a1_high a2_high
            a0_low a1_low a2_low spread_ready terms_ready terms_added gated y_psum xb_ready resid
            r_stats r_rstd r_xn r_xT_psum r_xT r_xb step_psum h_ready r_y r_stats2 r_rstd2 r_out
            f_stats f_rstd f_xn f_xT_psum f_xT f_lT_psum f_lT f_lg_psum f_lg f_onehot f_counts f_slots_ready f_scattered
            f_transposed f_turned f_hidden f_gelu f_y_psum f_y_ready f_gathered f_added out_stored""".split()
        S = {n: sem(n) for n in names}
        x_in = [sem(f"x_in{j}") for j in range(4)]
        xs_in = [sem(f"xs_in{u}") for u in range(RING)]
        w1_in = [sem(f"w1_in{u}") for u in range(RING)]
        ys_out = [sem(f"ys_out{u}") for u in range(2)]

        ident = cst[:, C_ID:C_ID + P]
        g2_first = next(i for i in range(CHUNKS) if active(i)[2])

        def sl(buf, at, width):
            return buf[:, at:at + width] if isinstance(at, int) else buf[:, ds(at, width)]

        def rows(t, at, n):
            return t[at:at + n, :] if isinstance(at, int) else t[ds(at, n), :]

        def x_dram(t, g):
            v = t.rearrange("b (g t) d -> g t b d", t=TT)
            return v[g] if isinstance(g, int) else v[ds(g, 1)].rearrange("a t b d -> (a t) b d")

        def later(i):
            return not isinstance(i, int) or i > 0

        def before(i, kind):
            return PRODUCTS_BEFORE[i] if isinstance(i, int) else (i - kind) * products_of(kind) + PRODUCTS_BEFORE[kind]

        def spread_before(i, kind):
            if isinstance(i, int):
                return PRODUCTS_BEFORE[i] - i
            return (i - kind) * (products_of(kind) - 1) + (PRODUCTS_BEFORE[kind] - kind)

        def packed_experts(eng, n):
            w = ST // PACK
            return [eng.value_load(te_p[:, n * w + k:n * w + k + 1], min_val=0, max_val=NE ** PACK - 1) for k in range(w)]

        def expert(words, s):
            return (words[s // PACK] >> (3 * (s % PACK))) & (NE - 1)

        def bc_out(v):
            return v.unsqueeze(1).broadcast_to([P, TPC, D])

        block = ctx.enter_context(nc.Block())

        @block.sync
        def _(sp):
            sp.dma_start(cst[:], consts[:, 0:C_KEPT]).then_inc(S["consts_in"], 16)
            sp.dma_start(eload, consts[:, C_ESEL:C_ALL]).then_inc(S["consts_in"], 16)
            for i in range(4):
                for c in range(TPC):
                    g = i * TPC + c
                    sp.dma_start(X[:, g * D:(g + 1) * D], x_dram(a["x"], g)).then_inc(x_in[i], 16)
            with sp.Fori(1, CHUNKS // 4) as r:
                for j in range(4):
                    sp.wait_ge(x_in[j], r * (16 * TPC))
                    for c in range(TPC):
                        g = r * (4 * TPC) + (j * TPC + c)
                        sp.dma_start(X[:, ds(g * D, D)], x_dram(a["x"], g)).then_inc(x_in[j], 16)
            sp.dma_start(w2[:].rearrange("p (e c d) -> p e c d", e=NE, c=HC),
                         a["W2"].rearrange("e (c p) d -> p e c d", p=P)).then_inc(S["w2_in"], 16)
            sp.dma_start(b2bc[:], a["b2"].rearrange("e d -> (e d)").partition_broadcast(P)).then_inc(S["w2_in"], 16)
            sp.wait_ge(S["filled"], 1)
            for f in range(2):
                v = xs[f].rearrange("(t p) d -> p t d", p=P)
                for t in range(0, ST, 4):
                    n = min(4, ST - t)
                    sp.dma_start(v[:, t:t + n, :],
                                 zero[:, 0:n * D].rearrange("p (t d) -> p t d", t=n)).then_inc(S["zeros_written"], 16)

            def load(n, s, u):
                if not isinstance(s, int) or n * ST + s >= RING:
                    sp.wait_ge(S["f_hidden"], s + (n * ST - (RING - 1)))
                e = sp.value_load(sl(te_i, s + n * ST, 1), min_val=0, max_val=NE - 1)
                sp.dma_start(xsb[u], rows(xs[n % 2], s * P, P)).then_inc(xs_in[u], 16)
                sp.dma_start(w1b[u], a["W1"][ds(e, 1), :, :].rearrange("a d h -> (a d) h")).then_inc(w1_in[u], 16)

            def store(n, s, u):
                sp.wait_ge(S["f_y_ready"], s + (n * ST + 1))
                sp.dma_start(rows(ys[n % 2], s * P, P), ysb[u % 2]).then_inc(ys_out[u % 2], 16)

            def tiles(n):
                sp.wait_ge(S["f_slots_ready"], 2 * n + 2)
                sp.wait_ge(S["f_scattered"], 16 * GT * (n + 1))
                for s in range(RING):
                    load(n, s, s)
                if n >= 2:
                    sp.wait_ge(S["f_added"], n - 1)
                with sp.Fori(1, ST // RING) as j:
                    for u in range(RING):
                        load(n, j * RING + u, u)
                        store(n, (j - 1) * RING + u, u)
                for s in range(ST - RING, ST):
                    store(n, s, s)

            def store_group(g):
                sp.wait_ge(S["f_added"], GROUPS + g + 1)
                with sp.Fori(g * GT, (g + 1) * GT) as t:
                    sp.dma_start(x_dram(out, t), X[:, ds(t * D, D)]).then_inc(S["out_stored"], 16)

            for n in range(JOBS):
                if n >= GROUPS + 2:
                    store_group(n - GROUPS - 2)
                tiles(n)
            for g in range(GROUPS - 2, GROUPS):
                store_group(g)
            sp.wait_ge(S["out_stored"], 16 * TILES)

        @block.gpsimd
        def _(pool):
            step = Steps(pool, S["pool_step"])
            for k, x in enumerate((-0.5, 0.5, 1.0 / D, EPS)):
                last = nc.gpsimd.memset(nums[:, k:k + 1], x)
            step.done(last)
            step.wait()

            def moments(r, mu, rs, n):
                def op(dst, x, y, o):
                    return nc.gpsimd.tensor_tensor(dst, x, y, o)

                r = r.rearrange("p (t s) -> p t s", s=6)
                m_even, q_even, m_odd, q_odd = (r[:, :, k] for k in (1, 2, 4, 5))
                total, diff, half, sq, var = (mom[:, k * GT:k * GT + n] for k in range(5))
                mhalf, phalf, inv, eps = (nums[:, k:k + 1].broadcast_to([P, n]) for k in range(4))
                op(total, m_even, m_odd, ALU.add)
                op(diff, m_even, m_odd, ALU.subtract)
                step.done(op(sq, q_even, q_odd, ALU.add))
                step.wait()
                op(mu, total, phalf, ALU.mult)
                op(half, diff, phalf, ALU.mult)
                step.done(op(var, sq, inv, ALU.mult))
                step.wait()
                op(diff, half, half, ALU.mult)
                step.done(op(total, var, eps, ALU.add))
                step.wait()
                step.done(op(var, total, diff, ALU.add))
                step.wait()
                return op(rs, var, mhalf, ALU.pow)

            MOMENTS = 4

            def head(n):
                pool.wait_ge(S["stats"], n + 1)
                moments(raw[:, 0:6 * TPC], mean[:, 0:TPC], rstd[:, 0:TPC], TPC).then_inc(S["rstd"], 1)
                pool.wait_ge(S["xn_ready"], n + 1)
                v = sl(X, n * CW, CW).rearrange("p (c d) -> p c d", d=D)
                nc.gpsimd.tensor_tensor(v, v, bc_out(brow[:, 0:D]), ALU.add).then_inc(S["xb_ready"], 1)

            def chunk(i, kind, nxt):
                n, base, adds = products_of(kind), before(i, kind), spread_before(i, kind)
                if nxt is not None:
                    head(nxt)
                if later(i):
                    pool.wait_ge(S["gated"], i)
                for j in range(1, n):
                    pool.wait_ge(S["terms_ready"], base + (j + 1))
                    if j > 1:
                        pool.wait_ge(S["terms_added"], adds + (j - 1))
                    nc.gpsimd.tensor_tensor(acc, acc if j > 1 else term[0], term[j % NTERM],
                                            ALU.add).then_inc(S["terms_added"], 1)

            pool.wait_ge(S["norm_in"], 16 * 3)
            head(0)
            chunk(0, 0, 1)
            for lo, hi in RANGES:
                start = step.n
                with pool.Fori(lo, hi) as i:
                    step.enter(start, i - lo, MOMENTS)
                    chunk(i, lo, i + 1)
                step.leave(start + (hi - lo) * MOMENTS)
            chunk(CHUNKS - 1, CHUNKS - 1, None)

            def scatter(n):
                pool.wait_ge(S["f_xn"], GC * (n + 1))
                pool.wait_ge(S["f_slots_ready"], 2 * n + 1)
                if n < 2:
                    pool.wait_ge(S["zeros_written"], 16 * 2 * ((ST + 3) // 4))
                else:
                    pool.wait_ge(S["f_hidden"], ST * (n - 1))
                for t in range(GT):
                    g = n % GROUPS * GT + t
                    nc.gpsimd.indirect_dma_start(
                        out=xs[n % 2], out_offset=bass.IndirectOffsetOnAxis(ap=slot_i[:, n * GT + t:n * GT + t + 1], axis=0),
                        in_=XN[:, g * D:(g + 1) * D], in_offset=None).then_inc(S["f_scattered"], 16)

            def gather(n):
                pool.wait_ge(S["f_scattered"], 16 * GT * (n + 1))
                for u in range(2):
                    pool.wait_ge(ys_out[u], 16 * (ST // 2) * (n + 1))
                for t in range(GT):
                    g = n % GROUPS * GT + t
                    nc.gpsimd.indirect_dma_start(
                        out=XN[:, g * D:(g + 1) * D], out_offset=None, in_=ys[n % 2],
                        in_offset=bass.IndirectOffsetOnAxis(ap=slot_i[:, n * GT + t:n * GT + t + 1], axis=0),
                    ).then_inc(S["f_gathered"], 16)

            def moments_in(c):
                pool.wait_ge(S["r_stats"], c + 1)
                moments(raw3[:], mean3[:], rstd3[:], TPC).then_inc(S["r_rstd"], 1)

            def moments_out(c):
                pool.wait_ge(S["r_stats2"], c + 1)
                moments(raw2[:], mean2[:], rstd2[:], TPC).then_inc(S["r_rstd2"], 1)

            def recurrence_moments(c):
                if c is not None:
                    if c > 0:
                        moments_out(c - 1)
                    if c + 1 < CHUNKS:
                        moments_in(c + 1)

            for slot in SLOTS:
                if slot.pair == 0:
                    gather(0)
                    moments_in(0)
                recurrence_moments(chunk_of(slot, 0))
                if slot.prep == JOBS - 1:
                    moments_out(CHUNKS - 1)
                if slot.prep is not None:
                    pool.wait_ge(S["f_stats"], GC * (slot.prep + 1))
                    moments(raw[:], mean[:], rstd[:], GT).then_inc(S["f_rstd"], 1)
                if slot.gather is not None:
                    gather(slot.gather)
                recurrence_moments(chunk_of(slot, 1))
                if slot.prep is not None:
                    scatter(slot.prep)
            gather(JOBS - 1)

        @block.scalar
        def _(act):
            def load(dst, src):
                act.dma_start(dst, src).then_inc(S["weights_in"], 16)

            for j in range(3):
                load(wload[:, j * D:(j + 1) * D], a["W_qkv"][j * D:(j + 1) * D, :])
            for j, n in enumerate(["W_gate", "W_out", "A", "B", "C"]):
                load(wload[:, (3 + j) * D:(4 + j) * D], a[n])
            load(small[0:NE, 0:D], a["Wg"])
            load(small[0:32, P:2 * P], a["b1"].rearrange("e (c p) -> (e c) p", p=P))
            with nc.allow_non_contiguous_dma(reason="a few small vectors become columns"):
                load(qkvb[:, 0:3], a["b_qkv"].rearrange("(a p) -> p a", p=P))
                load(qkvb[:, 3:4], a["b_gate"].rearrange("(p a) -> p a", a=1))
                load(byp[:, 0:1], bass.AP(a["identity_bypass"].tensor, 0, [[1, H], [0, HD], [1, 1]]))
                load(srows.rearrange("s (h i) -> s h i", i=HD),
                     bass.AP(a["W_qscale"].tensor, 0, [[HD, NS], [0, H], [1, HD]]))
                load(prow[:].rearrange("a (h s) -> a h s", h=H), bass.AP(a["scale_gain"].tensor, 0, [[0, 1], [1, H], [H, NS]]))
            for j, n in enumerate(["b_out", "gamma", "beta"]):
                act.dma_start(brow[:, j * D:(j + 1) * D], a[n].partition_broadcast(P)).then_inc(S["norm_in"], 16)
            step = Steps(act, S["act_step"])
            act.wait_ge(S["weights_in"], 16 * 15)
            step.done(nc.scalar.activation(byp[:, 1:2], byp[:, 0:1], ACT.Abs))
            step.wait()
            step.done(nc.scalar.activation(byp[:, 2:3], byp[:, 1:2], ACT.Exp, scale=-1.0))
            step.wait()
            nc.scalar.activation(byp[:, 3:4], byp[:, 2:3], ACT.Ln, bias=1.0).then_inc(S["softplus"], 1)
            act.wait_ge(S["setup_done"], 1)

            def head(n):
                act.wait_ge(S["xT_psum"], n + 1)
                nc.scalar.activation(xnT[:], bank[0][:], ACT.Copy).then_inc(S["xT_ready"], 1)
                for j, buf in ((0, K), (1, V)):
                    act.wait_ge(S["kv_psum"], n * 2 + (j + 1))
                    nc.scalar.activation(sl(buf, n * CW + PAD, CW), bank[2 + j][:], ACT.Identity,
                                         bias=qkvb[:, 1 + j:2 + j]).then_inc(S["kv_ready"], 1)

            def queries(n, products):
                act.wait_ge(S["q_psum"], n + 1)
                if products is not None:
                    act.wait_ge(S["products_ready"], products)
                nc.scalar.activation(qT, bank[1][:], ACT.Identity, bias=qkvb[:, 0:1]).then_inc(S["q_ready"], 1)

            by_scale = gains.rearrange("p (c h s) -> p c s h", c=TPC, h=H)

            def weights(n):
                act.wait_ge(S["shifted"], n + 1)
                nc.scalar.activation(gains, gains, ACT.Exp).then_inc(S["exp"], 1)
                act.wait_ge(S["gains_ready"], n + 1)
                nc.scalar.activation(w01[0][:].rearrange("p (c m h) -> p c m h", c=TPC, h=H), by_scale[:, :, 0:8, :],
                                     ACT.Copy, scale=D4[1]).then_inc(S["scaled"], 1)
                nc.scalar.activation(w8[:].rearrange("p (c h) -> p c h", c=TPC), by_scale[:, :, 8, :],
                                     ACT.Copy, scale=D4[1]).then_inc(S["scaled"], 1)
                nc.scalar.activation(w01[1][:].rearrange("p (c m h) -> p c m h", c=TPC, h=H), by_scale[:, :, 0:8, :],
                                     ACT.Copy, scale=D4[3]).then_inc(S["scaled"], 1)
                act.wait_ge(S["rows_psum"], n + 1)
                nc.scalar.activation(wt[0][:], bank[2][:], ACT.Copy).then_inc(S["rows_ready"], 1)
                nc.scalar.activation(wt[1], bank[3][:], ACT.Copy).then_inc(S["rows_ready"], 1)
                nc.scalar.activation(wt[2][0:H, :], bank[0][0:H, :], ACT.Copy).then_inc(S["rows_ready"], 1)

            def chunk(i, kind, nxt):
                n, base = products_of(kind), before(i, kind)
                act.wait_ge(S["gate_psum"], i + 1)
                if later(i):
                    act.wait_ge(S["gated"], i)
                nc.scalar.activation(th, bank[1][:], ACT.Tanh, scale=0.5, bias=halfgb[:]).then_inc(S["gate_ready"], 1)
                if nxt is not None:
                    head(nxt)
                act.wait_ge(S["a0_ready"], i + 1)
                nc.scalar.activation(ah[0][:], af[0][:], ACT.Copy).then_inc(S["a0_high"], 1)
                if nxt is not None:
                    queries(nxt, base + n)
                act.wait_ge(S["a1_ready"], i + 1)
                nc.scalar.activation(ah[1][:], af[1][:], ACT.Copy).then_inc(S["a1_high"], 1)
                if kind >= g2_first:
                    act.wait_ge(S["a2_ready"], i + (1 - g2_first))
                    nc.scalar.activation(ah[2][0:H, :], af[0][0:H, :], ACT.Copy).then_inc(S["a2_high"], 1)
                if nxt is not None:
                    weights(nxt)

            head(0)
            queries(0, None)
            weights(0)
            chunk(0, 0, 1)
            for lo, hi in RANGES:
                with act.Fori(lo, hi) as i:
                    chunk(i, lo, i + 1)
            chunk(CHUNKS - 1, CHUNKS - 1, None)

            def tokens_out(n, q):
                m = n * GC + q
                act.wait_ge(S["f_xT_psum"], m + 1)
                act.wait_ge(S["f_lT_psum"], m)
                nc.scalar.activation(xnT[:], bank[1][:], ACT.Copy).then_inc(S["f_xT"], 1)

            def logits_out(n):
                act.wait_ge(S["f_lT_psum"], (n + 1) * GC)
                act.wait_ge(S["f_lg_psum"], n)
                nc.scalar.activation(lT, bank[4][:], ACT.Copy).then_inc(S["f_lT"], 1)

            def turned(n, s):
                u = s % 2
                act.wait_ge(S["f_transposed"], n * ST + s + 1)
                if n * ST + s >= 2:
                    act.wait_ge(S["f_hidden"], n * ST + s - 1)
                nc.scalar.activation(xTb[u], bank[0][:, 0:P], ACT.Copy).then_inc(S["f_turned"], 1)

            def gelu(n, s, half, words):
                u = s % 2
                e = expert(words, s)
                act.wait_ge(S["f_hidden"], n * ST + s + 1)
                if n * ST + s >= 2:
                    act.wait_ge(S["f_y_psum"], n * ST + s - 1)
                for c in (2 * half, 2 * half + 1):
                    last = nc.scalar.activation(hT[u][:, c * P:(c + 1) * P], bank[2 + u][:, c * P:(c + 1) * P],
                                                ACT.Gelu, bias=b1T[:, ds(e * HC + c, 1)])
                if half:
                    last.then_inc(S["f_gelu"], 1)

            def state(c, k):
                act.wait_ge(S["step_psum"], c * CT + k + 1)
                nc.scalar.activation(hid[c % 2][:, k * NB:(k + 1) * NB], bank[6 + c % 2][:, k * NB:(k + 1) * NB],
                                     ACT.Tanh).then_inc(S["h_ready"], 1)

            for slot in SLOTS:
                for h in range(2):
                    c = chunk_of(slot, h)
                    for k in range(CT):
                        if c is not None:
                            state(c, k)
                        if slot.tiles is not None:
                            if h == 0 and k == LEAD:
                                act.wait_ge(S["f_slots_ready"], 2 * slot.tiles + 2)
                                words = packed_experts(act, slot.tiles)
                                turned(slot.tiles, 0)
                            for s, part in pieces_after(h, k):
                                if part == 1 and s + 1 < ST:
                                    turned(slot.tiles, s + 1)
                                if part >= 3:
                                    gelu(slot.tiles, s, part - 3, words)
                        if slot.prep is not None and h == 0:
                            if k in PREP_STEPS:
                                tokens_out(slot.prep, PREP_STEPS.index(k))
                            if k == CT - 2:
                                logits_out(slot.prep)

        @block.tensor
        def _(pe):
            pe.wait_ge(S["consts_in"], 32)
            pe.wait_ge(S["weights_in"], 16 * 15)
            for j in range(8):
                nc.tensor.transpose(bank[j // 4][:, (j % 4) * P:(j % 4 + 1) * P], wload[:, j * D:(j + 1) * D], ident)
            nc.tensor.transpose(bank[2][:, 0:NE], small[0:NE, 0:D], ident[0:NE, 0:NE])
            nc.tensor.transpose(bank[2][:, 32:64], small[0:32, P:2 * P], ident[0:32, 0:32])
            nc.tensor.transpose(bank[2][:, 64:64 + NS], srows, ident[0:NS, 0:NS])
            pe.wait_ge(S["filled"], 1)
            nc.tensor.matmul(bank[3][:, 0:H * NS], ones[0:1, :], prow[:], start=True, stop=True).then_inc(S["wT_psum"], 1)
            pe.wait_ge(S["setup_done"], 1)

            def tokens(n):
                pe.wait_ge(S["xn_ready"], n + 1)
                for c in range(TPC):
                    last = nc.tensor.transpose(bank[0][:, c * P:(c + 1) * P], xn[0][:, c * D:(c + 1) * D], ident)
                last.then_inc(S["xT_psum"], 1)
                pe.wait_ge(S["xT_ready"], n + 1)
                for j in range(2):
                    nc.tensor.matmul(bank[2 + j][:], projT[:, (1 + j) * D:(2 + j) * D], xnT[:],
                                     start=True, stop=True).then_inc(S["kv_psum"], 1)

            def queries(n):
                nc.tensor.matmul(bank[1][:], projT[:, 0:D], xnT[:], start=True, stop=True).then_inc(S["q_psum"], 1)

            def logits(n):
                pe.wait_ge(S["q_ready"], n + 1)
                pe.wait_ge(S["kv_ready"], n * 2 + 2)
                w = H * NS
                for c in range(TPC):
                    last = nc.tensor.matmul(bank[2 + c // 2][:, (c % 2) * w:(c % 2 + 1) * w], qT[:, c * P:(c + 1) * P],
                                            mqs[:], start=True, stop=True)
                last.then_inc(S["logits"], 1)

            def weight_rows(n):
                pe.wait_ge(S["weights_ready"], n + 1)
                for c in range(TPC):
                    cs = slice(c * P, (c + 1) * P)
                    nc.tensor.transpose(bank[2][:, cs], w01[0][:, cs], ident)
                    nc.tensor.transpose(bank[3][:, cs], w01[1][:, cs], ident)
                    last = nc.tensor.transpose(bank[0][0:H, cs], w8[:, c * H:(c + 1) * H], ident)
                last.then_inc(S["rows_psum"], 1)

            def output(n):
                pe.wait_ge(S["gated"], n + 1)
                for c in range(TPC):
                    last = nc.tensor.matmul(bank[0][:, c * D:(c + 1) * D], att[:, c * P:(c + 1) * P], outT[:],
                                            start=True, stop=True)
                last.then_inc(S["y_psum"], 1)

            sel = [cst[:, C_SEL + 32 * s:C_SEL + 32 * s + 32] for s in range(2)]

            def chunk(i, kind, nxt):
                g0, g1, g2 = active(kind)
                base = before(i, kind)
                if later(i):
                    pe.wait_ge(S["terms_ready"], base)
                pe.wait_ge(S["products_ready"], base + 1)
                nc.tensor.matmul(bank[6][:], blkw[:], prod[0], start=True, stop=True).then_inc(S["products_used"], 1)
                pe.wait_ge(S["rows_ready"], i * 3 + 3)
                nc.tensor.matmul(bank[1][:], projT[:, 3 * D:4 * D], xnT[:], start=True, stop=True).then_inc(S["gate_psum"], 1)
                if later(i):
                    output(i - 1)
                count = [0]

                def reduce(ms, bk):
                    for q in range(4):
                        if 2 * q not in ms:
                            nc.tensor.matmul(bank[bk][32 * q:32 * q + 32, :], sel[0], zero[:], start=True, stop=True)
                    for m in ms:
                        q, s = divmod(m, 2)
                        count[0] += 1
                        pe.wait_ge(S["products_ready"], base + (count[0] + 1))
                        nc.tensor.matmul(bank[bk][32 * q:32 * q + 32, :], sel[s], prod[count[0] % NPROD], start=(s == 0),
                                         stop=(s == 1 or m + 1 not in ms)).then_inc(S["products_used"], 1)

                reduce(g0, 4)
                if nxt is not None:
                    if later(i):
                        pe.wait_ge(S["resid"], i)
                    tokens(nxt)
                    pe.wait_ge(S["gate_ready"], i + 1)
                    queries(nxt)
                reduce(g1, 5)
                if g2:
                    count[0] += 1
                    pe.wait_ge(S["products_ready"], base + (count[0] + 1))
                    pe.wait_ge(S["a0_ready"], i + 1)
                    nc.tensor.matmul(bank[4][0:32, :], sel[0], prod[count[0] % NPROD], start=True,
                                     stop=True).then_inc(S["products_used"], 1)
                j = 0
                for g, ms in enumerate((g0, g1, [0] if g2 else [])):
                    if ms:
                        pe.wait_ge(S[f"a{g}_low"], i + 1 if g < 2 else i + (1 - g2_first))
                    for k, m in enumerate(ms):
                        j += 1
                        if j >= 2:
                            pe.wait_ge(S["terms_ready"], base + (j - 1))
                        lhs = esel[:, m * P:(m + 1) * P]
                        nc.tensor.matmul(bank[6 + j % 2][:], lhs, ah[g][:], start=True, stop=False)
                        nc.tensor.matmul(bank[6 + j % 2][:], lhs, al[g][:], start=False, stop=True).then_inc(
                            S["spread_ready"], 1)
                        if nxt is not None and (g, k) == (0, 0):
                            logits(nxt)
                        if nxt is not None and (g, k) == (1, 2):
                            weight_rows(nxt)

            tokens(0)
            queries(0)
            logits(0)
            weight_rows(0)
            chunk(0, 0, 1)
            for lo, hi in RANGES:
                with pe.Fori(lo, hi) as i:
                    chunk(i, lo, i + 1)
            chunk(CHUNKS - 1, CHUNKS - 1, None)
            output(CHUNKS - 1)

            def columns(v, at):
                for c in range(TPC):
                    last = nc.tensor.transpose(v[:, c * P:(c + 1) * P], XN[:, at + c * D:at + (c + 1) * D], ident)
                return last

            def prep_columns(n, q):
                m = n * GC + q
                pe.wait_ge(S["f_xn"], m + 1)
                pe.wait_ge(S["f_xT"], m)
                columns(bank[1], (n % GROUPS * GC + q) * CW).then_inc(S["f_xT_psum"], 1)

            def prep_logits(n, q):
                pe.wait_ge(S["f_xT"], n * GC + q + 1)
                if q == 0:
                    pe.wait_ge(S["f_slots_ready"], 2 * n)
                nc.tensor.matmul(bank[4][32 * q:32 * q + 32, :], wgT[:], xnT[:], start=True,
                                 stop=True).then_inc(S["f_lT_psum"], 1)

            def logit_rows(n):
                pe.wait_ge(S["f_lT"], n + 1)
                for c in range(TPC):
                    last = nc.tensor.transpose(bank[1][:, c * P:(c + 1) * P], lT[:, c * P:(c + 1) * P], ident)
                last.then_inc(S["f_lg_psum"], 1)

            def counts(n):
                w = GT * NE
                pe.wait_ge(S["f_onehot"], n + 1)
                nc.tensor.matmul(bank[4][:, 0:w], cst[:, C_UP:C_UP + P], oh, start=True, stop=True)
                nc.tensor.matmul(bank[4][:, w:2 * w], ones[:], oh, start=True, stop=True).then_inc(S["f_counts"], 1)

            def turn(n, s):
                pe.wait_ge(xs_in[s % RING], 16 * (n * (ST // RING) + s // RING + 1))
                pe.wait_ge(S["f_turned"], n * ST + s)
                nc.tensor.transpose(bank[0][:, 0:P], xsb[s % RING], ident).then_inc(S["f_transposed"], 1)

            def hidden(n, s, half):
                u = s % 2
                if half == 0:
                    pe.wait_ge(S["f_turned"], n * ST + s + 1)
                    pe.wait_ge(w1_in[s % RING], 16 * (n * (ST // RING) + s // RING + 1))
                    if n * ST + s >= 2:
                        pe.wait_ge(S["f_gelu"], n * ST + s - 1)
                for c in (2 * half, 2 * half + 1):
                    last = nc.tensor.matmul(bank[2 + u][:, c * P:(c + 1) * P], w1b[s % RING][:, c * P:(c + 1) * P],
                                            xTb[u], start=True, stop=True)
                if half:
                    last.then_inc(S["f_hidden"], 1)

            def result(n, s, half, words):
                u = s % 2
                e = expert(words, s)
                if half == 0:
                    pe.wait_ge(S["f_gelu"], n * ST + s + 1)
                    pe.wait_ge(S["f_y_ready"], n * ST + s)
                for c in (2 * half, 2 * half + 1):
                    last = nc.tensor.matmul(bank[5][:, 0:D], hT[u][:, c * P:(c + 1) * P],
                                            w2[:, ds(e * (HC * D) + c * D, D)], start=(c == 0), stop=(c == HC - 1),
                                            skip_group_check=True)
                if half:
                    last.then_inc(S["f_y_psum"], 1)

            def piece(n, s, part, words):
                if part == 0 and s + 1 < ST:
                    turn(n, s + 1)
                if part in (1, 2):
                    hidden(n, s, part - 1)
                if part in (3, 4) and s > 0:
                    result(n, s - 1, part - 3, words)

            def recurrence_columns(c):
                pe.wait_ge(S["r_xn"], c + 1)
                if c > 1:
                    pe.wait_ge(S["r_stats2"], c - 1)
                columns(bank[1], c * CW).then_inc(S["r_xT_psum"], 1)

            def recurrence_inputs(c):
                pe.wait_ge(S["r_xT"], c + 1)
                nc.tensor.matmul(bank[6 + c % 2][:], abcT[:, D:2 * D], xrT, start=True, stop=True,
                                 skip_group_check=True).then_inc(S["r_xb"], 1)

            def recurrence_output(c):
                u = c % 2
                for k in range(TPC):
                    last = nc.tensor.matmul(bank[1][:, k * D:(k + 1) * D], hid[u][:, k * P:(k + 1) * P],
                                            abcT[:, 2 * D:3 * D], start=True, stop=True)
                last.then_inc(S["r_y"], 1)

            def recurrence_step(c, k):
                u = c % 2
                prev = hid[u][:, (k - 1) * NB:k * NB] if k else hid[1 - u][:, CW - NB:CW]
                pe.wait_ge(S["h_ready"], c * CT + k + 1)
                for q in range(4):
                    last = nc.tensor.matmul(bank[6 + u][32 * q:32 * q + 32, k * NB:(k + 1) * NB],
                                            abcT[:, 32 * q:32 * q + 32], prev, start=False, stop=True,
                                            skip_group_check=True)
                last.then_inc(S["step_psum"], 1)

            pe.wait_ge(S["w2_in"], 32)
            for slot in SLOTS:
                if slot.pair == 0:
                    recurrence_columns(0)
                    recurrence_inputs(0)
                for h in range(2):
                    c = chunk_of(slot, h)
                    for k in range(CT):
                        if c is not None:
                            recurrence_step(c, k)
                            if k == 2 and c > 0:
                                if h == 1 and slot.prep is not None:
                                    pe.wait_ge(S["f_lg"], slot.prep + 1)
                                recurrence_output(c - 1)
                            if k == 10 and c + 1 < CHUNKS:
                                recurrence_columns(c + 1)
                            if k == 20 and c + 1 < CHUNKS:
                                recurrence_inputs(c + 1)
                        if slot.tiles is not None:
                            if h == 0 and k == LEAD:
                                pe.wait_ge(S["f_slots_ready"], 2 * slot.tiles + 2)
                                words = packed_experts(pe, slot.tiles)
                                turn(slot.tiles, 0)
                            for s, part in pieces_after(h, k):
                                piece(slot.tiles, s, part, words)
                        if slot.prep is not None and h == 0:
                            if k == PREP_STEPS[0] and c is not None:
                                pe.wait_ge(S["r_xT"], c + 2)
                            if k == PREP_STEPS[0] and slot.prep == JOBS - 1:
                                pe.wait_ge(S["r_stats2"], CHUNKS)
                            if k in PREP_STEPS:
                                prep_columns(slot.prep, PREP_STEPS.index(k))
                            if k - 2 in PREP_STEPS:
                                prep_logits(slot.prep, PREP_STEPS.index(k - 2))
                            if k == CT - 1:
                                logit_rows(slot.prep)
                        if slot.prep is not None and h == 1 and k == 4:
                            counts(slot.prep)
                if slot.tiles is not None:
                    for half in range(2):
                        result(slot.tiles, ST - 1, half, words)
                if slot.pair == CHUNKS // 2 - 1:
                    pe.wait_ge(S["h_ready"], CHUNKS * CT + 1)
                    recurrence_output(CHUNKS - 1)

        @block.vector
        def _(dve):
            V_ = nc.vector
            step = Steps(dve, S["dve_step"])
            V_.memset(zero[:], 0.0)
            V_.memset(ones[:], 1.0).then_inc(S["filled"], 1)
            V_.memset(K[:, 0:PAD], 0.0)
            V_.memset(V[:, 0:PAD], 0.0)
            step.done(V_.memset(wgT[:], 0.0))
            dve.wait_ge(S["consts_in"], 32)
            V_.tensor_copy(esel[:], eload)
            dve.wait_ge(S["filled"], 1)
            for t in (ah[2], al[2]):
                V_.tensor_copy(t[:], zero[:])
            dve.wait_ge(S["weights_in"], 16 * 15)
            V_.tensor_scalar(halfgb[:], qkvb[:, 3:4], 0.5, None, ALU.mult)
            dve.wait_ge(S["softplus"], 1)
            step.done(V_.scalar_tensor_tensor(out=byp[:, 4:5], in0=byp[:, 0:1], scalar=0.0, in1=byp[:, 3:4],
                                              op0=ALU.max, op1=ALU.add))
            step.wait()
            step.done(V_.tensor_scalar(byp[:, 5:6], byp[:, 4:5], D4[0], None, ALU.add))
            step.wait()
            V_.tensor_scalar(blkw[:], cst[:, C_BLK:C_BLK + P], byp[:, 5:6], None, ALU.mult)
            dve.wait_ge(S["wT_psum"], 1)
            V_.tensor_copy(projT[:], bank[0][:])
            V_.tensor_tensor(mqs[:].rearrange("p (h s) -> p h s", h=H),
                             cst[:, C_HM:C_HM + H].unsqueeze(2).broadcast_to([P, H, NS]),
                             bank[2][:, 64:64 + NS].unsqueeze(1).broadcast_to([P, H, NS]), ALU.mult)
            V_.tensor_scalar(outT[:], bank[1][:, 0:D], 0.5, None, ALU.mult)
            V_.tensor_copy(abcT[:], bank[1][:, D:4 * D])
            step.wait()
            V_.tensor_copy(wgT[:, 0:NE], bank[2][:, 0:NE])
            V_.tensor_copy(b1T[:], bank[2][:, 32:64])
            V_.tensor_copy(prior[:], bank[3][:, 0:H * NS]).then_inc(S["setup_done"], 1)
            dve.wait_ge(S["setup_done"], 1)

            def statistics(src, raw_of, ready):
                for c in range(TPC):
                    last = V_.bn_stats(raw_of(c), src(c))
                last.then_inc(ready, 1)

            def stats(n, j):
                if j is not None:
                    dve.wait_ge(x_in[j[0]], j[1])
                statistics(lambda c: sl(X, n * CW + c * D, D), lambda c: raw[:, 6 * c:6 * c + 6], S["stats"])

            def normalise(n):
                dve.wait_ge(S["rstd"], n + 1)
                if later(n):
                    dve.wait_ge(S["xT_psum"], n)
                for c in range(TPC):
                    last = V_.tensor_scalar(xn[0][:, c * D:(c + 1) * D], sl(X, n * CW + c * D, D), mean[:, c:c + 1],
                                            rstd[:, c:c + 1], ALU.subtract, ALU.mult)
                last.then_inc(S["xn_ready"], 1)

            def shift_logits(n):
                dve.wait_ge(S["logits"], n + 1)
                w = H * NS
                g3 = gains.rearrange("p (ch s) -> p ch s", s=NS)
                for k in range(2):
                    last = V_.tensor_tensor(gains[:, k * 2 * w:(k + 1) * 2 * w].rearrange("p (c w) -> p c w", c=2),
                                            bank[2 + k][:, 0:2 * w].rearrange("p (c w) -> p c w", c=2),
                                            prior[:].unsqueeze(1).broadcast_to([P, 2, w]), ALU.add)
                step.done(last)
                step.wait()
                step.done(V_.tensor_reduce(gmax, g3, X_AXIS, ALU.max))
                step.wait()
                V_.tensor_tensor(g3, g3, gmax.unsqueeze(2).broadcast_to([P, TPC * H, NS]),
                                 ALU.subtract).then_inc(S["shifted"], 1)

            def softmax(n):
                g3 = gains.rearrange("p (ch s) -> p ch s", s=NS)
                dve.wait_ge(S["exp"], n + 1)
                step.done(V_.tensor_reduce(gsum, g3, X_AXIS, ALU.add))
                step.wait()
                step.done(V_.reciprocal(gmax, gsum))
                step.wait()
                V_.tensor_tensor(g3, g3, gmax.unsqueeze(2).broadcast_to([P, TPC * H, NS]),
                                 ALU.mult).then_inc(S["gains_ready"], 1)

            def shift_weights(n):
                by_scale = gains.rearrange("p (c h s) -> p c s h", c=TPC, h=H)
                wv = w01[0][:].rearrange("p (c m h) -> p c m h", c=TPC, h=H)
                dve.wait_ge(S["scaled"], n * 3 + 3)
                for c in range(TPC):
                    V_.scalar_tensor_tensor(out=wv[:, c, 1:8, :], in0=by_scale[:, c, 0:7, :], scalar=D4[2],
                                            in1=wv[:, c, 1:8, :], op0=ALU.mult, op1=ALU.add)
                w8v = w8[:].rearrange("p (c h) -> p c h", c=TPC)
                V_.scalar_tensor_tensor(out=w8v, in0=by_scale[:, :, 7, :], scalar=D4[2], in1=w8v,
                                        op0=ALU.mult, op1=ALU.add).then_inc(S["weights_ready"], 1)

            def gate(n, adds):
                dve.wait_ge(S["gate_ready"], n + 1)
                dve.wait_ge(S["terms_added"], adds)
                V_.scalar_tensor_tensor(out=att, in0=th, scalar=1.0, in1=acc, op0=ALU.add,
                                        op1=ALU.mult).then_inc(S["gated"], 1)

            def residual(n):
                dve.wait_ge(S["y_psum"], n + 1)
                dve.wait_ge(S["xb_ready"], n + 1)
                V_.tensor_tensor(sl(X, n * CW, CW), sl(X, n * CW, CW), bank[0][:], ALU.add).then_inc(S["resid"], 1)

            STEPS = 4

            def chunk(i, kind, nxt, loaded):
                g0, g1, g2 = active(kind)
                n, base = products_of(kind), before(i, kind)
                adds = spread_before(i, kind)
                shifts = [0] + [POW[m] for m in g0] + [TRI[m] for m in g1] + ([POW[8]] if g2 else [])
                assert len(shifts) == n

                def product(j):
                    if j >= NPROD:
                        dve.wait_ge(S["products_used"], base + (j - NPROD + 1))
                    elif later(i):
                        dve.wait_ge(S["products_used"], base)
                    V_.tensor_tensor(prod[j % NPROD], qT, sl(K, i * CW + (PAD - NB * shifts[j]), CW),
                                     ALU.mult).then_inc(S["products_ready"], 1)

                def pack(g, bk, used, h=P):
                    dve.wait_ge(S["products_used"], used)
                    V_.tensor_tensor(af[g % 2][0:h, :], bank[bk][0:h, :], wt[g][0:h, :], ALU.mult).then_inc(
                        S[f"a{g}_ready"], 1)

                def low(g, h=P):
                    dve.wait_ge(S[f"a{g}_high"], i + 1 if g < 2 else i + (1 - g2_first))
                    V_.tensor_tensor(al[g][0:h, :], af[g % 2][0:h, :], ah[g][0:h, :].bitcast(F32),
                                     ALU.subtract).then_inc(S[f"a{g}_low"], 1)

                def make_term(j):
                    if j == 0:
                        dve.wait_ge(S["products_used"], base + 1)
                    else:
                        dve.wait_ge(S["spread_ready"], adds + j)
                    if j >= NTERM:
                        dve.wait_ge(S["terms_added"], adds + max(1, j - NTERM))
                    elif later(i):
                        dve.wait_ge(S["terms_added"], adds)
                    V_.tensor_tensor(term[j % NTERM], bank[6 + j % 2][:], sl(V, i * CW + (PAD - NB * shifts[j]), CW),
                                     ALU.mult).then_inc(S["terms_ready"], 1)

                dve.wait_ge(S["q_ready"], i + 1)
                dve.wait_ge(S["kv_ready"], i * 2 + 2)
                product(0)
                if later(i):
                    gate(i - 1, adds)
                if nxt is not None:
                    stats(nxt, loaded)
                for j in range(1, 5):
                    product(j)
                if later(i):
                    residual(i - 1)
                if nxt is not None:
                    normalise(nxt)
                split = min(1 + len(g0) + 2, n)
                for j in range(5, split):
                    product(j)
                dve.wait_ge(S["rows_ready"], i * 3 + 3)
                pack(0, 4, base + (1 + len(g0)))
                for j in range(split, 1 + len(g0) + len(g1)):
                    product(j)
                low(0)
                if g2:
                    product(n - 1)
                pack(1, 5, base + (1 + len(g0) + len(g1)))
                make_term(0)
                if g2:
                    pack(2, 4, base + n, H)
                low(1)
                if g2:
                    low(2, H)
                for j in range(1, n):
                    make_term(j)
                    if nxt is not None:
                        if j == 3:
                            shift_logits(nxt)
                        if j == 5:
                            softmax(nxt)
                        if j == 7:
                            shift_weights(nxt)

            stats(0, (0, 16 * TPC))
            normalise(0)
            shift_logits(0)
            softmax(0)
            shift_weights(0)
            chunk(0, 0, 1, (1, 16 * TPC))
            for lo, hi in RANGES:
                start = step.n
                for x in range(lo + 1, hi + 1):
                    dve.wait_ge(x_in[x % 4], 16 * TPC * (x // 4 + 1))
                with dve.Fori(lo, hi) as i:
                    step.enter(start, i - lo, STEPS)
                    chunk(i, lo, i + 1, None)
                    assert step.n == STEPS
                step.leave(start + (hi - lo) * STEPS)
            chunk(CHUNKS - 1, CHUNKS - 1, None, None)
            gate(CHUNKS - 1, PRODUCTS_BEFORE[CHUNKS] - CHUNKS)
            residual(CHUNKS - 1)
            dve.wait_ge(S["resid"], CHUNKS)

            def normalised(chunk, t, mu, rs, ready):
                for c in range(TPC):
                    at = chunk * CW + c * D
                    last = V_.tensor_scalar(XN[:, at:at + D], X[:, at:at + D], mu[:, t + c:t + c + 1],
                                            rs[:, t + c:t + c + 1], ALU.subtract, ALU.mult)
                last.then_inc(ready, 1)

            def prep_stats(n, q):
                at = (n % GROUPS * GC + q) * CW
                statistics(lambda c: X[:, at + c * D:at + (c + 1) * D],
                           lambda c: raw[:, 6 * (q * TPC + c):6 * (q * TPC + c + 1)], S["f_stats"])

            def prep_normalise(n, q):
                dve.wait_ge(S["f_rstd"], n + 1)
                normalised(n % GROUPS * GC + q, q * TPC, mean, rstd, S["f_xn"])

            def v3(t):
                return t.rearrange("p (g e) -> p g e", e=NE)

            full = [P, GT, NE]

            def choose(n):
                rev = cst[:, C_REV:C_REV + NE].unsqueeze(1).broadcast_to(full)
                dve.wait_ge(S["f_lg_psum"], n + 1)
                V_.tensor_copy(lg.rearrange("p (q c e) -> p q c e", q=4, e=NE),
                               bank[1][:].rearrange("p (c q e) -> p q c e", q=4, e=32)[:, :, :, 0:NE]
                               ).then_inc(S["f_lg"], 1)
                dve.wait_ge(S["f_lg"], n + 1)
                step.done(V_.tensor_reduce(m64, v3(lg), X_AXIS, ALU.max))
                step.wait()
                step.done(V_.tensor_tensor(v3(tmp), v3(lg), m64.unsqueeze(2).broadcast_to(full), ALU.is_equal))
                step.wait()
                step.done(V_.tensor_tensor(v3(tmp), v3(tmp), rev, ALU.mult))
                step.wait()
                step.done(V_.tensor_reduce(m64, v3(tmp), X_AXIS, ALU.max))
                step.wait()
                V_.tensor_tensor(v3(oh), v3(tmp), m64.unsqueeze(2).broadcast_to(full), ALU.is_equal).then_inc(
                    S["f_onehot"], 1)

            def assign(n):
                dve.wait_ge(S["f_onehot"], n + 1)
                dve.wait_ge(S["f_counts"], n + 1)
                below, tot = v3(bank[4][:, 0:GT * NE]), v3(bank[4][:, GT * NE:2 * GT * NE])
                inc3 = incl.rearrange("p (e g) -> p e g", e=NE)
                for e in range(NE):
                    last = V_.tensor_tensor_scan(inc3[:, e, :], ones[:, 0:GT], tot[:, :, e], 0.0, ALU.mult, ALU.add)
                step.done(last)
                step.wait()
                tmp3 = tmp.rearrange("p (e k) -> p e k", e=NE)
                kt = cst[:, C_KT:C_KT + GT].unsqueeze(1).broadcast_to([P, NE, GT])
                step.done(V_.tensor_tensor(tmp3, inc3[:, :, GT - 1:GT].broadcast_to([P, NE, GT]), kt, ALU.is_gt))
                step.wait()
                step.done(V_.tensor_reduce(ntl, tmp3, X_AXIS, ALU.add))
                step.wait()
                step.done(V_.tensor_tensor_scan(ctl, ones[:, 0:NE], ntl, 0.0, ALU.mult, ALU.add))
                step.wait()
                step.done(V_.tensor_tensor(bas, ctl, ntl, ALU.subtract))
                step.done(V_.tensor_tensor(v3(tmp), incl.rearrange("p (e g) -> p g e", e=NE), tot, ALU.subtract))
                step.wait()
                step.done(V_.tensor_tensor(v3(tmp), v3(tmp), below, ALU.add))
                step.wait()
                step.done(V_.scalar_tensor_tensor(out=v3(tmp), in0=bas.unsqueeze(1).broadcast_to(full), scalar=float(P),
                                                  in1=v3(tmp), op0=ALU.mult, op1=ALU.add))
                step.wait()
                step.done(V_.tensor_tensor(tmp, tmp, oh, ALU.mult))
                step.wait()
                step.done(V_.tensor_reduce(slotf, v3(tmp), X_AXIS, ALU.add))
                step.wait()
                V_.tensor_copy(slot_i[:, n * GT:(n + 1) * GT], slotf).then_inc(S["f_slots_ready"], 1)
                t3v, dims = t3[0:1, :].rearrange("p (s e) -> p s e", e=NE - 1), [1, ST, NE - 1]
                step.done(V_.tensor_tensor(t3v, cst[0:1, C_SI:C_SI + ST].unsqueeze(2).broadcast_to(dims),
                                           ctl[0:1, 0:NE - 1].unsqueeze(1).broadcast_to(dims), ALU.is_ge))
                step.wait()
                step.done(V_.tensor_reduce(tef[0:1, :], t3v, X_AXIS, ALU.add))
                step.wait()
                V_.tensor_copy(te_i[:, n * ST:(n + 1) * ST], tef[0:1, :])
                step.done(V_.tensor_tensor(t3[0:1, 0:ST], tef[0:1, :], cst[0:1, C_PW:C_PW + ST], ALU.mult))
                step.wait()
                step.done(V_.tensor_reduce(tef[0:1, 0:ST // PACK], t3[0:1, 0:ST].rearrange("p (w k) -> p w k", k=PACK),
                                           X_AXIS, ALU.add))
                step.wait()
                V_.tensor_copy(te_p[:, n * (ST // PACK):(n + 1) * (ST // PACK)], tef[0:1, 0:ST // PACK]).then_inc(
                    S["f_slots_ready"], 1)

            def result(n, s, words):
                u, t = s % 2, n * ST + s
                e = expert(words, s)
                dve.wait_ge(S["f_y_psum"], t + 1)
                if t >= 2:
                    dve.wait_ge(ys_out[u], 16 * (t // 2))
                V_.tensor_tensor(ysb[u], bank[5][:, 0:D], b2bc[:, ds(e * D, D)],
                                 ALU.add).then_inc(S["f_y_ready"], 1)

            def add_results(n):
                dve.wait_ge(S["f_gathered"], 16 * GT * (n + 1))
                at, w = n % GROUPS * GT * D, GT * D
                V_.tensor_tensor(X[:, at:at + w], X[:, at:at + w], XN[:, at:at + w], ALU.add).then_inc(S["f_added"], 1)
                dve.wait_ge(S["f_added"], n + 1)

            def in_stats(c):
                at = c * CW
                statistics(lambda k: X[:, at + k * D:at + (k + 1) * D], lambda k: raw3[:, 6 * k:6 * k + 6], S["r_stats"])

            def in_normalise(c):
                dve.wait_ge(S["r_rstd"], c + 1)
                normalised(c, 0, mean3, rstd3, S["r_xn"])

            def in_columns(c):
                dve.wait_ge(S["r_xT_psum"], c + 1)
                if c:
                    dve.wait_ge(S["r_xb"], c)
                V_.tensor_copy(xrT, bank[1][:]).then_inc(S["r_xT"], 1)

            def out_stats(c):
                dve.wait_ge(S["r_y"], c + 1)
                dve.wait_ge(S["r_xn"], c + 1)
                if c:
                    dve.wait_ge(S["r_out"], c)
                step.done(V_.tensor_tensor(res, XN[:, c * CW:(c + 1) * CW], bank[1][:], ALU.add))
                step.wait()
                statistics(lambda k: res[:, k * D:(k + 1) * D], lambda k: raw2[:, 6 * k:6 * k + 6], S["r_stats2"])

            def out_residual(c):
                dve.wait_ge(S["r_rstd2"], c + 1)
                for k in range(TPC):
                    last = V_.tensor_scalar(res[:, k * D:(k + 1) * D], res[:, k * D:(k + 1) * D],
                                            mean2[:, k:k + 1], rstd2[:, k:k + 1], ALU.subtract, ALU.mult)
                step.done(last)
                step.wait()
                r3 = res.rearrange("p (c d) -> p c d", d=D)
                step.done(V_.tensor_tensor(r3, r3, bc_out(brow[:, D:2 * D]), ALU.mult))
                step.wait()
                step.done(V_.tensor_tensor(r3, r3, bc_out(brow[:, 2 * D:3 * D]), ALU.add))
                step.wait()
                at = c * CW
                V_.tensor_tensor(X[:, at:at + CW], X[:, at:at + CW], res, ALU.add).then_inc(S["r_out"], 1)

            dve.wait_ge(S["w2_in"], 32)
            V_.memset(hid[1][:, CW - NB:CW], 0.0).then_inc(S["h_ready"], 1)
            for slot in SLOTS:
                if slot.pair == 0:
                    add_results(0)
                    in_stats(0)
                    in_normalise(0)
                    in_columns(0)
                for h in range(2):
                    c, n = chunk_of(slot, h), slot.prep if h == 0 else None
                    tiles = iter(range(11) if h == 0 else range(11, ST)) if slot.tiles is not None else iter(())

                    def results(count):
                        for _ in range(count):
                            s = next(tiles, None)
                            if s is not None:
                                result(slot.tiles, s, words)

                    if slot.tiles is not None and h == 0:
                        dve.wait_ge(S["f_slots_ready"], 2 * slot.tiles + 2)
                        words = packed_experts(dve, slot.tiles)
                    if h == 1 and slot.prep is not None:
                        choose(slot.prep)
                    if c is not None and c > 0:
                        out_stats(c - 1)
                    if c is not None and c + 1 < CHUNKS:
                        in_stats(c + 1)
                    if slot.prep == JOBS - 1 and h == 0:
                        out_stats(CHUNKS - 1)
                        out_residual(CHUNKS - 1)
                        dve.wait_ge(S["r_out"], CHUNKS)
                    results(1)
                    if c is not None and c > 0:
                        out_residual(c - 1)
                        dve.wait_ge(S["r_out"], c)
                    if c is not None and c + 1 < CHUNKS:
                        in_normalise(c + 1)
                    results(1)
                    if h == 1 and slot.prep is not None:
                        assign(slot.prep)
                    for q in range(GC):
                        if n is not None:
                            prep_stats(n, q)
                        if q == 1:
                            results(1)
                    if c is not None and c + 1 < CHUNKS:
                        in_columns(c + 1)
                    for q in range(GC):
                        if n is not None:
                            prep_normalise(n, q)
                        results(1)
                    results(ST)
                    if h == 0 and slot.gather is not None:
                        add_results(slot.gather)
            add_results(JOBS - 1)


_ARGS = {
    "x": "L0_attn_a_x", "W_qkv": "L0_attn_a_W_qkv", "b_qkv": "L0_attn_a_b_qkv", "W_out": "L0_attn_a_W_out",
    "b_out": "L0_attn_a_b_out", "W_gate": "L0_attn_a_W_gate", "b_gate": "L0_attn_a_b_gate",
    "scale_gain": "L0_attn_a_scale_gain", "W_qscale": "L0_attn_a_W_qscale",
    "identity_bypass": "L0_attn_a_identity_bypass", "A": "L0_attn_b_A", "B": "L0_attn_b_B", "C": "L0_attn_b_C",
    "gamma": "L0_attn_b_gamma", "beta": "L0_attn_b_beta", "Wg": "L0_ffn_Wg", "W1": "L0_ffn_W1", "b1": "L0_ffn_b1",
    "W2": "L0_ffn_W2", "b2": "L0_ffn_b2",
}


def kernel(**inputs):
    import concourse.bacc as _bacc
    from concourse.bass_utils import run_bass_kernel_spmd as _run

    nc = _bacc.Bacc("TRN2", target_bir_lowering=False, num_devices=1)
    arrays, args = {}, {}
    for short, name in _ARGS.items():
        arr = np.ascontiguousarray(inputs[name])
        arrays[f"in_{short}"] = arr
        args[short] = nc.dram_tensor(f"in_{short}", arr.shape, mybir.dt.from_np(arr.dtype), kind="ExternalInput").ap()
    arrays["in_consts"] = constants()
    consts = nc.dram_tensor("in_consts", (P, C_ALL), F32, kind="ExternalInput").ap()
    out = nc.dram_tensor("out_x", (NB, NT, D), F32, kind="ExternalOutput").ap()
    build(nc, args, consts, out)
    r = _run(nc, [arrays], core_ids=[0])
    return r.results[0]["out_x"]
```

```python
from collections import namedtuple
from contextlib import ExitStack

import numpy as np

import concourse.bass as bass
from concourse import mybir

F32 = mybir.dt.float32
F32R = mybir.dt.float32r
I32 = mybir.dt.int32
ACT = mybir.ActivationFunctionType
ALU = mybir.AluOpType
X_AXIS = mybir.AxisListType.X
ds = bass.ds

P = 128
NB, NT, D, H, NS, NE, NH = 16, 512, 128, 16, 11, 8, 512
HD = D // H
TILES = NB * NT // P
TT = P // NB
CT = 32
CW = CT * NB
TPC = CW // P
CHUNKS = NT // CT
Job = namedtuple("Job", "first chunks tiles slots")


def job(first, chunks):
    tiles = chunks * CW // P
    return Job(first, chunks, tiles, -(-(tiles + NE - 1) // PACK) * PACK)


PACK = 8
assert NE == 8
JOB = [job(0, 4), job(4, 4), job(8, 4), job(12, 4)] + [job(0, 4), job(4, 4), job(8, 4), job(12, 2), job(14, 2)]
JOBS, PASS1 = len(JOB), 4
CHUNKS_BEFORE = [sum(x.chunks for x in JOB[:n]) for n in range(JOBS + 1)]
TILES_BEFORE = [sum(x.tiles for x in JOB[:n]) for n in range(JOBS + 1)]
SLOTS_BEFORE = [sum(x.slots for x in JOB[:n]) for n in range(JOBS + 1)]
GT, ST = max(x.tiles for x in JOB), max(x.slots for x in JOB)
GC = GT * P // CW
HC = NH // P
RING = 8
EPS = 1e-5
D4 = [0.4829629131445341, 0.8365163037378079, 0.2241438680420134, -0.1294095225512604]

POW = [1 << m for m in range(9)]
TRI = [3 << m for m in range(8)]
PAD = 96 * NB

C_ID, C_UP, C_BLK, C_SEL = 0, 128, 256, 384
C_HM = C_SEL + 64
C_REV = C_HM + H
C_KT = C_REV + NE
C_SI = C_KT + GT
C_PW = C_SI + ST
C_KEPT = C_PW + ST
C_ESEL = C_KEPT
C_ALL = C_ESEL + 8 * P


def constants():
    c = np.zeros((P, C_ALL), np.float32)
    k = np.arange(P)
    c[:, C_ID:C_ID + P] = np.eye(P)
    c[:, C_UP:C_UP + P] = k[:, None] < k[None, :]
    c[:, C_BLK:C_BLK + P] = k[:, None] // HD == k[None, :] // HD
    for s in range(2):
        c[:, C_SEL + 32 * s + 16 * s:C_SEL + 32 * s + 16 * s + H] = k[:, None] // HD == np.arange(H)[None, :]
    for m in range(8):
        c[:, C_ESEL + P * m:C_ESEL + P * m + P] = k[:, None] == H * m + k[None, :] // HD
    c[:, C_HM:C_HM + H] = k[:, None] // HD == np.arange(H)[None, :]
    c[:, C_REV:C_REV + NE] = NE - np.arange(NE)
    c[:, C_KT:C_KT + GT] = P * np.arange(GT)
    c[:, C_SI:C_SI + ST] = np.arange(ST)
    c[:, C_PW:C_PW + ST] = float(NE) ** (np.arange(ST) % PACK)
    return c


class Steps:

    def __init__(self, eng, sem):
        self.eng, self.sem, self.base, self.n = eng, sem, 0, 0

    def enter(self, start, i, per):
        self.base, self.n = i * per + start, 0

    def leave(self, total):
        self.base, self.n = 0, total

    def done(self, ins):
        ins.then_inc(self.sem, 1)
        self.n += 1

    def wait(self):
        self.eng.wait_ge(self.sem, self.base + self.n)


def active(i):
    last = CT * (i + 1) - 1
    g0 = [m for m in range(8) if POW[m] <= last]
    g1 = [m for m in range(8) if TRI[m] <= last]
    return g0, g1, POW[8] <= last


def products_of(i):
    g0, g1, g2 = active(i)
    return 1 + len(g0) + len(g1) + int(g2)


def pool_products(i):
    return min(4, len(active(i)[1]) - 1) + int(active(i)[2])


def places(i):
    last = products_of(i) - 1
    return (1, 3, 5, 6, 7, 9, 13) if last >= 15 else (1, 2, 3, 4, 5, 6, min(13, last))


EARLY = 6

RANGES = [(1, 2), (2, 3), (3, 4), (4, 6), (6, 8), (8, 12), (12, CHUNKS - 1)]
for _lo, _hi in RANGES:
    assert all(active(x) == active(_lo) for x in range(_lo, _hi))
POOL_BEFORE = [sum(pool_products(x) for x in range(i)) for i in range(CHUNKS + 1)]
PRODUCTS_BEFORE = [sum(products_of(x) for x in range(i)) for i in range(CHUNKS + 1)]


def stats_parts(n):
    chunks = JOB[n].chunks
    return [(0, chunks)] if n < PASS1 else [(0, chunks - 1), (chunks - 1, chunks)]


def chunk_of(slot, h):
    return None if slot.pair is None else 2 * slot.pair + h


Slot = namedtuple("Slot", "tiles prep gather pair store")
SLOTS = [
    Slot(None, 0, None, None, None),
    Slot(0, 1, None, None, None),
    Slot(1, 2, None, 0, None),
    Slot(2, 3, 1, 1, None),
    Slot(3, 4, 2, 2, None),
    Slot(4, None, 3, 3, None),
    Slot(None, 5, 4, 4, None),
    Slot(5, None, None, 5, 4),
    Slot(None, 6, 5, 6, None),
    Slot(6, 7, None, 7, 5),
    Slot(7, 8, 6, None, 6),
    Slot(8, None, 7, None, None),
]


def prep_steps(slot):
    chunks = range(JOB[slot.prep].chunks)
    return [20 + 2 * q for q in chunks] if slot.tiles is None else [16 + 3 * q for q in chunks]


def columns_step(slot, h):
    return 20 if h == 1 and slot.tiles is None else 13


LEAD = {x.tiles: 14 if before.pair is not None and before.tiles is None else 6
        for before, x in zip(SLOTS, SLOTS[1:]) if x.tiles is not None}


def pieces_after(n, h, k):
    lead = LEAD[n] if h == 0 else 0
    if k < lead:
        return []
    steps, half = CT - lead, JOB[n].slots // 2
    at = range((k - lead) * 5 * half // steps, (k - lead + 1) * 5 * half // steps)
    return [(h * half + p // 5, p % 5) for p in at]


def build(nc, a, consts, out):
    with ExitStack() as ctx:
        def sb(name, shape, dt=F32):
            return ctx.enter_context(nc.sbuf_tensor(name, shape, dt))

        def sem(name):
            return ctx.enter_context(nc.semaphore(name))

        xs = [nc.dram_tensor(f"sorted_x{f}", (ST * P, D), F32, kind="Internal").ap() for f in range(2)]
        ys = [nc.dram_tensor(f"sorted_y{f}", (ST * P, D), F32, kind="Internal").ap() for f in range(2)]

        X = sb("X", [P, TILES * D])
        XN = sb("XN", [P, TILES * D])
        cst = sb("cst", [P, C_KEPT])
        w2 = sb("w2", [P, NE * HC * D])
        b1T = sb("b1T", [P, NE * HC])
        b2bc = sb("b2bc", [P, NE * D])
        wgT = sb("wgT", [P, 32])
        projT = sb("projT", [P, 4 * D])
        outT = sb("outT", [P, D])
        abcT = sb("abcT", [P, 3 * D])
        qkvb = sb("qkvb", [P, 4])
        halfgb = sb("halfgb", [P, 1])
        brow = sb("brow", [P, 3 * D])
        zero = sb("zero", [P, 512])
        ones = sb("ones", [P, P])
        mqs = sb("mqs", [P, H * NS])
        prow = sb("prow", [1, H * NS])
        byp = sb("byp", [P, 6])
        blkw = sb("blkw", [P, P])
        esel = sb("esel", [P, 8 * P], F32R)
        nums = sb("nums", [P, 4])
        raw = sb("raw", [P, TILES * 6])
        mean = sb("mean", [P, TILES])
        rstd = sb("rstd", [P, TILES])
        raw2 = sb("raw2", [P, TPC * 6])
        mean2 = sb("mean2", [P, TPC])
        rstd2 = sb("rstd2", [P, TPC])
        raw3 = sb("raw3", [P, TPC * 6])
        mean3 = sb("mean3", [P, TPC])
        rstd3 = sb("rstd3", [P, TPC])
        mom = sb("mom", [P, 5 * GT])
        slot_i = sb("slot_i", [P, TILES_BEFORE[JOBS]], I32)
        te_i = sb("te_i", [1, SLOTS_BEFORE[JOBS]], I32)
        te_p = sb("te_p", [1, SLOTS_BEFORE[JOBS] // PACK], I32)
        xn = sb("xn", [P, CW])
        xnT = sb("xnT", [P, CW])
        ah = [sb(f"ah{g}", [P, CW], F32R) for g in range(2)]
        al = [sb(f"al{g}", [P, CW], F32R) for g in range(2)]
        K = sb("K", [P, PAD + NB * NT])
        V = sb("V", [P, PAD + NB * NT])

        at = [0]

        def in_xn(n):
            at[0] += n
            assert at[0] <= TILES * D
            return XN[:, at[0] - n:at[0]]

        qT, th, acc, att = in_xn(CW), in_xn(CW), in_xn(CW), in_xn(CW)
        NPROD, NTERM = 10, 4
        spare = [w2[:, j * CW:(j + 1) * CW] for j in range(8)]
        ring = [in_xn(CW) for _ in range(7)] + spare[0:4] + [b2bc[:, CW:2 * CW]]
        ring += [sb(f"ring{j}", [P, CW])[:] for j in range(2)]
        prod, term = ring[:NPROD], ring[NPROD:]
        pool_prod = spare[4:8] + [in_xn(CW)]
        th_new = b2bc[:, 0:CW]
        gains = in_xn(TPC * H * NS)
        gmax, gsum = in_xn(TPC * H), in_xn(TPC * H)
        wload = V[:, PAD:PAD + 8 * D]
        small = V[:, PAD + 8 * D:PAD + 10 * D]
        srows = V[0:NS, PAD + 18 * D:PAD + 19 * D]
        eload = V[:, PAD + 10 * D:PAD + 18 * D]
        w8 = sb("w8", [P, TPC * H])
        w01 = [sb(f"w{g}", [P, TPC * P]) for g in range(2)]
        wt = [sb("wt0", [P, CW]), in_xn(CW), in_xn(CW)]
        af = [sb(f"af{g}", [P, CW]) for g in range(2)]

        kat = [0]

        def in_k(n):
            if kat[0] < PAD + NB * NT < kat[0] + n:
                kat[0] = PAD + NB * NT
            kat[0] += n
            end = kat[0] % (PAD + NB * NT)
            return (K if kat[0] <= PAD + NB * NT else V)[:, end - n:end]

        w1b = [in_k(NH) for _ in range(RING)]
        xsb = [in_k(P) for _ in range(RING)]
        xTb = [in_k(P) for _ in range(2)]
        hT = [in_k(HC * P) for _ in range(2)]
        ysb = [in_k(P) for _ in range(2)]
        lT = in_k(CW)
        lg = in_k(GT * NE)
        oh = in_k(GT * NE)
        tmp = in_k(GT * NE)
        incl = in_k(GT * NE)
        t3 = in_k(ST * (NE - 1))
        m64, slotf, tef = in_k(GT), in_k(GT), in_k(ST)
        ntl, ctl, bas = in_k(NE), in_k(NE), in_k(NE)
        hid = [in_k(CW) for _ in range(2)]
        res = in_k(CW)
        xrT = in_k(CW)

        bank = [ctx.enter_context(nc.psum_tensor(f"bank{j}", [P, 512], F32)) for j in range(8)]

        names = """consts_in weights_in w2_in norm_in filled wT_psum softplus setup_done
            zeros_written dve_step act_step pool_step
            stats rstd xn_ready xT_psum xT_ready kv_psum kv_ready q_psum q_ready gate_psum gate_taken gate_ready
            logits shifted exp gains_ready scaled weights_ready rows_psum rows_ready
            products_ready pool_products products_used a0_ready a1_ready a2_ready a0_high a1_high
            a0_low a1_low spread_ready terms_ready terms_added gated y_psum resid
            r_stats r_rstd r_xn r_xT_psum r_xT r_xb step_psum h_ready r_y r_stats2 r_rstd2 r_out
            f_stats f_rstd f_xn f_xT_psum f_xT f_lT_psum f_lT f_lg_psum f_lg f_onehot f_counts f_slots_ready f_scattered
            f_transposed f_turned f_hidden f_gelu f_y_psum f_y_ready f_gathered f_added out_stored pool_stored""".split()
        S = {n: sem(n) for n in names}
        x_in = [sem(f"x_in{j}") for j in range(4)]
        xs_in = [sem(f"xs_in{u}") for u in range(RING)]
        w1_in = [sem(f"w1_in{u}") for u in range(RING)]
        ys_out = [sem(f"ys_out{u}") for u in range(2)]

        ident = cst[:, C_ID:C_ID + P]
        g2_first = next(i for i in range(CHUNKS) if active(i)[2])

        def sl(buf, at, width):
            return buf[:, at:at + width] if isinstance(at, int) else buf[:, ds(at, width)]

        def rows(t, at, n):
            return t[at:at + n, :] if isinstance(at, int) else t[ds(at, n), :]

        def x_dram(t, g):
            v = t.rearrange("b (g t) d -> g t b d", t=TT)
            return v[g] if isinstance(g, int) else v[ds(g, 1)].rearrange("a t b d -> (a t) b d")

        def later(i):
            return not isinstance(i, int) or i > 0

        def before(i, kind):
            return PRODUCTS_BEFORE[i] if isinstance(i, int) else (i - kind) * products_of(kind) + PRODUCTS_BEFORE[kind]

        def pool_before(i, kind):
            return POOL_BEFORE[i] if isinstance(i, int) else (i - kind) * pool_products(kind) + POOL_BEFORE[kind]

        def vector_before(i, kind):
            if isinstance(i, int):
                return PRODUCTS_BEFORE[i] - POOL_BEFORE[i]
            return (i - kind) * (products_of(kind) - pool_products(kind)) + (PRODUCTS_BEFORE[kind] - POOL_BEFORE[kind])

        def shifts_of(kind):
            g0, g1, g2 = active(kind)
            return [0] + [POW[m] for m in g0] + [TRI[m] for m in g1] + ([POW[8]] if g2 else [])

        def spread_before(i, kind):
            if isinstance(i, int):
                return PRODUCTS_BEFORE[i] - i
            return (i - kind) * (products_of(kind) - 1) + (PRODUCTS_BEFORE[kind] - kind)

        def packed_experts(eng, n):
            ws = range(SLOTS_BEFORE[n] // PACK, SLOTS_BEFORE[n + 1] // PACK)
            return [eng.value_load(te_p[:, w:w + 1], min_val=0, max_val=NE ** PACK - 1) for w in ws]

        def expert(words, s):
            return (words[s // PACK] >> (3 * (s % PACK))) & (NE - 1)

        spread_bank = [bank[6], bank[7], bank[5]]

        def bc_out(v):
            return v.unsqueeze(1).broadcast_to([P, TPC, D])

        block = ctx.enter_context(nc.Block())

        @block.sync
        def _(sp):
            sp.dma_start(cst[:], consts[:, 0:C_KEPT]).then_inc(S["consts_in"], 16)
            sp.dma_start(eload, consts[:, C_ESEL:C_ALL]).then_inc(S["consts_in"], 16)
            for i in range(4):
                for c in range(TPC):
                    g = i * TPC + c
                    sp.dma_start(X[:, g * D:(g + 1) * D], x_dram(a["x"], g)).then_inc(x_in[i], 16)
            with sp.Fori(1, CHUNKS // 4) as r:
                for j in range(4):
                    sp.wait_ge(x_in[j], r * (16 * TPC))
                    for c in range(TPC):
                        g = r * (4 * TPC) + (j * TPC + c)
                        sp.dma_start(X[:, ds(g * D, D)], x_dram(a["x"], g)).then_inc(x_in[j], 16)
            sp.wait_ge(S["filled"], 1)
            for f in range(2):
                v = xs[f].rearrange("(t p) d -> p t d", p=P)
                for t in range(0, ST, 4):
                    n = min(4, ST - t)
                    sp.dma_start(v[:, t:t + n, :],
                                 zero[:, 0:n * D].rearrange("p (t d) -> p t d", t=n)).then_inc(S["zeros_written"], 16)

            sp.wait_ge(S["resid"], CHUNKS)
            sp.dma_start(w2[:].rearrange("p (e c d) -> p e c d", e=NE, c=HC),
                         a["W2"].rearrange("e (c p) d -> p e c d", p=P)).then_inc(S["w2_in"], 16)
            sp.dma_start(b2bc[:], a["b2"].rearrange("e d -> (e d)").partition_broadcast(P)).then_inc(S["w2_in"], 16)

            def load(n, s, u):
                if not isinstance(s, int) or SLOTS_BEFORE[n] + s >= RING:
                    sp.wait_ge(S["f_hidden"], s + (SLOTS_BEFORE[n] - (RING - 1)))
                e = sp.value_load(sl(te_i, s + SLOTS_BEFORE[n], 1), min_val=0, max_val=NE - 1)
                sp.dma_start(xsb[u], rows(xs[n % 2], s * P, P)).then_inc(xs_in[u], 16)
                sp.dma_start(w1b[u], a["W1"][ds(e, 1), :, :].rearrange("a d h -> (a d) h")).then_inc(w1_in[u], 16)

            def store(n, s, u):
                sp.wait_ge(S["f_y_ready"], s + (SLOTS_BEFORE[n] + 1))
                sp.dma_start(rows(ys[n % 2], s * P, P), ysb[u % 2]).then_inc(ys_out[u % 2], 16)

            def store_output(n):
                sp.wait_ge(S["f_added"], n + 1)
                first = JOB[n].first * TPC
                with sp.Fori(first, first + JOB[n].tiles) as t:
                    sp.dma_start(x_dram(out, t), X[:, ds(t * D, D)]).then_inc(S["out_stored"], 16)

            def tiles(n):
                sp.wait_ge(S["f_slots_ready"], 2 * n + 2)
                sp.wait_ge(S["f_scattered"], 16 * TILES_BEFORE[n + 1])
                for s in range(RING):
                    load(n, s, s)
                if n >= 2:
                    sp.wait_ge(S["f_added"], n - 1)
                with sp.Fori(1, JOB[n].slots // RING) as j:
                    for u in range(RING):
                        load(n, j * RING + u, u)
                        store(n, (j - 1) * RING + u, u)
                for s in range(JOB[n].slots - RING, JOB[n].slots):
                    store(n, s, s)

            for n in range(JOBS):
                tiles(n)
            for n in range(JOBS - 2, JOBS):
                store_output(n)
            own = JOB[JOBS - 2].tiles + JOB[JOBS - 1].tiles
            sp.wait_ge(S["out_stored"], 16 * own)
            sp.wait_ge(S["pool_stored"], 16 * (TILES - own))

        @block.gpsimd
        def _(pool):
            step = Steps(pool, S["pool_step"])
            for k, x in enumerate((-0.5, 0.5, 1.0 / D, EPS)):
                last = nc.gpsimd.memset(nums[:, k:k + 1], x)
            step.done(last)
            step.wait()

            def moments(r, mu, rs, n):
                def op(dst, x, y, o):
                    return nc.gpsimd.tensor_tensor(dst, x, y, o)

                r = r.rearrange("p (t s) -> p t s", s=6)
                m_even, q_even, m_odd, q_odd = (r[:, :, k] for k in (1, 2, 4, 5))
                total, diff, half, sq, var = (mom[:, k * GT:k * GT + n] for k in range(5))
                mhalf, phalf, inv, eps = (nums[:, k:k + 1].broadcast_to([P, n]) for k in range(4))
                op(total, m_even, m_odd, ALU.add)
                op(diff, m_even, m_odd, ALU.subtract)
                step.done(op(sq, q_even, q_odd, ALU.add))
                step.wait()
                op(mu, total, phalf, ALU.mult)
                op(half, diff, phalf, ALU.mult)
                step.done(op(var, sq, inv, ALU.mult))
                step.wait()
                op(diff, half, half, ALU.mult)
                step.done(op(total, var, eps, ALU.add))
                step.wait()
                step.done(op(var, total, diff, ALU.add))
                step.wait()
                return op(rs, var, mhalf, ALU.pow)

            MOMENTS = 4

            def statistics_of(r):
                pool.wait_ge(S["stats"], (r + 1) * GC)
                ts = slice(r * GT, (r + 1) * GT)
                moments(raw[:, r * GT * 6:(r + 1) * GT * 6], mean[:, ts], rstd[:, ts], GT).then_inc(S["rstd"], 1)

            def chunk(i, kind, nxt):
                n, base, adds = products_of(kind), before(i, kind), spread_before(i, kind)
                pool.wait_ge(S["q_ready"], i + 1)
                pool.wait_ge(S["kv_ready"], i * 2 + 2)
                if later(i):
                    pool.wait_ge(S["products_used"], base)
                for j in range(pool_products(kind)):
                    shift = shifts_of(kind)[n - pool_products(kind) + j]
                    nc.gpsimd.tensor_tensor(pool_prod[j], qT, sl(K, i * CW + (PAD - NB * shift), CW),
                                            ALU.mult).then_inc(S["pool_products"], 1)
                if later(i):
                    pool.wait_ge(S["gated"], i)
                for j in range(1, n):
                    pool.wait_ge(S["terms_ready"], base + (j + 1))
                    if j > 1:
                        pool.wait_ge(S["terms_added"], adds + (j - 1))
                    nc.gpsimd.tensor_tensor(acc, acc if j > 1 else term[0], term[j % NTERM],
                                            ALU.add).then_inc(S["terms_added"], 1)

            statistics_of(0)
            chunk(0, 0, 1)
            for lo, hi in RANGES:
                if lo < CHUNKS // GC:
                    statistics_of(lo)
                with pool.Fori(lo, hi) as i:
                    chunk(i, lo, i + 1)
            chunk(CHUNKS - 1, CHUNKS - 1, None)

            def scatter(n):
                pool.wait_ge(S["f_xn"], CHUNKS_BEFORE[n + 1])
                pool.wait_ge(S["f_slots_ready"], 2 * n + 1)
                if n < 2:
                    pool.wait_ge(S["zeros_written"], 16 * 2 * ((ST + 3) // 4))
                else:
                    pool.wait_ge(S["f_hidden"], SLOTS_BEFORE[n - 1])
                for t in range(JOB[n].tiles):
                    g = JOB[n].first * TPC + t
                    at = TILES_BEFORE[n] + t
                    nc.gpsimd.indirect_dma_start(
                        out=xs[n % 2], out_offset=bass.IndirectOffsetOnAxis(ap=slot_i[:, at:at + 1], axis=0),
                        in_=XN[:, g * D:(g + 1) * D], in_offset=None).then_inc(S["f_scattered"], 16)

            def gather(n):
                pool.wait_ge(S["f_scattered"], 16 * TILES_BEFORE[n + 1])
                for u in range(2):
                    pool.wait_ge(ys_out[u], 16 * SLOTS_BEFORE[n + 1] // 2)
                for t in range(JOB[n].tiles):
                    g = JOB[n].first * TPC + t
                    at = TILES_BEFORE[n] + t
                    nc.gpsimd.indirect_dma_start(
                        out=XN[:, g * D:(g + 1) * D], out_offset=None, in_=ys[n % 2],
                        in_offset=bass.IndirectOffsetOnAxis(ap=slot_i[:, at:at + 1], axis=0),
                    ).then_inc(S["f_gathered"], 16)

            def moments_in(c):
                pool.wait_ge(S["r_stats"], c + 1)
                moments(raw3[:], mean3[:], rstd3[:], TPC).then_inc(S["r_rstd"], 1)

            def moments_out(c):
                pool.wait_ge(S["r_stats2"], c + 1)
                moments(raw2[:], mean2[:], rstd2[:], TPC).then_inc(S["r_rstd2"], 1)

            def recurrence_moments(c):
                if c is not None:
                    if c + 1 < CHUNKS:
                        moments_in(c + 1)
                    if c > 0:
                        moments_out(c - 1)

            def store_output(n):
                pool.wait_ge(S["f_added"], n + 1)
                first = JOB[n].first * TPC
                with pool.Fori(first, first + JOB[n].tiles) as t:
                    pool.dma_start(x_dram(out, t), X[:, ds(t * D, D)]).then_inc(S["pool_stored"], 16)

            for slot in SLOTS:
                if slot.pair == 0:
                    gather(0)
                    moments_in(0)
                recurrence_moments(chunk_of(slot, 0))
                if slot.prep == JOBS - 1:
                    moments_out(CHUNKS - 1)
                if slot.prep is not None:
                    for first, end in stats_parts(slot.prep):
                        pool.wait_ge(S["f_stats"], CHUNKS_BEFORE[slot.prep] + end)
                        ts = slice(first * TPC, end * TPC)
                        moments(raw[:, 6 * first * TPC:6 * end * TPC], mean[:, ts], rstd[:, ts],
                                (end - first) * TPC).then_inc(S["f_rstd"], end - first)
                if slot.gather is not None:
                    gather(slot.gather)
                if slot.store is not None and slot.pair is not None:
                    store_output(slot.store)
                recurrence_moments(chunk_of(slot, 1))
                if slot.prep is not None:
                    scatter(slot.prep)
                if slot.store is not None and slot.pair is None:
                    store_output(slot.store)
            gather(JOBS - 1)

        @block.scalar
        def _(act):
            def load(dst, src):
                act.dma_start(dst, src).then_inc(S["weights_in"], 16)

            for j in range(3):
                load(wload[:, j * D:(j + 1) * D], a["W_qkv"][j * D:(j + 1) * D, :])
            for j, n in enumerate(["W_gate", "W_out", "A", "B", "C"]):
                load(wload[:, (3 + j) * D:(4 + j) * D], a[n])
            load(small[0:NE, 0:D], a["Wg"])
            load(small[0:32, P:2 * P], a["b1"].rearrange("e (c p) -> (e c) p", p=P))
            with nc.allow_non_contiguous_dma(reason="a few small vectors become columns"):
                load(qkvb[:, 0:3], a["b_qkv"].rearrange("(a p) -> p a", p=P))
                load(qkvb[:, 3:4], a["b_gate"].rearrange("(p a) -> p a", a=1))
                load(byp[:, 0:1], bass.AP(a["identity_bypass"].tensor, 0, [[1, H], [0, HD], [1, 1]]))
                load(srows.rearrange("s (h i) -> s h i", i=HD),
                     bass.AP(a["W_qscale"].tensor, 0, [[HD, NS], [0, H], [1, HD]]))
                load(prow[:].rearrange("a (h s) -> a h s", h=H), bass.AP(a["scale_gain"].tensor, 0, [[0, 1], [1, H], [H, NS]]))
            for j, n in enumerate(["b_out", "gamma", "beta"]):
                act.dma_start(brow[:, j * D:(j + 1) * D], a[n].partition_broadcast(P)).then_inc(S["norm_in"], 16)
            step = Steps(act, S["act_step"])
            act.wait_ge(S["weights_in"], 16 * 15)
            step.done(nc.scalar.activation(byp[:, 1:2], byp[:, 0:1], ACT.Abs))
            step.wait()
            step.done(nc.scalar.activation(byp[:, 2:3], byp[:, 1:2], ACT.Exp, scale=-1.0))
            step.wait()
            nc.scalar.activation(byp[:, 3:4], byp[:, 2:3], ACT.Ln, bias=1.0).then_inc(S["softplus"], 1)
            act.wait_ge(S["setup_done"], 1)

            def tokens(n):
                act.wait_ge(S["xT_psum"], n + 1)
                nc.scalar.activation(xnT[:], bank[0][:], ACT.Copy).then_inc(S["xT_ready"], 1)

            def keys_values(n):
                for j, buf in ((0, K), (1, V)):
                    act.wait_ge(S["kv_psum"], n * 2 + (j + 1))
                    nc.scalar.activation(sl(buf, n * CW + PAD, CW), bank[2 + j][:], ACT.Identity,
                                         bias=qkvb[:, 1 + j:2 + j]).then_inc(S["kv_ready"], 1)

            def queries(n, products):
                act.wait_ge(S["q_psum"], n + 1)
                if products is not None:
                    act.wait_ge(S["products_ready"], products[0])
                    act.wait_ge(S["pool_products"], products[1])
                nc.scalar.activation(qT, bank[1][:], ACT.Identity, bias=qkvb[:, 0:1]).then_inc(S["q_ready"], 1)

            by_scale = gains.rearrange("p (c h s) -> p c s h", c=TPC, h=H)

            def weights(n):
                act.wait_ge(S["shifted"], n + 1)
                nc.scalar.activation(gains, gains, ACT.Exp).then_inc(S["exp"], 1)
                act.wait_ge(S["gains_ready"], n + 1)
                nc.scalar.activation(w01[0][:].rearrange("p (c m h) -> p c m h", c=TPC, h=H), by_scale[:, :, 0:8, :],
                                     ACT.Copy, scale=D4[1]).then_inc(S["scaled"], 1)
                nc.scalar.activation(w8[:].rearrange("p (c h) -> p c h", c=TPC), by_scale[:, :, 8, :],
                                     ACT.Copy, scale=D4[1]).then_inc(S["scaled"], 1)
                nc.scalar.activation(w01[1][:].rearrange("p (c m h) -> p c m h", c=TPC, h=H), by_scale[:, :, 0:8, :],
                                     ACT.Copy, scale=D4[3]).then_inc(S["scaled"], 1)
                act.wait_ge(S["rows_psum"], n + 1)
                nc.scalar.activation(wt[0][:], bank[2][:], ACT.Copy).then_inc(S["rows_ready"], 1)
                nc.scalar.activation(wt[1], bank[3][:], ACT.Copy).then_inc(S["rows_ready"], 1)
                nc.scalar.activation(wt[2][0:H, :], bank[0][0:H, :], ACT.Copy).then_inc(S["rows_ready"], 1)

            def chunk(i, kind, nxt):
                own = pool_products(kind)
                made = (vector_before(i, kind) + (products_of(kind) - own), pool_before(i, kind) + own)
                act.wait_ge(S["gate_psum"], i + 1)
                if later(i):
                    act.wait_ge(S["gate_ready"], i)
                nc.scalar.activation(th_new, bank[1][:], ACT.Tanh, scale=0.5, bias=halfgb[:]).then_inc(S["gate_taken"], 1)
                act.wait_ge(S["a0_ready"], i + 1)
                nc.scalar.activation(ah[0][:], af[0][:], ACT.Copy).then_inc(S["a0_high"], 1)
                if nxt is not None:
                    tokens(nxt)
                act.wait_ge(S["a1_ready"], i + 1)
                nc.scalar.activation(ah[1][:], af[1][:], ACT.Copy).then_inc(S["a1_high"], 1)
                if nxt is not None:
                    keys_values(nxt)
                    queries(nxt, made)
                if later(i):
                    act.wait_ge(S["gated"], i)
                act.wait_ge(S["gate_taken"], i + 1)
                nc.scalar.activation(th, th_new, ACT.Copy).then_inc(S["gate_ready"], 1)
                if nxt is not None:
                    weights(nxt)

            tokens(0)
            keys_values(0)
            queries(0, None)
            weights(0)
            chunk(0, 0, 1)
            for lo, hi in RANGES:
                with act.Fori(lo, hi) as i:
                    chunk(i, lo, i + 1)
            chunk(CHUNKS - 1, CHUNKS - 1, None)

            def tokens_out(n, q):
                m = CHUNKS_BEFORE[n] + q
                act.wait_ge(S["f_xT_psum"], m + 1)
                act.wait_ge(S["f_lT_psum"], m)
                nc.scalar.activation(xnT[:], bank[1][:], ACT.Copy).then_inc(S["f_xT"], 1)

            def logits_out(n):
                act.wait_ge(S["f_lT_psum"], CHUNKS_BEFORE[n + 1])
                act.wait_ge(S["f_lg_psum"], n)
                h = 32 * JOB[n].chunks
                nc.scalar.activation(lT[0:h, :], bank[4][0:h, :], ACT.Copy).then_inc(S["f_lT"], 1)

            def turned(n, s):
                u = s % 2
                act.wait_ge(S["f_transposed"], SLOTS_BEFORE[n] + s + 1)
                if SLOTS_BEFORE[n] + s >= 2:
                    act.wait_ge(S["f_hidden"], SLOTS_BEFORE[n] + s - 1)
                nc.scalar.activation(xTb[u], bank[0][:, 0:P], ACT.Copy).then_inc(S["f_turned"], 1)

            def gelu(n, s, half, words):
                u = s % 2
                e = expert(words, s)
                act.wait_ge(S["f_hidden"], SLOTS_BEFORE[n] + s + 1)
                if SLOTS_BEFORE[n] + s >= 2:
                    act.wait_ge(S["f_y_psum"], SLOTS_BEFORE[n] + s - 1)
                for c in (2 * half, 2 * half + 1):
                    last = nc.scalar.activation(hT[u][:, c * P:(c + 1) * P], bank[2 + u][:, c * P:(c + 1) * P],
                                                ACT.Gelu, bias=b1T[:, ds(e * HC + c, 1)])
                if half:
                    last.then_inc(S["f_gelu"], 1)

            def state(c, k):
                act.wait_ge(S["step_psum"], c * CT + k + 1)
                nc.scalar.activation(hid[c % 2][:, k * NB:(k + 1) * NB], bank[6 + c % 2][:, k * NB:(k + 1) * NB],
                                     ACT.Tanh).then_inc(S["h_ready"], 1)

            for slot in SLOTS:
                for h in range(2):
                    c = chunk_of(slot, h)
                    for k in range(CT):
                        if c is not None:
                            state(c, k)
                        if slot.tiles is not None:
                            if h == 0 and k == LEAD[slot.tiles]:
                                act.wait_ge(S["f_slots_ready"], 2 * slot.tiles + 2)
                                words = packed_experts(act, slot.tiles)
                                turned(slot.tiles, 0)
                            for s, part in pieces_after(slot.tiles, h, k):
                                if part == 1 and s + 1 < JOB[slot.tiles].slots:
                                    turned(slot.tiles, s + 1)
                                if part >= 3:
                                    gelu(slot.tiles, s, part - 3, words)
                        if slot.prep is not None and h == 0:
                            if k in prep_steps(slot):
                                tokens_out(slot.prep, prep_steps(slot).index(k))
                            if k == CT - 4:
                                logits_out(slot.prep)

        @block.tensor
        def _(pe):
            pe.wait_ge(S["consts_in"], 32)
            pe.wait_ge(S["weights_in"], 16 * 15)
            for j in range(8):
                nc.tensor.transpose(bank[j // 4][:, (j % 4) * P:(j % 4 + 1) * P], wload[:, j * D:(j + 1) * D], ident)
            nc.tensor.transpose(bank[2][:, 0:NE], small[0:NE, 0:D], ident[0:NE, 0:NE])
            nc.tensor.transpose(bank[2][:, 32:64], small[0:32, P:2 * P], ident[0:32, 0:32])
            nc.tensor.transpose(bank[2][:, 64:64 + NS], srows, ident[0:NS, 0:NS]).then_inc(S["wT_psum"], 1)
            pe.wait_ge(S["filled"], 1)
            pe.wait_ge(S["setup_done"], 1)
            pe.wait_ge(S["norm_in"], 16 * 3)

            def tokens(n):
                pe.wait_ge(S["xn_ready"], n + 1)
                for c in range(TPC):
                    last = nc.tensor.transpose(bank[0][:, c * P:(c + 1) * P], xn[:, c * D:(c + 1) * D], ident)
                last.then_inc(S["xT_psum"], 1)

            def keys_values(n, j):
                if j == 0:
                    pe.wait_ge(S["xT_ready"], n + 1)
                nc.tensor.matmul(bank[2 + j][:], projT[:, (1 + j) * D:(2 + j) * D], xnT[:],
                                 start=True, stop=True).then_inc(S["kv_psum"], 1)

            def queries(n):
                nc.tensor.matmul(bank[1][:], projT[:, 0:D], xnT[:], start=True, stop=True).then_inc(S["q_psum"], 1)

            def logits(n, tiles):
                pe.wait_ge(S["q_ready"], n + 1)
                pe.wait_ge(S["kv_ready"], n * 2 + 2)
                w = H * NS
                for c in tiles:
                    dst = bank[2 + c // 2][:, (c % 2) * w:(c % 2 + 1) * w]
                    nc.tensor.matmul(dst, qT[:, c * P:(c + 1) * P], mqs[:], start=True, stop=False)
                    last = nc.tensor.matmul(dst, ones[0:1, :], prow[:], start=False, stop=True)
                if TPC - 1 in tiles:
                    last.then_inc(S["logits"], 1)

            def weight_rows(n, first, end):
                pe.wait_ge(S["weights_ready"], n + 1)
                for c in range(first, end):
                    cs = slice(c * P, (c + 1) * P)
                    nc.tensor.transpose(bank[2][:, cs], w01[0][:, cs], ident)
                    nc.tensor.transpose(bank[3][:, cs], w01[1][:, cs], ident)
                    last = nc.tensor.transpose(bank[0][0:H, cs], w8[:, c * H:(c + 1) * H], ident)
                if end == TPC:
                    last.then_inc(S["rows_psum"], 1)

            def output(n):
                pe.wait_ge(S["gated"], n + 1)
                for c in range(TPC):
                    cs = slice(c * D, (c + 1) * D)
                    nc.tensor.matmul(bank[0][:, cs], att[:, c * P:(c + 1) * P], outT[:], start=True, stop=False)
                    last = nc.tensor.matmul(bank[0][:, cs], ones[0:1, :], brow[0:1, 0:D], start=False, stop=True)
                last.then_inc(S["y_psum"], 1)

            sel = [cst[:, C_SEL + 32 * s:C_SEL + 32 * s + 32] for s in range(2)]

            def chunk(i, kind, nxt):
                g0, g1, g2 = active(kind)
                base = before(i, kind)
                if later(i):
                    pe.wait_ge(S["terms_ready"], base)
                pe.wait_ge(S["products_ready"], vector_before(i, kind) + 1)
                nc.tensor.matmul(bank[6][:], blkw[:], prod[0], start=True, stop=True).then_inc(S["products_used"], 1)
                nc.tensor.matmul(bank[1][:], projT[:, 3 * D:4 * D], xnT[:], start=True, stop=True).then_inc(S["gate_psum"], 1)
                count = [0]
                mine = products_of(kind) - pool_products(kind)

                def next_product():
                    count[0] += 1
                    j = count[0]
                    if j < mine:
                        pe.wait_ge(S["products_ready"], vector_before(i, kind) + (j + 1))
                        return prod[j % NPROD]
                    pe.wait_ge(S["pool_products"], pool_before(i, kind) + (j - mine + 1))
                    return pool_prod[j - mine]

                def reduce(ms, bk, between=()):
                    for q in range(4):
                        if 2 * q not in ms:
                            nc.tensor.matmul(bank[bk][32 * q:32 * q + 32, :], sel[0], zero[:], start=True, stop=True)
                    for m in ms:
                        q, s = divmod(m, 2)
                        nc.tensor.matmul(bank[bk][32 * q:32 * q + 32, :], sel[s], next_product(), start=(s == 0),
                                         stop=(s == 1 or m + 1 not in ms)).then_inc(S["products_used"], 1)
                        if m < len(between):
                            between[m]()

                def next_queries():
                    pe.wait_ge(S["gate_taken"], i + 1)
                    queries(nxt)

                def next_tokens():
                    pe.wait_ge(S["rows_ready"], i * 3 + 3)
                    tokens(nxt)

                reduce(g0, 4)
                reduce(g1, 5, () if nxt is None else (lambda: None, lambda: None, next_tokens))
                if g2:
                    product = next_product()
                    pe.wait_ge(S["a0_ready"], i + 1)
                    nc.tensor.matmul(bank[4][0:32, :], sel[0], product, start=True,
                                     stop=True).then_inc(S["products_used"], 1)
                j = 0
                for g, ms in enumerate((g0, g1, [0] if g2 else [])):
                    if ms and g < 2:
                        pe.wait_ge(S[f"a{g}_low"], i + 1)
                    for k, m in enumerate(ms):
                        j += 1
                        if j == 2:
                            pe.wait_ge(S["a1_ready"], i + 1)
                        if j >= 3:
                            pe.wait_ge(S["terms_ready"], base + (j - 2))
                        lhs = esel[:, m * P:(m + 1) * P]
                        if g == 2:
                            pe.wait_ge(S["a2_ready"], i + (1 - g2_first))
                            nc.tensor.matmul(spread_bank[j % 3][:], lhs[0:H, :].bitcast(F32), af[0][0:H, :], start=True,
                                             stop=True).then_inc(S["spread_ready"], 1)
                        else:
                            nc.tensor.matmul(spread_bank[j % 3][:], lhs, ah[g][:], start=True, stop=False)
                            nc.tensor.matmul(spread_bank[j % 3][:], lhs, al[g][:], start=False, stop=True).then_inc(
                                S["spread_ready"], 1)
                        at_k, at_v, at_q, at_out, at_l0, at_l1, at_rows = places(kind)
                        if nxt is not None and j in (at_k, at_v):
                            keys_values(nxt, int(j == at_v))
                        if nxt is not None and j == at_q:
                            next_queries()
                        if later(i) and j == at_out:
                            output(i - 1)
                        if nxt is not None and j in (at_l0, at_l1):
                            logits(nxt, range(0, 2) if j == at_l0 else range(2, 4))
                        at, end = j - at_rows, products_of(kind) - 1
                        if nxt is not None and 0 <= at < TPC:
                            if later(i) and at == 0:
                                pe.wait_ge(S["resid"], i)
                            weight_rows(nxt, at, TPC if j == end else at + 1)

            tokens(0)
            keys_values(0, 0)
            keys_values(0, 1)
            queries(0)
            logits(0, range(TPC))
            weight_rows(0, 0, TPC)
            chunk(0, 0, 1)
            for lo, hi in RANGES:
                with pe.Fori(lo, hi) as i:
                    chunk(i, lo, i + 1)
            chunk(CHUNKS - 1, CHUNKS - 1, None)
            output(CHUNKS - 1)

            def columns(v, at):
                for c in range(TPC):
                    last = nc.tensor.transpose(v[:, c * P:(c + 1) * P], XN[:, at + c * D:at + (c + 1) * D], ident)
                return last

            def prep_columns(n, q):
                m = CHUNKS_BEFORE[n] + q
                pe.wait_ge(S["f_xn"], m + 1)
                pe.wait_ge(S["f_xT"], m)
                columns(bank[1], (JOB[n].first + q) * CW).then_inc(S["f_xT_psum"], 1)

            def prep_logits(n, q):
                pe.wait_ge(S["f_xT"], CHUNKS_BEFORE[n] + q + 1)
                if q == 0:
                    pe.wait_ge(S["f_slots_ready"], 2 * n)
                nc.tensor.matmul(bank[4][32 * q:32 * q + 32, :], wgT[:], xnT[:], start=True,
                                 stop=True).then_inc(S["f_lT_psum"], 1)

            def logit_rows(n):
                pe.wait_ge(S["f_lT"], n + 1)
                h = 32 * JOB[n].chunks
                for c in range(TPC):
                    last = nc.tensor.transpose(bank[1][:, c * P:c * P + h], lT[0:h, c * P:(c + 1) * P], ident[0:h, 0:h])
                last.then_inc(S["f_lg_psum"], 1)

            def counts(n):
                w = JOB[n].tiles * NE
                pe.wait_ge(S["f_onehot"], n + 1)
                nc.tensor.matmul(bank[4][:, 0:w], cst[:, C_UP:C_UP + P], oh[:, 0:w], start=True, stop=True)
                nc.tensor.matmul(bank[4][:, w:2 * w], ones[:], oh[:, 0:w], start=True, stop=True).then_inc(S["f_counts"], 1)

            def turn(n, s):
                pe.wait_ge(xs_in[s % RING], 16 * (SLOTS_BEFORE[n] // RING + s // RING + 1))
                pe.wait_ge(S["f_turned"], SLOTS_BEFORE[n] + s)
                nc.tensor.transpose(bank[0][:, 0:P], xsb[s % RING], ident).then_inc(S["f_transposed"], 1)

            def hidden(n, s, half):
                u = s % 2
                if half == 0:
                    pe.wait_ge(S["f_turned"], SLOTS_BEFORE[n] + s + 1)
                    pe.wait_ge(w1_in[s % RING], 16 * (SLOTS_BEFORE[n] // RING + s // RING + 1))
                    if SLOTS_BEFORE[n] + s >= 2:
                        pe.wait_ge(S["f_gelu"], SLOTS_BEFORE[n] + s - 1)
                for c in (2 * half, 2 * half + 1):
                    last = nc.tensor.matmul(bank[2 + u][:, c * P:(c + 1) * P], w1b[s % RING][:, c * P:(c + 1) * P],
                                            xTb[u], start=True, stop=True)
                if half:
                    last.then_inc(S["f_hidden"], 1)

            def result(n, s, half, words):
                u = s % 2
                e = expert(words, s)
                if half == 0:
                    pe.wait_ge(S["f_gelu"], SLOTS_BEFORE[n] + s + 1)
                    pe.wait_ge(S["f_y_ready"], SLOTS_BEFORE[n] + s)
                for c in (2 * half, 2 * half + 1):
                    last = nc.tensor.matmul(bank[5][:, 0:D], hT[u][:, c * P:(c + 1) * P],
                                            w2[:, ds(e * (HC * D) + c * D, D)], start=(c == 0), stop=(c == HC - 1),
                                            skip_group_check=True)
                if half:
                    last.then_inc(S["f_y_psum"], 1)

            def piece(n, s, part, words):
                if part == 0 and s + 1 < JOB[n].slots:
                    turn(n, s + 1)
                if part in (1, 2):
                    hidden(n, s, part - 1)
                if part in (3, 4) and s > 0:
                    result(n, s - 1, part - 3, words)

            def recurrence_columns(c):
                pe.wait_ge(S["r_xn"], c + 1)
                if c > 1:
                    pe.wait_ge(S["r_stats2"], c - 1)
                columns(bank[1], c * CW).then_inc(S["r_xT_psum"], 1)

            def recurrence_inputs(c, quarters):
                pe.wait_ge(S["r_xT"], c + 1)
                for q in quarters:
                    cs = slice(q * P, (q + 1) * P)
                    last = nc.tensor.matmul(bank[6 + c % 2][:, cs], abcT[:, D:2 * D], xrT[:, cs], start=(q == 0),
                                            stop=True, skip_group_check=True)
                if 3 in quarters:
                    last.then_inc(S["r_xb"], 1)

            def recurrence_output(c):
                u = c % 2
                for k in range(TPC):
                    last = nc.tensor.matmul(bank[1][:, k * D:(k + 1) * D], hid[u][:, k * P:(k + 1) * P],
                                            abcT[:, 2 * D:3 * D], start=True, stop=True)
                last.then_inc(S["r_y"], 1)

            def recurrence_step(c, k):
                u = c % 2
                prev = hid[u][:, (k - 1) * NB:k * NB] if k else hid[1 - u][:, CW - NB:CW]
                pe.wait_ge(S["h_ready"], c * CT + k + 1)
                for q in range(4):
                    last = nc.tensor.matmul(bank[6 + u][32 * q:32 * q + 32, k * NB:(k + 1) * NB],
                                            abcT[:, 32 * q:32 * q + 32], prev, start=False, stop=True,
                                            skip_group_check=True)
                last.then_inc(S["step_psum"], 1)

            def finish(n, s, words):
                for half in range(2):
                    result(n, s, half, words)

            last_tile = None
            for at, slot in enumerate(SLOTS):
                if slot.pair == 0:
                    recurrence_columns(0)
                    recurrence_inputs(0, range(4))
                for h in range(2):
                    c = chunk_of(slot, h)
                    for k in range(CT):
                        if c is not None:
                            recurrence_step(c, k)
                            if k == 1 and last_tile is not None:
                                finish(*last_tile)
                                last_tile = None
                            if k == (6 if h == 1 and slot.prep is not None else 2) and c > 0:
                                if h == 1 and slot.prep is not None:
                                    pe.wait_ge(S["f_lg"], slot.prep + 1)
                                recurrence_output(c - 1)
                            if k == columns_step(slot, h) and c + 1 < CHUNKS:
                                recurrence_columns(c + 1)
                            q = k - columns_step(slot, h) - 5
                            if 0 <= q < 4 and c + 1 < CHUNKS:
                                recurrence_inputs(c + 1, [q])
                        if slot.tiles is not None:
                            if h == 0 and k == LEAD[slot.tiles]:
                                pe.wait_ge(S["w2_in"], 32)
                                pe.wait_ge(S["f_slots_ready"], 2 * slot.tiles + 2)
                                words = packed_experts(pe, slot.tiles)
                                turn(slot.tiles, 0)
                            for s, part in pieces_after(slot.tiles, h, k):
                                piece(slot.tiles, s, part, words)
                        if slot.prep is not None and h == 0:
                            if k == prep_steps(slot)[0] and c is not None:
                                pe.wait_ge(S["r_xT"], c + 2)
                            if k == prep_steps(slot)[0] and slot.prep == JOBS - 1:
                                pe.wait_ge(S["r_stats2"], CHUNKS)
                            if k in prep_steps(slot):
                                prep_columns(slot.prep, prep_steps(slot).index(k))
                            if k - 2 in prep_steps(slot):
                                prep_logits(slot.prep, prep_steps(slot).index(k - 2))
                            if k == CT - 2:
                                logit_rows(slot.prep)
                        if slot.prep is not None and h == 1 and k == 7:
                            counts(slot.prep)
                if slot.tiles is not None:
                    last_tile = (slot.tiles, JOB[slot.tiles].slots - 1, words)
                    if SLOTS[at + 1].pair in (None, 0) if at + 1 < len(SLOTS) else True:
                        finish(*last_tile)
                        last_tile = None
                if slot.pair == CHUNKS // 2 - 1:
                    pe.wait_ge(S["h_ready"], CHUNKS * CT + 1)
                    recurrence_output(CHUNKS - 1)

        @block.vector
        def _(dve):
            V_ = nc.vector
            step = Steps(dve, S["dve_step"])

            def statistics(src, raw_of, ready):
                for c in range(TPC):
                    last = V_.bn_stats(raw_of(c), src(c))
                last.then_inc(ready, 1)

            def stats(r):
                for n in range(r * GC, (r + 1) * GC):
                    dve.wait_ge(x_in[n % 4], 16 * TPC * (n // 4 + 1))
                    statistics(lambda c: X[:, n * CW + c * D:n * CW + (c + 1) * D],
                               lambda c: raw[:, 6 * (n * TPC + c):6 * (n * TPC + c + 1)], S["stats"])

            def prep_stats(n, q):
                at = (JOB[n].first + q) * CW
                statistics(lambda c: X[:, at + c * D:at + (c + 1) * D],
                           lambda c: raw[:, 6 * (q * TPC + c):6 * (q * TPC + c + 1)], S["f_stats"])

            V_.memset(zero[:], 0.0)
            V_.memset(ones[:], 1.0).then_inc(S["filled"], 1)
            V_.memset(K[:, 0:PAD], 0.0)
            V_.memset(V[:, 0:PAD], 0.0)
            step.done(V_.memset(wgT[:], 0.0))
            stats(0)
            dve.wait_ge(S["consts_in"], 32)
            V_.tensor_copy(esel[:], eload)
            dve.wait_ge(S["filled"], 1)
            dve.wait_ge(S["weights_in"], 16 * 15)
            V_.tensor_scalar(halfgb[:], qkvb[:, 3:4], 0.5, None, ALU.mult)
            dve.wait_ge(S["softplus"], 1)
            step.done(V_.scalar_tensor_tensor(out=byp[:, 4:5], in0=byp[:, 0:1], scalar=0.0, in1=byp[:, 3:4],
                                              op0=ALU.max, op1=ALU.add))
            step.wait()
            step.done(V_.tensor_scalar(byp[:, 5:6], byp[:, 4:5], D4[0], None, ALU.add))
            step.wait()
            V_.tensor_scalar(blkw[:], cst[:, C_BLK:C_BLK + P], byp[:, 5:6], None, ALU.mult)
            dve.wait_ge(S["wT_psum"], 1)
            V_.tensor_copy(projT[:], bank[0][:])
            V_.tensor_tensor(mqs[:].rearrange("p (h s) -> p h s", h=H),
                             cst[:, C_HM:C_HM + H].unsqueeze(2).broadcast_to([P, H, NS]),
                             bank[2][:, 64:64 + NS].unsqueeze(1).broadcast_to([P, H, NS]), ALU.mult)
            V_.tensor_scalar(outT[:], bank[1][:, 0:D], 0.5, None, ALU.mult)
            V_.tensor_copy(abcT[:], bank[1][:, D:4 * D])
            step.wait()
            V_.tensor_copy(wgT[:, 0:NE], bank[2][:, 0:NE])
            V_.tensor_copy(b1T[:], bank[2][:, 32:64]).then_inc(S["setup_done"], 1)
            dve.wait_ge(S["setup_done"], 1)

            def normalise(n):
                if later(n):
                    dve.wait_ge(S["xT_psum"], n)
                for c in range(TPC):
                    last = V_.tensor_scalar(xn[:, c * D:(c + 1) * D], sl(X, n * CW + c * D, D),
                                            sl(mean, n * TPC + c, 1), sl(rstd, n * TPC + c, 1), ALU.subtract, ALU.mult)
                last.then_inc(S["xn_ready"], 1)

            def shift_logits(n):
                dve.wait_ge(S["logits"], n + 1)
                w, hs = 2 * H * NS, 2 * H
                lv = [bank[2 + k][:, 0:w].rearrange("p (ch s) -> p ch s", s=NS) for k in range(2)]
                for k in range(2):
                    last = V_.tensor_reduce(gmax[:, k * hs:(k + 1) * hs], lv[k], X_AXIS, ALU.max)
                step.done(last)
                step.wait()
                for k in range(2):
                    last = V_.tensor_tensor(gains[:, k * w:(k + 1) * w].rearrange("p (ch s) -> p ch s", s=NS), lv[k],
                                            gmax[:, k * hs:(k + 1) * hs].unsqueeze(2).broadcast_to([P, hs, NS]),
                                            ALU.subtract)
                last.then_inc(S["shifted"], 1)

            def softmax(n):
                g3 = gains.rearrange("p (ch s) -> p ch s", s=NS)
                dve.wait_ge(S["exp"], n + 1)
                step.done(V_.tensor_reduce(gsum, g3, X_AXIS, ALU.add))
                step.wait()
                step.done(V_.reciprocal(gmax, gsum))
                step.wait()
                V_.tensor_tensor(g3, g3, gmax.unsqueeze(2).broadcast_to([P, TPC * H, NS]),
                                 ALU.mult).then_inc(S["gains_ready"], 1)

            def shift_weights(n):
                by_scale = gains.rearrange("p (c h s) -> p c s h", c=TPC, h=H)
                wv = w01[0][:].rearrange("p (c m h) -> p c m h", c=TPC, h=H)
                dve.wait_ge(S["scaled"], n * 3 + 3)
                for c in range(TPC):
                    V_.scalar_tensor_tensor(out=wv[:, c, 1:8, :], in0=by_scale[:, c, 0:7, :], scalar=D4[2],
                                            in1=wv[:, c, 1:8, :], op0=ALU.mult, op1=ALU.add)
                w8v = w8[:].rearrange("p (c h) -> p c h", c=TPC)
                V_.scalar_tensor_tensor(out=w8v, in0=by_scale[:, :, 7, :], scalar=D4[2], in1=w8v,
                                        op0=ALU.mult, op1=ALU.add).then_inc(S["weights_ready"], 1)

            def gate(n, adds):
                dve.wait_ge(S["gate_ready"], n + 1)
                dve.wait_ge(S["terms_added"], adds)
                V_.scalar_tensor_tensor(out=att, in0=th, scalar=1.0, in1=acc, op0=ALU.add,
                                        op1=ALU.mult).then_inc(S["gated"], 1)

            def residual(n):
                dve.wait_ge(S["y_psum"], n + 1)
                V_.tensor_tensor(sl(X, n * CW, CW), sl(X, n * CW, CW), bank[0][:], ALU.add).then_inc(S["resid"], 1)

            STEPS = 3

            def chunk(i, kind, nxt):
                g0, g1, g2 = active(kind)
                n, base = products_of(kind), before(i, kind)
                adds = spread_before(i, kind)
                shifts, mine = shifts_of(kind), n - pool_products(kind)

                def product(j):
                    if j >= NPROD:
                        dve.wait_ge(S["products_used"], base + (j - NPROD + 1))
                    elif later(i):
                        dve.wait_ge(S["products_used"], base)
                    V_.tensor_tensor(prod[j % NPROD], qT, sl(K, i * CW + (PAD - NB * shifts[j]), CW),
                                     ALU.mult).then_inc(S["products_ready"], 1)

                def early_product(j):
                    if j == 0:
                        dve.wait_ge(S["q_ready"], i + 2)
                        dve.wait_ge(S["kv_ready"], i * 2 + 4)
                        dve.wait_ge(S["products_used"], base + n)
                    V_.tensor_tensor(prod[j], qT, sl(K, i * CW + (PAD + CW - NB * shifts[j]), CW),
                                     ALU.mult).then_inc(S["products_ready"], 1)

                def pack(g, bk, used, h=P):
                    dve.wait_ge(S["products_used"], used)
                    V_.tensor_tensor(af[g % 2][0:h, :], bank[bk][0:h, :], wt[g][0:h, :], ALU.mult).then_inc(
                        S[f"a{g}_ready"], 1)

                def low(g):
                    dve.wait_ge(S[f"a{g}_high"], i + 1)
                    V_.tensor_tensor(al[g][:], af[g][:], ah[g][:].bitcast(F32),
                                     ALU.subtract).then_inc(S[f"a{g}_low"], 1)

                def make_term(j):
                    if j == 0:
                        dve.wait_ge(S["products_used"], base + 1)
                    else:
                        dve.wait_ge(S["spread_ready"], adds + j)
                    if j >= NTERM:
                        dve.wait_ge(S["terms_added"], adds + max(1, j - NTERM))
                    elif later(i):
                        dve.wait_ge(S["terms_added"], adds)
                    V_.tensor_tensor(term[j % NTERM], spread_bank[j % 3][:], sl(V, i * CW + (PAD - NB * shifts[j]), CW),
                                     ALU.mult).then_inc(S["terms_ready"], 1)

                if nxt is not None:
                    normalise(nxt)
                if not later(i):
                    dve.wait_ge(S["q_ready"], 1)
                    dve.wait_ge(S["kv_ready"], 2)
                    for j in range(EARLY):
                        product(j)
                split = min(1 + len(g0) + 3, mine)
                for j in range(EARLY, split):
                    product(j)
                dve.wait_ge(S["rows_ready"], i * 3 + 3)
                pack(0, 4, base + (1 + len(g0)))
                for j in range(split, mine):
                    product(j)
                low(0)
                pack(1, 5, base + (1 + len(g0) + len(g1)))
                if later(i):
                    gate(i - 1, adds)
                make_term(0)
                if g2:
                    dve.wait_ge(S["a0_low"], i + 1)
                    pack(2, 4, base + n, H)
                low(1)
                for j in range(1, n):
                    make_term(j)
                    _, _, _, at_out, _, at_logits, at_rows = places(kind)
                    if later(i) and j == at_out + 2:
                        residual(i - 1)
                    if nxt is not None:
                        if j == at_logits + 1:
                            shift_logits(nxt)
                        if j == min(at_logits + 2, n - 2):
                            softmax(nxt)
                        if j == at_rows - (at_rows < n - 1):
                            shift_weights(nxt)
                        if j >= n - EARLY:
                            early_product(j - (n - EARLY))

            dve.wait_ge(S["rstd"], 1)
            normalise(0)
            shift_logits(0)
            softmax(0)
            shift_weights(0)
            chunk(0, 0, 1)
            for lo, hi in RANGES:
                start = step.n
                if lo < CHUNKS // GC:
                    stats(lo)
                    dve.wait_ge(S["rstd"], lo + 1)
                with dve.Fori(lo, hi) as i:
                    step.enter(start, i - lo, STEPS)
                    chunk(i, lo, i + 1)
                    assert step.n == STEPS
                step.leave(start + (hi - lo) * STEPS)
            chunk(CHUNKS - 1, CHUNKS - 1, None)
            for q in range(JOB[0].chunks):
                prep_stats(0, q)
            gate(CHUNKS - 1, PRODUCTS_BEFORE[CHUNKS] - CHUNKS)
            residual(CHUNKS - 1)
            dve.wait_ge(S["resid"], CHUNKS)

            def normalised(chunk, t, mu, rs, ready):
                for c in range(TPC):
                    at = chunk * CW + c * D
                    last = V_.tensor_scalar(XN[:, at:at + D], X[:, at:at + D], mu[:, t + c:t + c + 1],
                                            rs[:, t + c:t + c + 1], ALU.subtract, ALU.mult)
                last.then_inc(ready, 1)

            def prep_normalise(n, q):
                dve.wait_ge(S["f_rstd"], CHUNKS_BEFORE[n] + q + 1)
                normalised(JOB[n].first + q, q * TPC, mean, rstd, S["f_xn"])

            def v3(t):
                return t.rearrange("p (g e) -> p g e", e=NE)

            def choose(n):
                g, w = JOB[n].tiles, JOB[n].tiles * NE
                full = [P, g, NE]
                lg_, tmp_, m_ = v3(lg[:, 0:w]), v3(tmp[:, 0:w]), m64[:, 0:g]
                rev = cst[:, C_REV:C_REV + NE].unsqueeze(1).broadcast_to(full)
                dve.wait_ge(S["f_lg_psum"], n + 1)
                V_.tensor_copy(lg[:, 0:w].rearrange("p (q c e) -> p q c e", c=TPC, e=NE),
                               bank[1][:].rearrange("p (c q e) -> p q c e", q=4, e=32)[:, 0:JOB[n].chunks, :, 0:NE]
                               ).then_inc(S["f_lg"], 1)
                dve.wait_ge(S["f_lg"], n + 1)
                step.done(V_.tensor_reduce(m_, lg_, X_AXIS, ALU.max))
                step.wait()
                step.done(V_.tensor_tensor(tmp_, lg_, m_.unsqueeze(2).broadcast_to(full), ALU.is_equal))
                step.wait()
                step.done(V_.tensor_tensor(tmp_, tmp_, rev, ALU.mult))
                step.wait()
                step.done(V_.tensor_reduce(m_, tmp_, X_AXIS, ALU.max))
                step.wait()
                V_.tensor_tensor(v3(oh[:, 0:w]), tmp_, m_.unsqueeze(2).broadcast_to(full), ALU.is_equal).then_inc(
                    S["f_onehot"], 1)

            def experts_tiles(n):
                g, w = JOB[n].tiles, JOB[n].tiles * NE
                dve.wait_ge(S["f_onehot"], n + 1)
                dve.wait_ge(S["f_counts"], n + 1)
                tot = v3(bank[4][:, w:2 * w])
                inc3, tmp3 = (t[:, 0:w].rearrange("p (e g) -> p e g", e=NE) for t in (incl, tmp))
                for e in range(NE):
                    last = V_.tensor_tensor_scan(inc3[:, e, :], ones[:, 0:g], tot[:, :, e], 0.0, ALU.mult, ALU.add)
                step.done(last)
                step.wait()
                kt = cst[:, C_KT:C_KT + g].unsqueeze(1).broadcast_to([P, NE, g])
                step.done(V_.tensor_tensor(tmp3, inc3[:, :, g - 1:g].broadcast_to([P, NE, g]), kt, ALU.is_gt))
                step.wait()
                step.done(V_.tensor_reduce(ntl, tmp3, X_AXIS, ALU.add))
                step.wait()
                step.done(V_.tensor_tensor_scan(ctl, ones[:, 0:NE], ntl, 0.0, ALU.mult, ALU.add))
                step.wait()
                step.done(V_.tensor_tensor(bas, ctl, ntl, ALU.subtract))

            def token_slots(n):
                g, w = JOB[n].tiles, JOB[n].tiles * NE
                full = [P, g, NE]
                tmp_ = v3(tmp[:, 0:w])
                step.wait()
                step.done(V_.tensor_tensor(tmp_, incl[:, 0:w].rearrange("p (e g) -> p g e", e=NE), v3(bank[4][:, w:2 * w]),
                                           ALU.subtract))
                step.wait()
                step.done(V_.tensor_tensor(tmp_, tmp_, v3(bank[4][:, 0:w]), ALU.add))
                step.wait()
                step.done(V_.scalar_tensor_tensor(out=tmp_, in0=bas.unsqueeze(1).broadcast_to(full), scalar=float(P),
                                                  in1=tmp_, op0=ALU.mult, op1=ALU.add))
                step.wait()
                step.done(V_.tensor_tensor(tmp_, tmp_, v3(oh[:, 0:w]), ALU.mult))
                step.wait()
                step.done(V_.tensor_reduce(slotf[:, 0:g], tmp_, X_AXIS, ALU.add))
                step.wait()
                V_.tensor_copy(slot_i[:, TILES_BEFORE[n]:TILES_BEFORE[n + 1]], slotf[:, 0:g]).then_inc(
                    S["f_slots_ready"], 1)

            def tile_experts(n):
                k, w = JOB[n].slots, JOB[n].slots // PACK
                t3v, dims = t3[0:1, 0:k * (NE - 1)].rearrange("p (s e) -> p s e", e=NE - 1), [1, k, NE - 1]
                step.done(V_.tensor_tensor(t3v, cst[0:1, C_SI:C_SI + k].unsqueeze(2).broadcast_to(dims),
                                           ctl[0:1, 0:NE - 1].unsqueeze(1).broadcast_to(dims), ALU.is_ge))
                step.wait()
                step.done(V_.tensor_reduce(tef[0:1, 0:k], t3v, X_AXIS, ALU.add))
                step.wait()
                V_.tensor_copy(te_i[:, SLOTS_BEFORE[n]:SLOTS_BEFORE[n + 1]], tef[0:1, 0:k])
                step.done(V_.tensor_tensor(t3[0:1, 0:k], tef[0:1, 0:k], cst[0:1, C_PW:C_PW + k], ALU.mult))
                step.wait()
                step.done(V_.tensor_reduce(tef[0:1, 0:w], t3[0:1, 0:k].rearrange("p (w k) -> p w k", k=PACK),
                                           X_AXIS, ALU.add))
                step.wait()
                V_.tensor_copy(te_p[:, SLOTS_BEFORE[n] // PACK:SLOTS_BEFORE[n + 1] // PACK], tef[0:1, 0:w]).then_inc(
                    S["f_slots_ready"], 1)

            def result(n, s, words):
                u, t = s % 2, SLOTS_BEFORE[n] + s
                e = expert(words, s)
                dve.wait_ge(S["f_y_psum"], t + 1)
                if t >= 2:
                    dve.wait_ge(ys_out[u], 16 * (t // 2))
                V_.tensor_tensor(ysb[u], bank[5][:, 0:D], b2bc[:, ds(e * D, D)],
                                 ALU.add).then_inc(S["f_y_ready"], 1)

            def add_results(n):
                dve.wait_ge(S["f_gathered"], 16 * TILES_BEFORE[n + 1])
                at, w = JOB[n].first * CW, JOB[n].chunks * CW
                V_.tensor_tensor(X[:, at:at + w], X[:, at:at + w], XN[:, at:at + w], ALU.add).then_inc(S["f_added"], 1)
                dve.wait_ge(S["f_added"], n + 1)

            def in_stats(c):
                at = c * CW
                statistics(lambda k: X[:, at + k * D:at + (k + 1) * D], lambda k: raw3[:, 6 * k:6 * k + 6], S["r_stats"])

            def in_normalise(c):
                dve.wait_ge(S["r_rstd"], c + 1)
                normalised(c, 0, mean3, rstd3, S["r_xn"])

            def in_columns(c):
                dve.wait_ge(S["r_xT_psum"], c + 1)
                if c:
                    dve.wait_ge(S["r_xb"], c)
                V_.tensor_copy(xrT, bank[1][:]).then_inc(S["r_xT"], 1)

            def out_stats(c):
                dve.wait_ge(S["r_y"], c + 1)
                dve.wait_ge(S["r_xn"], c + 1)
                if c:
                    dve.wait_ge(S["r_out"], c)
                step.done(V_.tensor_tensor(res, XN[:, c * CW:(c + 1) * CW], bank[1][:], ALU.add))
                step.wait()
                statistics(lambda k: res[:, k * D:(k + 1) * D], lambda k: raw2[:, 6 * k:6 * k + 6], S["r_stats2"])

            def out_residual(c):
                dve.wait_ge(S["r_rstd2"], c + 1)
                for k in range(TPC):
                    last = V_.tensor_scalar(res[:, k * D:(k + 1) * D], res[:, k * D:(k + 1) * D],
                                            mean2[:, k:k + 1], rstd2[:, k:k + 1], ALU.subtract, ALU.mult)
                step.done(last)
                step.wait()
                r3 = res.rearrange("p (c d) -> p c d", d=D)
                step.done(V_.tensor_tensor(r3, r3, bc_out(brow[:, D:2 * D]), ALU.mult))
                step.wait()
                step.done(V_.tensor_tensor(r3, r3, bc_out(brow[:, 2 * D:3 * D]), ALU.add))
                step.wait()
                at = c * CW
                V_.tensor_tensor(X[:, at:at + CW], X[:, at:at + CW], res, ALU.add).then_inc(S["r_out"], 1)

            V_.memset(hid[1][:, CW - NB:CW], 0.0).then_inc(S["h_ready"], 1)
            for slot in SLOTS:
                if slot.pair == 0:
                    add_results(0)
                    in_stats(0)
                    in_normalise(0)
                    in_columns(0)
                for h in range(2):
                    c, n = chunk_of(slot, h), slot.prep if h == 0 else None
                    chunks = 0 if n is None else JOB[n].chunks
                    tiles = iter(())
                    if slot.tiles is not None:
                        half = JOB[slot.tiles].slots // 2
                        tiles = iter(range(half - 1) if h == 0 else range(half - 1, 2 * half))

                    def results(count):
                        for _ in range(count):
                            s = next(tiles, None)
                            if s is not None:
                                result(slot.tiles, s, words)

                    early = chunks if n is None or n < PASS1 else chunks - 1
                    if slot.tiles is not None and h == 0:
                        dve.wait_ge(S["w2_in"], 32)
                        dve.wait_ge(S["f_slots_ready"], 2 * slot.tiles + 2)
                        words = packed_experts(dve, slot.tiles)
                    if h == 1 and slot.prep is not None:
                        choose(slot.prep)
                        results(1)
                    if c is not None and c + 1 < CHUNKS:
                        in_stats(c + 1)
                    for q in range(early if n != 0 else 0):
                        prep_stats(n, q)
                    if c is not None and c > 0:
                        out_stats(c - 1)
                    if n == JOBS - 1:
                        out_stats(CHUNKS - 1)
                        out_residual(CHUNKS - 1)
                        dve.wait_ge(S["r_out"], CHUNKS)
                    if h == 1:
                        results(1)
                    if c is not None and c + 1 < CHUNKS:
                        in_normalise(c + 1)
                    if h == 1:
                        results(1)
                    if c is not None and c > 0:
                        out_residual(c - 1)
                        dve.wait_ge(S["r_out"], c)
                    for q in range(early, chunks):
                        prep_stats(n, q)
                    late = h == 0 and slot.tiles is not None and LEAD[slot.tiles] > columns_step(slot, h)
                    if not late:
                        results(1)
                    if h == 1 and slot.prep is not None:
                        experts_tiles(slot.prep)
                        results(1)
                        token_slots(slot.prep)
                        results(1)
                        tile_experts(slot.prep)
                    elif not late:
                        results(1)
                    if c is not None and c + 1 < CHUNKS:
                        in_columns(c + 1)
                    for q in range(chunks):
                        prep_normalise(n, q)
                        results(1)
                    results(ST)
                    if slot.gather is not None and h == int(slot.pair is not None and slot.gather != 1):
                        add_results(slot.gather)
            add_results(JOBS - 1)


_ARGS = {
    "x": "L0_attn_a_x", "W_qkv": "L0_attn_a_W_qkv", "b_qkv": "L0_attn_a_b_qkv", "W_out": "L0_attn_a_W_out",
    "b_out": "L0_attn_a_b_out", "W_gate": "L0_attn_a_W_gate", "b_gate": "L0_attn_a_b_gate",
    "scale_gain": "L0_attn_a_scale_gain", "W_qscale": "L0_attn_a_W_qscale",
    "identity_bypass": "L0_attn_a_identity_bypass", "A": "L0_attn_b_A", "B": "L0_attn_b_B", "C": "L0_attn_b_C",
    "gamma": "L0_attn_b_gamma", "beta": "L0_attn_b_beta", "Wg": "L0_ffn_Wg", "W1": "L0_ffn_W1", "b1": "L0_ffn_b1",
    "W2": "L0_ffn_W2", "b2": "L0_ffn_b2",
}


def kernel(**inputs):
    import concourse.bacc as _bacc
    from concourse.bass_utils import run_bass_kernel_spmd as _run

    nc = _bacc.Bacc("TRN2", target_bir_lowering=False, num_devices=1)
    arrays, args = {}, {}
    for short, name in _ARGS.items():
        arr = np.ascontiguousarray(inputs[name])
        arrays[f"in_{short}"] = arr
        args[short] = nc.dram_tensor(f"in_{short}", arr.shape, mybir.dt.from_np(arr.dtype), kind="ExternalInput").ap()
    arrays["in_consts"] = constants()
    consts = nc.dram_tensor("in_consts", (P, C_ALL), F32, kind="ExternalInput").ap()
    out = nc.dram_tensor("out_x", (NB, NT, D), F32, kind="ExternalOutput").ap()
    build(nc, args, consts, out)
    r = _run(nc, [arrays], core_ids=[0])
    return r.results[0]["out_x"]
```
